# Optimizing a Trainium2 kernel written in Bass

```python
import numpy as np
import jax
import jax.numpy as jnp

def _softmax(x, axis=-1):
    return jax.nn.softmax(x, axis=axis)

def _gelu(x):
    return jax.nn.gelu(x, approximate=True)

def _silu(x):
    return jax.nn.silu(x)

def _sigmoid(x):
    return jax.nn.sigmoid(x)

def _layernorm(x, axis=-1, eps=1e-05):
    m = jnp.mean(x, axis=axis, keepdims=True)
    v = jnp.var(x, axis=axis, keepdims=True)
    return (x - m) / jnp.sqrt(v + eps)

def _scatter_add(tgt, idx, src, axis=0):
    return tgt.at[idx].add(src)

def _segment_sum(src, seg, n):
    return jax.ops.segment_sum(src, seg, n)
kernel_name = 'mk_gps_d1_gnn_r8_2ac593'

def setup_inputs(seed: int=0):
    np.random.seed(seed)
    _w = jnp.asarray

    def _rec_inputs():
        import jax
        import jax.numpy as jnp
        _gk = jax.random.key(seed)
        x = -8.776e-05 + 1 * jax.random.normal(jax.random.fold_in(_gk, 1), (1250, 512), jnp.float32)
        _s = jax.random.randint(jax.random.fold_in(_gk, 2), (10000,), 0, 1250, jnp.int32)
        _d = jax.random.randint(jax.random.fold_in(_gk, 3), (10000,), 0, 1250, jnp.int32)
        _loop = jnp.arange(1250, dtype=jnp.int32)
        src = jnp.concatenate([_s, _d, _loop])
        dst = jnp.concatenate([_d, _s, _loop])
        _o = jnp.argsort(dst, stable=True)
        src = src[_o]
        dst = dst[_o]
        return (x, src, dst)
    x, src, dst = _rec_inputs()

    def _L0_gnn_setup():
        import jax, jax.numpy as jnp
        import numpy as np
        N_NODES = 1250
        N_EDGES = 20000
        D = 512
        key = jax.random.key(seed)
        k_h, k_e, k_w1, k_w2 = jax.random.split(key, 4)
        h = jax.random.normal(k_h, (N_NODES, D), dtype=jnp.float32)
        edge_index = jax.random.randint(k_e, (2, N_EDGES), 0, N_NODES, dtype=jnp.int64)
        scale = 1.0 / np.sqrt(D)
        W1 = jax.random.normal(k_w1, (D, D), dtype=jnp.float32) * scale
        b1 = jnp.zeros((D,), dtype=jnp.float32)
        W2 = jax.random.normal(k_w2, (D, D), dtype=jnp.float32) * scale
        b2 = jnp.zeros((D,), dtype=jnp.float32)
        return {'h': h, 'edge_index': edge_index, 'W1': W1, 'b1': b1, 'W2': W2, 'b2': b2}
    _L0_gnn_all = _L0_gnn_setup()
    _L0_gnn_in = {k: v for k, v in _L0_gnn_all.items() if k in ('W1', 'b1', 'W2', 'b2')}
    del _L0_gnn_all

    def _L0_mix_setup():
        import jax, jax.numpy as jnp
        import numpy as np
        NUM_HEADS = 8
        EPS = 1e-06
        key = jax.random.key(seed)
        k1, k2, k3 = jax.random.split(key, 3)
        B, N, C = (8, 512, 512)
        x = jax.random.normal(k1, (B, N, C), dtype=jnp.float32)
        Wq = jax.random.normal(k2, (C, C), dtype=jnp.float32) * (1.0 / np.sqrt(C))
        Wkv = jax.random.normal(k3, (2 * C, C), dtype=jnp.float32) * (1.0 / np.sqrt(C))
        return {'x': x, 'Wq': Wq, 'Wkv': Wkv}
    _L0_mix_all = _L0_mix_setup()
    _L0_mix_in = {k: v for k, v in _L0_mix_all.items() if k in ('Wq', 'Wkv')}
    del _L0_mix_all

    def _L0_ffn_setup():
        import jax, jax.numpy as jnp
        import numpy as np
        B, T, C = (8, 1024, 512)
        H = 1024
        G, EG = (2, 4)
        E = G * EG
        K = 2
        LN_EPS = 1e-05

        def _swiglu(x):
            a, b = jnp.split(x, 2, axis=-1)
            return jax.nn.silu(a) * b
        key = jax.random.key(seed)
        ks = jax.random.split(key, 8)
        n = lambda k, shape, s: jax.random.normal(k, shape, dtype=jnp.float32) * s
        return {'x': n(ks[0], (B, T, C), 1.0), 'ln_scale': jnp.ones((C,), jnp.float32), 'ln_bias': jnp.zeros((C,), jnp.float32), 'shared_in_w': n(ks[1], (2 * H, C), 0.02), 'shared_out_w': n(ks[2], (C, H), 0.02), 'shared_out_b': jnp.zeros((C,), jnp.float32), 'expert_in_w': n(ks[3], (2 * H, C), 0.02), 'expert_out_weight': n(ks[4], (E, C, H), 0.02), 'expert_out_bias': jnp.zeros((E, C), jnp.float32), 'group_gate_w': n(ks[5], (G, C), 0.02), 'expert_gate_w': n(ks[6], (E, C), 0.02), 'group_bias': jnp.zeros((G,), jnp.float32), 'expert_bias': jnp.zeros((E,), jnp.float32)}
    _L0_ffn_all = _L0_ffn_setup()
    _L0_ffn_in = {k: v for k, v in _L0_ffn_all.items() if k in ('ln_scale', 'ln_bias', 'shared_in_w', 'shared_out_w', 'shared_out_b', 'expert_in_w', 'expert_out_weight', 'expert_out_bias', 'group_gate_w', 'expert_gate_w', 'group_bias', 'expert_bias')}
    del _L0_ffn_all
    return {'x': x, 'src': src, 'dst': dst, 'L0_gnn_W1': _L0_gnn_in['W1'], 'L0_gnn_b1': _L0_gnn_in['b1'], 'L0_gnn_W2': _L0_gnn_in['W2'], 'L0_gnn_b2': _L0_gnn_in['b2'], 'L0_mix_Wq': _L0_mix_in['Wq'], 'L0_mix_Wkv': _L0_mix_in['Wkv'], 'L0_ffn_ln_scale': _L0_ffn_in['ln_scale'], 'L0_ffn_ln_bias': _L0_ffn_in['ln_bias'], 'L0_ffn_shared_in_w': _L0_ffn_in['shared_in_w'], 'L0_ffn_shared_out_w': _L0_ffn_in['shared_out_w'], 'L0_ffn_shared_out_b': _L0_ffn_in['shared_out_b'], 'L0_ffn_expert_in_w': _L0_ffn_in['expert_in_w'], 'L0_ffn_expert_out_weight': _L0_ffn_in['expert_out_weight'], 'L0_ffn_expert_out_bias': _L0_ffn_in['expert_out_bias'], 'L0_ffn_group_gate_w': _L0_ffn_in['group_gate_w'], 'L0_ffn_expert_gate_w': _L0_ffn_in['expert_gate_w'], 'L0_ffn_group_bias': _L0_ffn_in['group_bias'], 'L0_ffn_expert_bias': _L0_ffn_in['expert_bias']}

def reference(x, src, dst, L0_gnn_W1, L0_gnn_b1, L0_gnn_W2, L0_gnn_b2, L0_mix_Wq, L0_mix_Wkv, L0_ffn_ln_scale, L0_ffn_ln_bias, L0_ffn_shared_in_w, L0_ffn_shared_out_w, L0_ffn_shared_out_b, L0_ffn_expert_in_w, L0_ffn_expert_out_weight, L0_ffn_expert_out_bias, L0_ffn_group_gate_w, L0_ffn_expert_gate_w, L0_ffn_group_bias, L0_ffn_expert_bias):
    import jax
    import jax.numpy as jnp

    def _L0_gnn_ref(h, edge_index, W1, b1, W2, b2):
        import jax, jax.numpy as jnp
        import numpy as np
        N_NODES = 1250
        N_EDGES = 20000
        D = 512
        send, rec = (edge_index[0], edge_index[1])
        agg = jax.ops.segment_sum(h[send], rec, num_segments=h.shape[0])
        x = h + agg
        x = jax.nn.relu(x @ W1 + b1)
        x = x @ W2 + b2
        return x

    def _L0_mix_ref(x, Wq, Wkv):
        import jax, jax.numpy as jnp
        import numpy as np
        NUM_HEADS = 8
        EPS = 1e-06
        B, N, C = x.shape
        h = NUM_HEADS
        d = C // h
        q = (x @ Wq.T).reshape(B, N, h, d)
        kv = (x @ Wkv.T).reshape(B, N, 2, h, d)
        k = kv[:, :, 0]
        v = kv[:, :, 1]
        Q = jax.nn.elu(q) + 1.0
        K = jax.nn.elu(k) + 1.0
        v_length = v.shape[1]
        v = v / v_length
        KV = jnp.einsum('nshd,nshv->nhdv', K, v)
        Z = 1.0 / (jnp.einsum('nlhd,nhd->nlh', Q, K.sum(axis=1)) + EPS)
        out = jnp.einsum('nlhd,nhdv,nlh->nlhv', Q, KV, Z) * v_length
        return out.reshape(B, N, C)

    def _L0_ffn_ref(x, ln_scale, ln_bias, shared_in_w, shared_out_w, shared_out_b, expert_in_w, expert_out_weight, expert_out_bias, group_gate_w, expert_gate_w, group_bias, expert_bias):
        import jax, jax.numpy as jnp
        import numpy as np
        B, T, C = (8, 1024, 512)
        H = 1024
        G, EG = (2, 4)
        E = G * EG
        K = 2
        LN_EPS = 1e-05

        def _swiglu(x):
            a, b = jnp.split(x, 2, axis=-1)
            return jax.nn.silu(a) * b
        Bx, Tx, Cx = x.shape
        S = Bx * Tx
        flat = x.reshape(S, Cx)
        mu = flat.mean(-1, keepdims=True)
        var = ((flat - mu) ** 2).mean(-1, keepdims=True)
        flat = (flat - mu) * jax.lax.rsqrt(var + LN_EPS) * ln_scale + ln_bias
        h_shared = _swiglu(flat @ shared_in_w.T)
        out_shared = h_shared @ shared_out_w.T + shared_out_b
        g_logits = flat @ group_gate_w.T + group_bias
        g_idx = jnp.argmax(g_logits, axis=-1)
        e_logits = (flat @ expert_gate_w.T).reshape(S, G, EG)
        e_sel = jnp.take_along_axis(e_logits, g_idx[:, None, None], axis=1)[:, 0, :]
        e_sel = e_sel + expert_bias.reshape(G, EG)[g_idx]
        e_probs = jax.nn.softmax(e_sel, axis=-1)
        topv, topi = jax.lax.top_k(e_probs, K)
        topv = topv / (topv.sum(-1, keepdims=True) + 1e-08)
        disp = g_idx[:, None] * EG + topi
        h_expert = _swiglu(flat @ expert_in_w.T)
        rows = jnp.arange(S)[:, None]
        comb = jnp.zeros((S, E), flat.dtype).at[rows, disp].add(topv)
        cnt = jnp.zeros((S, E), flat.dtype).at[rows, disp].add(1.0)
        routed = cnt @ expert_out_bias
        for e in range(E):
            routed = routed + comb[:, e:e + 1] * (h_expert @ expert_out_weight[e].T)
        return (out_shared + routed).reshape(Bx, Tx, Cx)
    edge_index = jnp.stack([src, dst])
    xn = _layernorm(x, axis=-1)
    x = x + _L0_gnn_ref(xn, edge_index, L0_gnn_W1, L0_gnn_b1, L0_gnn_W2, L0_gnn_b2) + _L0_mix_ref(xn[None], L0_mix_Wq, L0_mix_Wkv)[0]
    x = x + _L0_ffn_ref(_layernorm(x, axis=-1)[None], L0_ffn_ln_scale, L0_ffn_ln_bias, L0_ffn_shared_in_w, L0_ffn_shared_out_w, L0_ffn_shared_out_b, L0_ffn_expert_in_w, L0_ffn_expert_out_weight, L0_ffn_expert_out_bias, L0_ffn_group_gate_w, L0_ffn_expert_gate_w, L0_ffn_group_bias, L0_ffn_expert_bias)[0]
    return x

_drawn_inputs = setup_inputs


def setup_inputs(seed=0):
    import zlib

    import numpy as np

    out = dict(_drawn_inputs(seed))
    spreads = {'L0_gnn_b1': (0.0, 0.337),
     'L0_gnn_b2': (0.0, 0.1),
     'L0_ffn_ln_scale': (1.0, 0.6),
     'L0_ffn_ln_bias': (0.0, 0.438),
     'L0_ffn_shared_out_b': (0.0, 0.269),
     'L0_ffn_expert_out_bias': (0.0, 0.1),
     'L0_ffn_group_bias': (0.0, 0.718),
     'L0_ffn_expert_bias': (0.0, 0.416)}
    factors = {'L0_mix_Wq': 8.0, 'L0_mix_Wkv': 6.053, 'L0_ffn_expert_in_w': 2.755}
    for name, (base, spread) in spreads.items():
        noise = np.random.default_rng([zlib.crc32(name.encode()), seed]).standard_normal(out[name].shape)
        drawn = base * np.exp(spread * noise) if base else spread * noise
        out[name] = jnp.asarray(drawn.astype(out[name].dtype))
    for name, factor in factors.items():
        out[name] = (out[name] * factor).astype(out[name].dtype)
    return out
```

```python
from contextlib import ExitStack

import numpy as np

import concourse.bass as bass
from concourse import mybir

F32 = mybir.dt.float32
F16 = mybir.dt.float16
I32 = mybir.dt.int32
U32 = mybir.dt.uint32
ALU = mybir.AluOpType
ACT = mybir.ActivationFunctionType
AX = mybir.AxisListType

N_NODES, D, HEADS, HID = 1250, 512, 8, 1024
N_EDGES = 21250
P = 125
T = N_NODES // P
KB = D // 128
HB = HID // 128
EXPERTS, GROUPS, PER_GROUP = 8, 2, 4
GATES = GROUPS + EXPERTS
CHUNKS = N_EDGES // P
HALF = CHUNKS // 2
COLS = [(0, 417), (417, 417), (834, 416)]
WIDE = 3 * 417
UNIT = 2048
MAX_TILES = (2 * N_NODES + EXPERTS * 127) // 128
JW = 32

U_WK, U_WV, U_WQ, U_W1, U_W2, U_EIN, U_SIN, U_SOUT, U_EXP = 0, 1, 2, 3, 4, 5, 9, 13, 15
N_UNITS = U_EXP + 2 * EXPERTS
LATE = 8
U_LATE = N_UNITS - LATE
SLOT_WK, SLOT_WV, SLOT_WQ, SLOT_W1, SLOT_W2 = 4, 5, 6, 14, 15
SLOT_EIN, SLOT_SIN, SLOT_SOUT, SLOT_LATE = 0, 4, 11, 16 - LATE

S_X = 2.0 ** 8
S_F = 2.0 ** 6
S_W = 2.0 ** 8
S_G = 2.0 ** -4
S_H = 2.0 ** 4
LN_EPS = 1e-5
ATT_EPS = 1e-6
IN_RANGE = "the tables of the chunk search stay within the chunks"
CO_SHIFT = 4096


class Region:

    def __init__(self, nc, start, size):
        self.nc, self.at, self.end = nc, start, start + size

    def put(self, name, shape, dt):
        size = int(np.prod(shape[1:])) * (2 if dt == F16 else 4)
        t = self.nc.alloc_sbuf_tensor_at(name, list(shape), dt, offset=self.at, align_bytes=4)
        self.at += (size + 3) // 4 * 4
        assert self.at <= self.end, (name, self.at, self.end)
        return t


def gps_layer(nc, d, out, hid_dram):
    with ExitStack() as ctx:
        base = (nc.sbuf_base + 31) // 32 * 32
        slot_bytes = 2 * UNIT * 2

        def region(start, size):
            return Region(nc, start, size)

        def slots(first, n=1):
            return region(base + first * slot_bytes, n * slot_bytes)

        top = base + 16 * slot_bytes
        r_x = region(top, T * D * 4)
        r_stage = region(r_x.end, 2 * UNIT * 4)
        r_f = region(r_stage.end, T * D * 4)
        r_g = region(r_f.end, 20000)
        small = region(r_g.end, nc.sbuf_usable_end - r_g.end)

        wslots = slots(0, 16).put("wslots", [128, 16, 2, UNIT], F16)
        x_sb = r_x.put("x_sb", [P, T, D], F32)
        stage = r_stage.put("stage", [128, 2, UNIT], F32)

        def again(r):
            return region(r.end - size_of[r], size_of[r])

        size_of = {r_f: T * D * 4, r_g: 20000}
        xn = r_f.put("xn", [P, 2, T, D], F16)
        xnT = r_g.put("xnT", [128, 2, KB, N_NODES], F16)
        h1T = again(r_g).put("h1T", [128, 2, KB, N_NODES], F16)
        r = again(r_g)
        bias_in = r.put("bias_in", [EXPERTS + 1, D], F32)
        r = slots(0, 2)
        hot_src = r.put("hot_src", [P, 4, WIDE + 1], F16)
        hot_dst = r.put("hot_dst", [P, 4, P + 1], F16)
        a_row = r.put("a_row", [P, 2, WIDE + 1], F16)
        r = slots(2, 2)
        hot_self = r.put("hot_self", [P, WIDE + 1], F16)
        z1 = r.put("z1", [P, 2, D], F32)
        srci = r.put("srci", [P, CHUNKS], I32)
        dsti = r.put("dsti", [P, CHUNKS], I32)
        srcf = r.put("srcf", [P, CHUNKS + 2], F32)
        dstf = r.put("dstf", [P, CHUNKS + 2], F32)
        dst2 = r.put("dst2", [HALF, 2, P], I32)
        diag = r.put("diag", [HALF, 4, HALF], F16)
        mnmx = r.put("mnmx", [HALF, 4], F32)
        rngf = r.put("rngf", [T, 4, CHUNKS], F32)
        cup = r.put("cup", [T, 2, CHUNKS], F32)
        rsm = r.put("rsm", [T, 8], F32)
        rs16 = r.put("rs16", [T, 2], F16)
        even = r.put("even", [T, HALF], F32)
        r = slots(7)
        kbuf = r.put("kbuf", [P, 2, D], F32)
        vbuf = r.put("vbuf", [P, 2, D], F32)
        r = slots(7)
        kvd = r.put("kvd", [128, KB, 130], F32)
        b2b = r.put("b2b", [P, D], F32)
        r_q = slots(8, 3)
        qT = r_q.put("qT", [128, KB, N_NODES], F32)
        spare = (r_q.at, r_q.end - 424 - r_q.at)
        r1T = slots(8, 3).put("r1T", [128, 2, KB, N_NODES], F16)
        iota = region(*spare).put("iota", [P, WIDE + 1], F16)
        ebuf = region(*spare).put("ebuf", [128, 2, D], F32)
        att = region(*spare).put("att", [P, 2, D], F32)
        rbuf = region(*spare).put("rbuf", [128, 2, 417], F32)
        adjT = region(r_q.end - 424, 3 * slot_bytes + 424).put("adjT", [P, T, N_NODES], F16)
        fT = again(r_f).put("fT", [128, 2, KB, N_NODES], F16)
        r = again(r_g)
        z2 = r.put("z2", [P, 2, D], F32)
        ft = r.put("ft", [128, 2, KB, P], F32)
        hot_p = r.put("hot_p", [P, 2 * T, 128], F16)
        hot_j = r.put("hot_j", [P, 2 * T, 4, JW], F16)
        lg = r.put("lg", [P, T, GATES], F32)
        identf = r.put("identf", [128, 128], F32)
        r = region(*spare)
        cntT = r.put("cntT", [EXPERTS + 1, N_NODES], F16)
        mask16 = r.put("mask16", [P, T, EXPERTS], F16)
        before = r.put("before", [P, T + 1, EXPERTS], F16)
        oh8 = r.put("oh8", [P, 2, T, EXPERTS], F32)
        tk = r.put("tk", [P, 8, 2 * T], F32)
        r = slots(14)
        sil = r.put("sil", [P, 2, D], F32)
        h32 = r.put("h32", [P, 2, D], F32)
        r = slots(8, 2)
        rt = r.put("rt", [P, 12, T, EXPERTS], F32)
        iop = r.put("iop", [128, 128], F32)
        thr = r.put("thr", [P, JW + 1], F32)
        ge16 = r.put("ge16", [P, 2 * T, JW + 1], F16)
        c16 = r.put("c16", [P, 2 * T], F16)
        padw = r.put("padw", [128, JW], F32)
        he = slots(13).put("he", [P, 2, 2, HID], F16)
        r = slots(13)
        sil_s = r.put("sil_s", [128, 2, 417], F32)
        h32_s = r.put("h32_s", [128, 2, 417], F32)
        acc = slots(13).put("acc", [P, 2, D], F32)
        hsh = slots(8, 3).put("hsh", [128, HB, N_NODES], F16)
        hsl = again(r_g).put("hsl", [128, HB, N_NODES], F16)
        r = again(r_f)
        got = r.put("got", [128, 2, 2 * HID], F16)
        y = r.put("y", [128, 2, D], F32)
        pad0 = r.put("pad0", [128, D], F32)
        heT = again(r_g).put("heT", [128, 2, 2, HB, 128], F16)

        ident = small.put("ident", [128, 128], F16)
        tri = small.put("tri", [128, 128], F16)
        ones = small.put("ones", [128, 128], F16)
        onesf = small.put("onesf", [128, 2], F32)
        b1 = small.put("b1", [128, KB], F32)
        b1s = small.put("b1s", [128, KB], F32)
        lnp = small.put("lnp", [128, 2, KB], F32)
        lns = small.put("lns", [128, 2, KB], F32)
        gw = small.put("gw", [128, KB, GATES], F32)
        gb = small.put("gb", [P, GATES], F32)
        tabs = small.put("tabs", [1, 32], I32)
        tabf = small.put("tabf", [1, 32], F32)
        st6 = small.put("st6", [P, 2, 6], F32)
        mv = small.put("mv", [P, 2, 2], F32)
        ve = small.put("ve", [P, 2, 1], F32)
        sd = small.put("sd", [P, 2, 1], F32)
        rst = small.put("rst", [P, 2, 4], F32)
        den = small.put("den", [P, 2, 2, HEADS], F32)
        node_id = small.put("node_id", [P, T], F32)
        tlo = small.put("tlo", [T, 2], F32)
        pad_row = small.put("pad_row", [128, 1], F32)
        bias9 = small.put("bias9", [EXPERTS + 1, 2, D], F16)
        eidt = small.put("eidt", [1, JW], I32)
        gidx = small.put("gidx", [128, JW], U32)
        sidx = small.put("sidx", [128, JW], U32)
        wsl = small.put("wsl", [128, JW], F32)
        gcur = small.put("gcur", [128, 2], U32)
        scur = small.put("scur", [128, 2], U32)

        ps = ctx.enter_context(nc.psum_tensor("ps", [128, 8, 512], F32))
        ps16 = ps[:, :, :].bitcast(F16)

        def sem(name):
            return ctx.enter_context(nc.semaphore(name))

        edge_in, x_in, small_in, stage_in = sem("edge_in"), sem("x_in"), sem("small_in"), sem("stage_in")
        b2_in, hid_out, acc_out, pad_out = sem("b2_in"), sem("hid_out"), sem("acc_out"), sem("pad_out")
        const_ok, const2_ok = sem("const_ok"), sem("const2_ok")
        w_hi, w_lo = sem("w_hi"), sem("w_lo")
        bias_hi, bias_lo, par_ok = sem("bias_hi"), sem("bias_lo"), sem("par_ok")
        dve_c = sem("dve_c")
        edges_f, diag_ok, rows_ps, range_ok, tab_ps, tab_ok = (
            sem("edges_f"), sem("diag_ok"), sem("rows_ps"), sem("range_ok"), sem("tab_ps"), sem("tab_ok"))
        hot_ready, hot_used, self_hot, self_used = (
            sem("hot_ready"), sem("hot_used"), sem("self_hot"), sem("self_used"))
        a_copied, a_turned, adj_out = sem("a_copied"), sem("a_turned"), sem("adj_out")
        ln_bn, ln_mv, ln_ve, ln_sd, ln_r, z_ok = (
            sem("ln_bn"), sem("ln_mv"), sem("ln_ve"), sem("ln_sd"), sem("ln_r"), sem("z_ok"))
        xn_hi, xn_lo = sem("xn_hi"), sem("xn_lo")
        xcol_ps, xcol_out = sem("xcol_ps"), sem("xcol_out")
        k_ps, v_ps, k_act, k_done, v_done, kv_used = (
            sem("k_ps"), sem("v_ps"), sem("k_act"), sem("k_done"), sem("v_done"), sem("kv_used"))
        k_neg, q_neg = sem("k_neg"), sem("q_neg")
        q_ps, q_act, q_done = sem("q_ps"), sem("q_act"), sem("q_done")
        kvd_ok, o_ps, den_c, o_done, att_added = (
            sem("kvd_ok"), sem("o_ps"), sem("den_c"), sem("o_done"), sem("att_added"))
        n_ps, n_hi, n_lo = sem("n_ps"), sem("n_hi"), sem("n_lo")
        f1_ps, g_act, g_lo = sem("f1_ps"), sem("g_act"), sem("g_lo")
        w2_ps, x1_done, zt_ps, ft_act, f_hi, f_lo, gate_ps, lg_done = (
            sem("w2_ps"), sem("x1_done"), sem("zt_ps"), sem("ft_act"), sem("f_hi"), sem("f_lo"),
            sem("gate_ps"), sem("lg_done"))
        ei_ps, ei_sil, ei_mul, ei_hi, ei_lo = (
            sem("ei_ps"), sem("ei_sil"), sem("ei_mul"), sem("ei_hi"), sem("ei_lo"))
        rank_in, rank_ps, hots_ok, slot_ps, slots_ok, cnt_ps, cnt_ok, eid_ok = (
            sem("rank_in"), sem("rank_ps"), sem("hots_ok"), sem("slot_ps"), sem("slots_ok"),
            sem("cnt_ps"), sem("cnt_ok"), sem("eid_ok"))
        si_ps, si_sil, si_mul, si_hi, si_lo = (
            sem("si_ps"), sem("si_sil"), sem("si_mul"), sem("si_hi"), sem("si_lo"))
        so_ps, so_done = sem("so_ps"), sem("so_done")
        pad_ok, idx_ok, got_ok, tr_ps, ht_hi, ht_lo, ex_ps, y_ok = (
            sem("pad_ok"), sem("idx_ok"), [sem("got_ok0"), sem("got_ok1")], sem("tr_ps"),
            sem("ht_hi"), sem("ht_lo"), sem("ex_ps"), sem("y_ok"))
        passed = sem("passed")
        sel_ok, sel_exp, identf_ok = sem("sel_ok"), sem("sel_exp"), sem("identf_ok")
        idx2_ok, added = sem("idx2_ok"), sem("added")

        n_small = 7 * 16
        block = ctx.enter_context(nc.Block())

        def tiles(eng, step, peeled=1):
            for i in range(peeled):
                step(i)
            with eng.Fori(peeled, T // 2) as i:
                step(i)

        def later(i, b, n=1):
            return not isinstance(i, int) or 2 * i + b >= n

        @block.sync
        def _(sp):
            sp.dma_start(dst2[:, :, :], d["dst_rows"]).then_inc(edge_in, 16)
            sp.dma_start(dsti[:, :], d["dst_cols"]).then_inc(edge_in, 16)
            sp.dma_start(srci[:, :], d["src_cols"]).then_inc(edge_in, 16)
            xv = d["x"].rearrange("(t p) c -> p t c", p=P)
            sp.dma_start(x_sb[0:112, :, :], xv[0:112]).then_inc(x_in, 16)
            sp.dma_start(x_sb[112:P, :, :], xv[112:P]).then_inc(x_in, 16)
            sp.dma_start(stage[:, 0, :], d["weights"][0]).then_inc(stage_in, 16)
            sp.dma_start(b1[:, :], d["b1"]).then_inc(small_in, 16)
            sp.dma_start(lnp[:, 0, :], d["ln_scale"]).then_inc(small_in, 16)
            sp.dma_start(lnp[:, 1, :], d["ln_bias"]).then_inc(small_in, 16)
            sp.dma_start(gw[:, :, :], d["gate_w"]).then_inc(small_in, 16)
            sp.dma_start(gb[:, :], d["gate_b"].broadcast_to((P, GATES))).then_inc(small_in, 16)
            sp.dma_start(bias_in[0:EXPERTS, :], d["expert_b"]).then_inc(small_in, 16)
            sp.dma_start(bias_in[EXPERTS:EXPERTS + 1, :], d["shared_b"]).then_inc(small_in, 16)
            sp.wait_ge(stage_in, 16)
            sp.dma_start(stage[:, 1, :], d["weights"][1]).then_inc(stage_in, 16)
            with sp.Fori(2, N_UNITS) as u:
                sp.wait_ge(stage_in, 16 * u)
                sp.sem_inc(passed, 1)
                sp.wait_ge(w_lo, u - 1)
                sp.sem_inc(passed, 1)
                sp.dma_start(stage[:, u % 2, :], d["weights"][u]).then_inc(stage_in, 16)

        @block.gpsimd
        def _(pool):
            pool.memset(ident[:, :], 0.0).then_inc(const_ok, 1)
            pool.memset(ones[:, :], 1.0).then_inc(const_ok, 1)
            pool.wait_ge(const_ok, 2)
            pool.affine_select(out=ident[:, :], in_=ident[:, :], compare_op=ALU.not_equal, fill=1.0,
                               base=0, pattern=[[-1, 128]], channel_multiplier=1).then_inc(const_ok, 1)
            pool.affine_select(out=tri[:, :], in_=ones[:, :], compare_op=ALU.is_gt, fill=0.0,
                               base=0, pattern=[[1, 128]], channel_multiplier=-1).then_inc(const_ok, 1)
            exact = {"allow_small_or_imprecise_dtypes": True}
            pool.iota(cup[:, 0, :], [[1, CHUNKS]], base=1, channel_multiplier=0, **exact).then_inc(const_ok, 1)
            pool.iota(cup[:, 1, :], [[-1, CHUNKS]], base=CHUNKS, channel_multiplier=0, **exact).then_inc(const_ok, 1)
            pool.iota(even[:, :], [[2, HALF]], base=0, channel_multiplier=0, **exact).then_inc(const_ok, 1)
            pool.iota(tlo[:, :], [[P, 2]], base=0, channel_multiplier=P, **exact).then_inc(const_ok, 1)
            pool.iota(iota[:, :], [[1, WIDE + 1]], base=0, channel_multiplier=0, **exact).then_inc(const_ok, 1)
            pool.iota(node_id[:, :], [[P, T]], base=0, channel_multiplier=1, **exact).then_inc(const_ok, 1)
            pool.memset(onesf[:, :], 1.0).then_inc(const_ok, 1)
            pool.iota(pad_row[:, :], [[1, 1]], base=N_NODES, channel_multiplier=1, **exact).then_inc(const_ok, 1)
            pool.memset(srcf[:, CHUNKS:], -1.0).then_inc(const_ok, 1)
            pool.memset(dstf[:, CHUNKS:], -1.0).then_inc(const_ok, 1)

            def ln_low(i):
                for b in range(2):
                    t = 2 * i + b
                    pool.wait_ge(xn_hi, t + 1)
                    pool.sem_inc(passed, 1)
                    pool.tensor_tensor(xn[:, 1, t, :], z1[:, b, :], xn[:, 0, t, :], ALU.subtract)\
                        .then_inc(xn_lo, 1)
            tiles(pool, ln_low)

            pool.wait_ge(b2_in, 16)

            def add_att(i):
                for b in range(2):
                    t = 2 * i + b
                    pool.tensor_tensor(x_sb[:, t, :], x_sb[:, t, :], b2b[:, :], ALU.add).then_inc(att_added, 1)
                    pool.wait_ge(att_added, 2 * t + 1)
                    pool.wait_ge(o_done, t + 1)
                    pool.sem_inc(passed, 1)
                    pool.tensor_tensor(x_sb[:, t, :], x_sb[:, t, :], att[:, b, :], ALU.add)\
                        .then_inc(att_added, 1)
            tiles(pool, add_att)

            def ein_low(i):
                for b in range(2):
                    for j in range(2):
                        n = 2 * (2 * i + b) + j
                        pool.wait_ge(ei_hi, n + 1)
                        pool.tensor_tensor(he[:, b, 1, j * 512:(j + 1) * 512], h32[:, j, :],
                                           he[:, b, 0, j * 512:(j + 1) * 512], ALU.subtract).then_inc(ei_lo, 1)
            tiles(pool, ein_low)
            pool.wait_ge(w2_ps, T)
            pool.iota(iop[:, :], [[1, 128]], base=0, channel_multiplier=0, **exact).then_inc(const2_ok, 1)

            def sin_low(u):
                for m2 in range(2):
                    for c, (at, w) in enumerate(COLS):
                        n = 3 * m2 + c
                        pool.wait_ge(si_hi, 6 * u + n + 1)
                        pool.tensor_tensor(hsl[:, 2 * u + m2, at:at + w], h32_s[:, n % 2, 0:w],
                                           hsh[:, 2 * u + m2, at:at + w], ALU.subtract).then_inc(si_lo, 1)
            pool.wait_ge(slots_ok, 1)
            with pool.Fori(0, 4) as u:
                sin_low(u)

            pool.wait_ge(si_ps, 24)
            pool.memset(pad0[:, :], 0.0).then_inc(pad_ok, 1)
            pool.wait_ge(hid_out, 16 * T)
            pool.wait_ge(slots_ok, 1)

            def fetch(i, b):
                j = 2 * i + b
                pool.tensor_copy(gcur[:, b:b + 1], gidx[:, bass.ds(j, 1)]).then_inc(idx_ok, 1)
                pool.wait_ge(idx_ok, j + 1)
                pool.sem_inc(passed, 1)
                pool.indirect_dma_start(
                    out=got[:, b, :], out_offset=None, in_=hid_dram[:, :],
                    in_offset=bass.IndirectOffsetOnAxis(ap=gcur[:, b:b + 1], axis=0)).then_inc(got_ok[b], 16)

            def put(i, b):
                j = 2 * i + b
                pool.tensor_copy(scur[:, b:b + 1], sidx[:, bass.ds(j, 1)]).then_inc(idx2_ok, 1)
                pool.wait_ge(idx2_ok, j + 1)
                pool.wait_ge(y_ok, j + 1)
                if later(i, b):
                    pool.wait_ge(added, 16 * j)
                pool.sem_inc(passed, 1)
                pool.indirect_dma_start(
                    out=out[:, :], out_offset=bass.IndirectOffsetOnAxis(ap=scur[:, b:b + 1], axis=0),
                    in_=y[:, b, :], in_offset=None, compute_op=ALU.add).then_inc(added, 16)

            fetch(0, 0)
            fetch(0, 1)
            pool.wait_ge(acc_out, 16 * T)
            pool.wait_ge(pad_out, 16)

            def step(i):
                for b in range(2):
                    pool.wait_ge(tr_ps, 2 * i + b + 1)
                    if not (isinstance(i, int) and 2 * i + b + 2 >= MAX_TILES):
                        fetch(i + 1, b)
                    put(i, b)
            n_pairs = MAX_TILES // 2
            step(0)
            with pool.Fori(1, n_pairs - 1) as i:
                step(i)
            step(n_pairs - 1)
            put(n_pairs, 0)
            pool.wait_ge(added, 16 * MAX_TILES)

        @block.scalar
        def _(act):
            def split_hi(u, slot, half=None):
                half = u % 2 if half is None else half
                act.wait_ge(stage_in, 16 * (u + 1))
                act.activation(wslots[:, slot, 0, :], stage[:, half, :], ACT.Copy, scale=S_W).then_inc(w_hi, 1)

            act.wait_ge(edge_in, 48)
            act.activation(dstf[:, 0:CHUNKS], dsti[:, :], ACT.Copy).then_inc(edges_f, 1)
            act.activation(srcf[:, 0:CHUNKS], srci[:, :], ACT.Copy).then_inc(edges_f, 1)
            act.wait_ge(small_in, n_small)
            act.activation(bias9[:, 0, :], bias_in[:, :], ACT.Copy, scale=S_W).then_inc(bias_hi, 1)
            act.activation(b1s[:, :], b1[:, :], ACT.Copy, scale=S_G).then_inc(par_ok, 1)
            act.activation(lns[:, :, :], lnp[:, :, :], ACT.Copy, scale=S_F).then_inc(par_ok, 1)

            def turn_out(t):
                act.wait_ge(a_turned, t + 1)
                v = ps16[0:P, 6:8, 0:640].rearrange("p a (s c) -> p a s c", c=128)[:, :, :, 0:P]
                o = adjT[:, :, bass.ds(t * P, P)].rearrange("p (a s) c -> p a s c", a=2)
                act.activation(o, v, ACT.Copy).then_inc(adj_out, 1)

            act.wait_ge(tab_ok, 1)
            split_hi(U_WK, SLOT_WK)

            def count_rows(i):
                for b in range(2):
                    t = 2 * i + b
                    act.wait_ge(ln_ve, t + 1)
                    act.activation(sd[:, b, :], ve[:, b, :], ACT.Sqrt).then_inc(ln_sd, 1)
                    end = act.value_load(tabs[0:1, bass.ds(t + 1, 1)], min_val=1, max_val=T * (HALF + 1))
                    act.wait_ge(hot_used, end + 2)
                    act.wait_ge(self_used, t + 1)
                    if later(i, b, 2):
                        act.wait_ge(a_turned, t - 1)
                    act.activation(a_row[:, b, 0:WIDE].rearrange("p (c w) -> p c w", c=3),
                                   ps[0:P, 3 * b:3 * b + 3, 0:417], ACT.Copy).then_inc(a_copied, 1)
                    if later(i, b):
                        turn_out(t - 1)
                    act.wait_ge(z_ok, t + 1)
                    act.activation(xn[:, 0, t, :], z1[:, b, :], ACT.Copy).then_inc(xn_hi, 1)
            first_units = [(U_WK, SLOT_WK), (U_WV, SLOT_WV), (U_WQ, SLOT_WQ), (U_W1, SLOT_W1), (U_W2, SLOT_W2)]
            tiles(act, count_rows)
            turn_out(T - 1)
            for u, s in first_units[1:]:
                split_hi(u, s)

            act.wait_ge(xn_lo, T)
            for u in range(4):
                split_hi(U_EIN + u, SLOT_EIN + u)

            def xcol(t):
                act.wait_ge(xcol_ps, t + 1)
                act.activation(xnT[:, :, :, bass.ds(t * P, P)],
                               ps[:, 6:8, 0:4 * P].rearrange("p a (k n) -> p a k n", k=KB),
                               ACT.Copy).then_inc(xcol_out, 1)

            act.wait_ge(bias_lo, 1)
            xcol(0)

            def keys(i, last=False):
                for b in range(2):
                    t = 2 * i + b
                    if not (last and b == 1):
                        xcol(t + 1)
                    act.wait_ge(k_ps, t + 1)
                    if later(i, b, 2):
                        act.wait_ge(k_done, t - 1)
                        act.wait_ge(kv_used, t - 1)
                    act.activation(ebuf[0:P, b, :], ps[0:P, 2 * b, :], ACT.Relu,
                                   scale=-1 / (S_X * S_W)).then_inc(k_neg, 1)
                    act.activation(kbuf[:, b, :], ps[0:P, 2 * b, :], ACT.Relu, scale=1 / (S_X * S_W))
                    act.wait_ge(k_neg, t + 1)
                    act.activation(ebuf[0:P, b, :], ebuf[0:P, b, :], ACT.Exp, scale=-1.0).then_inc(k_act, 1)
            keys(0)
            with act.Fori(1, T // 2 - 1) as i:
                keys(i)
            keys(T // 2 - 1, last=True)

            act.wait_ge(k_done, T)

            def queries(i):
                for m2 in range(2):
                    for c, (at, w) in enumerate(COLS):
                        n = 3 * m2 + c
                        bank = [0, 1, 2, 3, 6, 7][n]
                        act.wait_ge(q_ps, 6 * i + n + 1)
                        if not isinstance(i, int) or i or n >= 2:
                            act.wait_ge(q_done, 6 * i + n - 1)
                        act.activation(ebuf[:, n % 2, 0:w], ps[:, bank, 0:w], ACT.Relu,
                                       scale=-1 / (S_X * S_W)).then_inc(q_neg, 1)
                        act.activation(qT[:, 2 * i + m2, at:at + w], ps[:, bank, 0:w], ACT.Relu,
                                       scale=1 / (S_X * S_W))
                        act.wait_ge(q_neg, 6 * i + n + 1)
                        act.activation(ebuf[:, n % 2, 0:w], ebuf[:, n % 2, 0:w], ACT.Exp,
                                       scale=-1.0).then_inc(q_act, 1)
            queries(0)
            queries(1)
            act.wait_ge(kv_used, T)
            act.dma_start(b2b[:, :], d["b2"].broadcast_to((P, D))).then_inc(b2_in, 16)

            def sums(i):
                for m2 in range(2):
                    act.wait_ge(n_ps, 2 * i + m2 + 1)
                    for c, (at, w) in enumerate(COLS):
                        bank = [4, 5, 6, 7, 0, 1][3 * m2 + c]
                        act.activation(h1T[:, 0, 2 * i + m2, at:at + w], ps[:, bank, 0:w], ACT.Copy,
                                       scale=S_G / S_X).then_inc(n_hi, 1)
            sums(0)
            sums(1)
            act.wait_ge(att_added, 2 * T)
            act.wait_ge(o_ps, T)
            for u in range(4):
                split_hi(U_SIN + u, SLOT_SIN + u)

            act.wait_ge(par_ok, 2)

            def hidden(i):
                for m2 in range(2):
                    m = 2 * i + m2
                    for c, (at, w) in enumerate(COLS):
                        n = 3 * m2 + c
                        act.wait_ge(f1_ps, 6 * i + n + 1)
                        if not isinstance(i, int) or i or n >= 2:
                            act.wait_ge(g_lo, 6 * i + n - 1)
                        act.activation(rbuf[:, n % 2, 0:w], ps[:, 2 + n, 0:w], ACT.Relu,
                                       scale=1 / S_W, bias=b1s[:, m:m + 1])
                        act.activation(r1T[:, 0, m, at:at + w], ps[:, 2 + n, 0:w], ACT.Relu,
                                       scale=1 / S_W, bias=b1s[:, m:m + 1]).then_inc(g_act, 1)
            hidden(0)
            hidden(1)
            for u in range(2):
                split_hi(U_SOUT + u, SLOT_SOUT + u)

            def columns2(t, b, reused):
                act.wait_ge(zt_ps, t + 1)
                if reused:
                    act.wait_ge(gate_ps, t - 1)
                    act.wait_ge(f_lo, t - 1)
                for k in range(KB):
                    ins = act.activation(ft[:, b, k, :], ps[:, 6, k * P:(k + 1) * P], ACT.Identity,
                                         scale=lns[:, 0, k:k + 1], bias=lns[:, 1, k:k + 1])
                ins.then_inc(ft_act, 1)
                act.wait_ge(ft_act, t + 1)
                act.activation(fT[:, 0, :, bass.ds(t * P, P)], ft[:, b, :, :], ACT.Copy).then_inc(f_hi, 1)

            def store_hidden(t, b):
                act.wait_ge(ei_lo, 2 * t + 2)
                act.dma_start(hid_dram[bass.ds(t * P, P), :].rearrange("p (h c) -> p h c", h=2),
                              he[:, b, :, :]).then_inc(hid_out, 16)

            def ein_silu(t, b, j, reused):
                act.wait_ge(ei_ps, 2 * t + j + 1)
                if reused:
                    act.wait_ge(ei_mul, 2 * t + j - 1)
                act.activation(sil[:, j, :], ps[0:P, 2 * j, :], ACT.Silu,
                               scale=1 / (S_F * S_W)).then_inc(ei_sil, 1)

            def ein_high(t, b, j):
                act.wait_ge(ei_mul, 2 * t + j + 1)
                act.activation(he[:, b, 0, j * 512:(j + 1) * 512], h32[:, j, :], ACT.Copy).then_inc(ei_hi, 1)

            def norm2(i):
                for b in range(2):
                    t = 2 * i + b
                    act.wait_ge(ln_ve, T + t + 1)
                    act.activation(sd[:, b, :], ve[:, b, :], ACT.Sqrt).then_inc(ln_sd, 1)
                    if later(i, b):
                        ein_silu(t - 1, 1 - b, 0, later(i, b, 2))
                        if later(i, b, 3):
                            act.wait_ge(hid_out, 16 * (t - 2))
                        if later(i, b, 2):
                            store_hidden(t - 2, b)
                        ein_high(t - 1, 1 - b, 0)
                        ein_silu(t - 1, 1 - b, 1, later(i, b, 2))
                    columns2(t, b, later(i, b, 2))
                    if later(i, b):
                        ein_high(t - 1, 1 - b, 1)
            tiles(act, norm2, peeled=2)
            ein_silu(T - 1, 1, 0, True)
            act.wait_ge(hid_out, 16 * (T - 2))
            store_hidden(T - 2, 0)
            ein_high(T - 1, 1, 0)
            ein_silu(T - 1, 1, 1, True)
            ein_high(T - 1, 1, 1)
            for u in range(2):
                split_hi(U_EXP + u, u)
            store_hidden(T - 1, 1)

            act.wait_ge(sel_ok, 1)
            act.activation(rt[:, 2, :, 0:PER_GROUP], rt[:, 1, :, 0:PER_GROUP], ACT.Exp).then_inc(sel_exp, 1)
            act.wait_ge(hid_out, 16 * T)
            act.wait_ge(slots_ok, 1)
            act.wait_ge(eid_ok, 1)

            def sin(u, first):
                split_hi(U_EXP + 2 + u, 2 + u)
                for m2 in range(2):
                    for c, (at, w) in enumerate(COLS):
                        n = 3 * m2 + c
                        act.wait_ge(si_ps, 6 * u + n + 1)
                        if not first or n >= 2:
                            act.wait_ge(si_mul, 6 * u + n - 1)
                        act.activation(sil_s[:, n % 2, 0:w], ps[:, 2 * c, 0:w], ACT.Silu,
                                       scale=1 / (S_F * S_W)).then_inc(si_sil, 1)
                        act.wait_ge(si_mul, 6 * u + n + 1)
                        act.activation(hsh[:, 2 * u + m2, at:at + w], h32_s[:, n % 2, 0:w], ACT.Copy)\
                            .then_inc(si_hi, 1)
            sin(0, True)
            with act.Fori(1, 4) as u:
                sin(u, False)

            act.wait_ge(cnt_ps, 1)
            for g, n in ((0, 4), (1, 4), (2, 2)):
                act.activation(cntT[0:EXPERTS, g * 500:g * 500 + n * P], ps[0:EXPERTS, [6, 7, 0][g], 0:n * P],
                               ACT.Copy, scale=S_H).then_inc(cnt_ok, 1)

            act.wait_ge(pad_ok, 1)
            act.dma_start(out[N_NODES:N_NODES + 128, :], pad0[:, :]).then_inc(pad_out, 16)

            for u in range(6, 2 * EXPERTS - LATE):
                split_hi(U_EXP + u, u)

            def sout(i):
                for b in range(2):
                    t = 2 * i + b
                    act.wait_ge(so_done, t + 1)
                    act.dma_start(out[bass.ds(t * P, P), :], acc[:, b, :]).then_inc(acc_out, 16)
            with act.Fori(0, T // 2) as i:
                sout(i)

            act.wait_ge(acc_out, 16 * T)

            def turned_hi(i, b):
                j = 2 * i + b
                act.wait_ge(tr_ps, j + 1)
                if later(i, b, 2):
                    act.wait_ge(ex_ps, j - 1)
                act.activation(heT[:, b, 0, :, :], ps16[:, 4 + 2 * b, :].rearrange("p (h n) -> p h n", h=HB),
                               ACT.Copy).then_inc(ht_hi, 1)

            def weighted(i, b):
                j = 2 * i + b
                act.wait_ge(ex_ps, j + 1)
                if later(i, b, 2):
                    act.wait_ge(added, 16 * (j - 1))
                act.activation(y[:, b, :], ps[:, b, :], ACT.Copy, scale=wsl[:, bass.ds(j, 1)]).then_inc(y_ok, 1)

            def routed(i, units):
                for b in range(2):
                    turned_hi(i, 1) if b == 0 else turned_hi(i + 1, 0)
                    if units:
                        split_hi(2 * i + (U_LATE + b), 2 * i + (SLOT_LATE + b), (U_LATE + b) % 2)
                    weighted(i, b)
            turned_hi(0, 0)
            routed(0, True)
            with act.Fori(1, LATE // 2) as i:
                routed(i, True)
            with act.Fori(LATE // 2, MAX_TILES // 2) as i:
                routed(i, False)
            weighted(MAX_TILES // 2, 0)

        @block.vector
        def _(dve):
            steps = [0]

            def link(ins):
                steps[0] += 1
                ins.then_inc(dve_c, 1)
                dve.wait_ge(dve_c, steps[0])

            def split_lo(u, slot, half=None):
                half = u % 2 if half is None else half
                dve.wait_ge(w_hi, u + 1)
                dve.scalar_tensor_tensor(out=wslots[:, slot, 1, :], in0=stage[:, half, :], scalar=S_W,
                                         in1=wslots[:, slot, 0, :], op0=ALU.mult, op1=ALU.subtract)\
                   .then_inc(w_lo, 1)

            def stats(n, b, src, scale, add):
                dve.sem_inc(passed, 1)
                dve.bn_stats(st6[:, b, :], src).then_inc(ln_bn, 1)
                dve.wait_ge(ln_bn, n + 1)
                dve.sem_inc(passed, 1)
                dve.bn_aggr(mv[:, b, :], st6[:, b, :]).then_inc(ln_mv, 1)
                dve.wait_ge(ln_mv, n + 1)
                dve.tensor_scalar(ve[:, b, :], mv[:, b, 1:2], scale, add, ALU.mult, ALU.add).then_inc(ln_ve, 1)

            def normalise(n, b, src, dst, scale):
                dve.wait_ge(ln_sd, n + 1)
                dve.reciprocal(rst[:, b, 0:1], sd[:, b, :]).then_inc(ln_r, 1)
                dve.wait_ge(ln_r, 4 * n + 1)
                dve.tensor_scalar(rst[:, b, 1:2], ve[:, b, :], rst[:, b, 0:1], rst[:, b, 0:1],
                                  ALU.mult, ALU.mult).then_inc(ln_r, 1)
                dve.wait_ge(ln_r, 4 * n + 2)
                dve.tensor_scalar(rst[:, b, 2:3], rst[:, b, 1:2], -0.5, 1.5, ALU.mult, ALU.add).then_inc(ln_r, 1)
                dve.wait_ge(ln_r, 4 * n + 3)
                dve.tensor_scalar(rst[:, b, 3:4], rst[:, b, 2:3], rst[:, b, 0:1], scale,
                                  ALU.mult, ALU.mult).then_inc(ln_r, 1)
                dve.wait_ge(ln_r, 4 * n + 4)
                dve.tensor_scalar(dst, src, mv[:, b, 0:1], rst[:, b, 3:4],
                                  ALU.subtract, ALU.mult).then_inc(z_ok, 1)

            dve.wait_ge(edge_in, 48)
            dve.tensor_reduce(mnmx[:, 0:2], dst2[:, :, :], AX.X, ALU.max)
            link(dve.tensor_reduce(mnmx[:, 2:4], dst2[:, :, :], AX.X, ALU.min))
            dve.wait_ge(const_ok, 14)
            for q in range(4):
                ins = dve.tensor_scalar(diag[:, q, :], ident[0:HALF, 0:HALF], mnmx[:, q:q + 1], None, ALU.mult)
            ins.then_inc(diag_ok, 1)
            dve.wait_ge(rows_ps, 1)
            link(dve.tensor_scalar(rngf[:, 0, :], ps[0:T, 6, 0:CHUNKS], tlo[:, 0:1], None, ALU.is_ge))
            link(dve.scalar_tensor_tensor(out=rngf[:, 1, :], in0=ps[0:T, 6, CHUNKS:2 * CHUNKS], scalar=tlo[:, 1:2],
                                          in1=rngf[:, 0, :], op0=ALU.is_lt, op1=ALU.mult))
            link(dve.tensor_tensor(rngf[:, 2:4, :], rngf[:, 1:2, :].broadcast_to((T, 2, CHUNKS)), cup[:, :, :],
                                   ALU.mult))
            link(dve.tensor_reduce(rsm[:, 0:2], rngf[:, 2:4, :], AX.X, ALU.max))
            link(dve.tensor_scalar(rsm[:, 2:3], rsm[:, 0:1], 1.0, None, ALU.max))
            link(dve.tensor_scalar(rsm[:, 3:4], rsm[:, 2:3], -1.0, None, ALU.add))
            link(dve.tensor_scalar(rsm[:, 4:5], rsm[:, 1:2], -1.0, float(CHUNKS), ALU.mult, ALU.add))
            link(dve.tensor_tensor(rsm[:, 5:6], rsm[:, 4:5], rsm[:, 3:4], ALU.min))
            link(dve.tensor_tensor(rsm[:, 6:7], rsm[:, 2:3], rsm[:, 5:6], ALU.subtract))
            link(dve.tensor_scalar(rngf[:, 0, 0:HALF], even[:, :], rsm[:, 6:7], None, ALU.is_lt, ALU.add,
                                   accum_out=rsm[:, 7:8]))
            dve.tensor_copy(rs16[:, 0:1], rsm[:, 5:6])
            dve.tensor_copy(rs16[:, 1:2], rsm[:, 7:8]).then_inc(range_ok, 1)
            dve.wait_ge(tab_ps, 1)
            link(dve.tensor_copy(tabf[0:1, 0:T + 1], ps[0:1, 7, 0:T + 1]))
            link(dve.scalar_tensor_tensor(out=tabf[0:1, 16:16 + T], in0=tabf[0:1, 0:T], scalar=-2.0,
                                          in1=ps[0:1, 7, 16:16 + T], op0=ALU.mult, op1=ALU.add))
            dve.tensor_scalar(tabs[0:1, 16:16 + T], tabf[0:1, 16:16 + T], float(CO_SHIFT), None, ALU.add)
            link(dve.tensor_copy(tabs[0:1, 0:T + 1], tabf[0:1, 0:T + 1]))
            dve.nop().then_inc(tab_ok, 1)

            dve.wait_ge(edges_f, 2)
            dve.wait_ge(x_in, 32)
            split_lo(U_WK, SLOT_WK)

            def count_edges(i):
                for b in range(2):
                    t = 2 * i + b
                    if later(i, b):
                        dve.wait_ge(self_used, t)
                    dve.tensor_scalar(hot_self[:, 0:WIDE], iota[:, 0:WIDE], node_id[:, bass.ds(t, 1)], None,
                                      ALU.is_equal).then_inc(self_hot, 1)
                    stats(t, b, x_sb[:, t, :], 1.0, LN_EPS)
                    first = dve.value_load(tabs[0:1, bass.ds(t, 1)], min_val=0, max_val=T * (HALF + 1))
                    end = dve.value_load(tabs[0:1, bass.ds(t + 1, 1)], min_val=1, max_val=T * (HALF + 1))
                    off = dve.value_load(tabs[0:1, bass.ds(16 + t, 1)], min_val=0, max_val=2 * CO_SHIFT)
                    with dve.Fori(first, end) as v:
                        dve.wait_ge(hot_used, v + 1)
                        pair = nc.s_assert_within(v * 2 + off - CO_SHIFT, 0, CHUNKS,
                                                  skip_runtime_bounds_check_because=IN_RANGE)
                        for q in range(2):
                            chunk = pair + q
                            slot = (v % 2) * 2 + q
                            dve.tensor_scalar(hot_src[:, slot, 0:WIDE], iota[:, 0:WIDE],
                                              srcf[:, bass.ds(chunk, 1)], None, ALU.is_equal)
                            ins = dve.tensor_scalar(hot_dst[:, slot, 0:P], iota[:, bass.ds(t * P, P)],
                                                    dstf[:, bass.ds(chunk, 1)], None, ALU.is_equal)
                        ins.then_inc(hot_ready, 1)
                    if later(i, b, 2):
                        dve.wait_ge(xn_lo, t - 1)
                    normalise(t, b, x_sb[:, t, :], z1[:, b, :], S_X)
            tiles(dve, count_edges)
            for u, s in [(U_WV, SLOT_WV), (U_WQ, SLOT_WQ), (U_W1, SLOT_W1), (U_W2, SLOT_W2)]:
                split_lo(u, s)
            for u in range(4):
                split_lo(U_EIN + u, SLOT_EIN + u)
            dve.wait_ge(bias_hi, 1)
            dve.scalar_tensor_tensor(out=bias9[:, 1, :], in0=bias_in[:, :], scalar=S_W, in1=bias9[:, 0, :],
                                     op0=ALU.mult, op1=ALU.subtract).then_inc(bias_lo, 1)

            def keys(i):
                for b in range(2):
                    t = 2 * i + b
                    dve.wait_ge(v_ps, t + 1)
                    if later(i, b, 2):
                        dve.wait_ge(kv_used, t - 1)
                    dve.tensor_scalar(vbuf[:, b, :], ps[0:P, 2 * b + 1, :], 1 / (S_X * S_W * N_NODES), None,
                                      ALU.mult).then_inc(v_done, 1)
                    dve.wait_ge(k_act, t + 1)
                    dve.tensor_tensor(kbuf[:, b, :], ebuf[0:P, b, :], kbuf[:, b, :], ALU.add).then_inc(k_done, 1)
            tiles(dve, keys)

            def queries(i):
                for m2 in range(2):
                    for c, (at, w) in enumerate(COLS):
                        n = 3 * m2 + c
                        dve.wait_ge(q_act, 6 * i + n + 1)
                        o = qT[:, 2 * i + m2, at:at + w]
                        dve.tensor_tensor(o, ebuf[:, n % 2, 0:w], o, ALU.add).then_inc(q_done, 1)
            queries(0)
            queries(1)

            dve.wait_ge(kv_used, T)
            link(dve.memset(kvd[:, :, :], 0.0))
            for h, lo in ((0, 0), (1, 64)):
                rows = slice(lo, lo + 64)
                dve.tensor_scalar(kvd[rows, :, lo:lo + 64],
                                  ps[rows, 4, :].rearrange("p (a c) -> p a c", a=KB)[:, :, lo:lo + 64],
                                  float(N_NODES), None, ALU.mult)
                ins = dve.tensor_copy(kvd[rows, :, 128 + h:129 + h],
                                      ps[rows, 5, 0:8].rearrange("p (a c) -> p a c", a=KB)[:, :, 0:1])
            ins.then_inc(kvd_ok, 1)
            dve.wait_ge(q_done, 12)

            def attend(i):
                for b in range(2):
                    t = 2 * i + b
                    dve.wait_ge(o_ps, t + 1)
                    banks = ps[0:P, 2 * b:2 * b + 2, 0:260].rearrange("p a (q c) -> p a q c", q=2)
                    dve.tensor_scalar(den[:, b, 0, :].rearrange("p (a q h) -> p a q h", a=2, q=2),
                                      banks[:, :, :, 128:130], ATT_EPS, None, ALU.add).then_inc(den_c, 1)
                    dve.wait_ge(den_c, 2 * t + 1)
                    dve.reciprocal(den[:, b, 1, :], den[:, b, 0, :]).then_inc(den_c, 1)
                    dve.wait_ge(den_c, 2 * t + 2)
                    if later(i, b, 2):
                        dve.wait_ge(att_added, 2 * t - 2)
                    for g in range(2):
                        o = att[:, b, 256 * g:256 * g + 256].rearrange("p (q h c) -> p q h c", q=2, h=2)
                        s = ps[0:P, 2 * b + g, 0:260].rearrange("p (q c) -> p q c", q=2)[:, :, 0:128]\
                            .rearrange("p q (h c) -> p q h c", h=2)
                        z = den[:, b, 1, 4 * g:4 * g + 4].rearrange("p (q h c) -> p q h c", q=2, c=1)\
                            .broadcast_to((P, 2, 2, 64))
                        ins = dve.tensor_tensor(o, s, z, ALU.mult)
                    ins.then_inc(o_done, 1)
            tiles(dve, attend)

            for m in range(KB):
                for c, (at, w) in enumerate(COLS):
                    bank = [4, 5, 6, 7, 0, 1][3 * (m % 2) + c]
                    dve.wait_ge(n_hi, 3 * m + c + 1)
                    dve.scalar_tensor_tensor(out=h1T[:, 1, m, at:at + w], in0=ps[:, bank, 0:w], scalar=S_G / S_X,
                                             in1=h1T[:, 0, m, at:at + w], op0=ALU.mult, op1=ALU.subtract)\
                       .then_inc(n_lo, 1)
            for u in range(4):
                split_lo(U_SIN + u, SLOT_SIN + u)

            for m in range(KB):
                for c, (at, w) in enumerate(COLS):
                    n = 3 * m + c
                    dve.wait_ge(g_act, n + 1)
                    dve.tensor_tensor(r1T[:, 1, m, at:at + w], rbuf[:, n % 2, 0:w], r1T[:, 0, m, at:at + w],
                                      ALU.subtract).then_inc(g_lo, 1)
            for u in range(2):
                split_lo(U_SOUT + u, SLOT_SOUT + u)

            dve.wait_ge(att_added, 2 * T)
            dve.wait_ge(f1_ps, 12)
            dve.tensor_copy(identf[:, :], ident[:, :]).then_inc(identf_ok, 1)

            def ein_product(t, b, j, reused):
                dve.wait_ge(ei_sil, 2 * t + j + 1)
                if reused:
                    dve.wait_ge(ei_lo, 2 * t + j - 1)
                dve.scalar_tensor_tensor(out=h32[:, j, :], in0=ps[0:P, 2 * j + 1, :],
                                         scalar=S_H / (S_F * S_W), in1=sil[:, j, :],
                                         op0=ALU.mult, op1=ALU.mult).then_inc(ei_mul, 1)

            def logits(t):
                dve.wait_ge(gate_ps, t + 1)
                dve.scalar_tensor_tensor(out=lg[:, t, :], in0=ps[0:P, 7, 0:GATES], scalar=1 / S_F,
                                         in1=gb[:, :], op0=ALU.mult, op1=ALU.add).then_inc(lg_done, 1)

            def norm2(i):
                for b in range(2):
                    t = 2 * i + b
                    dve.wait_ge(w2_ps, t + 1)
                    dve.scalar_tensor_tensor(out=x_sb[:, t, :], in0=ps[0:P, 4 + b, :], scalar=1 / (S_G * S_W),
                                             in1=x_sb[:, t, :], op0=ALU.mult, op1=ALU.add).then_inc(x1_done, 1)
                    dve.wait_ge(x1_done, t + 1)
                    stats(T + t, b, x_sb[:, t, :], 1.0 + LN_EPS, LN_EPS * LN_EPS)
                    if later(i, b):
                        logits(t - 1)
                    if later(i, b, 2):
                        dve.wait_ge(zt_ps, t - 1)
                    normalise(T + t, b, x_sb[:, t, :], z2[:, b, :], 1.0)
                    if later(i, b):
                        for j in range(2):
                            ein_product(t - 1, 1 - b, j, later(i, b, 2))
                    dve.wait_ge(f_hi, t + 1)
                    dve.tensor_tensor(fT[:, 1, :, bass.ds(t * P, P)], ft[:, b, :, :],
                                      fT[:, 0, :, bass.ds(t * P, P)], ALU.subtract).then_inc(f_lo, 1)
            tiles(dve, norm2, peeled=2)
            logits(T - 1)
            for j in range(2):
                ein_product(T - 1, 1, j, True)
            for u in range(2):
                split_lo(U_EXP + u, u)

            dve.wait_ge(const2_ok, 1)
            dve.wait_ge(lg_done, T)

            def plane(k, n=EXPERTS):
                return rt[:, k, :, 0:n]

            def wide(ap, n):
                return ap.broadcast_to((P, T, n))

            pg = PER_GROUP
            in1st, in2nd, best = rt[:, 0, :, 0:1], rt[:, 0, :, 1:2], rt[:, 0, :, 2:3]
            second, total, inv = rt[:, 0, :, 3:4], rt[:, 0, :, 4:5], rt[:, 0, :, 5:6]
            c1, c2 = rt[:, 0, :, 6:7], rt[:, 0, :, 7:8]
            link(dve.tensor_tensor(in2nd, lg[:, :, 1:2], lg[:, :, 0:1], ALU.is_gt))
            link(dve.tensor_scalar(in1st, in2nd, -1.0, 1.0, ALU.mult, ALU.add))
            link(dve.tensor_tensor(plane(3, pg), lg[:, :, 2:2 + pg], wide(in1st, pg), ALU.mult))
            link(dve.tensor_tensor(plane(4, pg), lg[:, :, 2 + pg:2 + 2 * pg], wide(in2nd, pg), ALU.mult))
            link(dve.tensor_tensor(plane(3, pg), plane(3, pg), plane(4, pg), ALU.add))
            link(dve.tensor_reduce(best, plane(3, pg), AX.X, ALU.max))
            dve.tensor_tensor(plane(1, pg), plane(3, pg), wide(best, pg), ALU.subtract).then_inc(sel_ok, 1)
            link(dve.tensor_scalar(rt[:, 5, 0, 0:pg], iop[0:P, 0:pg], -1.0, float(pg), ALU.mult, ALU.add))
            rank4 = rt[:, 5, 0:1, 0:pg].broadcast_to((P, T, pg))
            dve.wait_ge(sel_exp, 1)
            link(dve.tensor_reduce(total, plane(2, pg), AX.X, ALU.add))
            link(dve.reciprocal(inv, total))
            link(dve.tensor_tensor(plane(2, pg), plane(2, pg), wide(inv, pg), ALU.mult))

            def choose(probs, value, hot):
                link(dve.tensor_reduce(value, probs, AX.X, ALU.max))
                link(dve.tensor_tensor(hot, probs, wide(value, pg), ALU.is_equal))
                link(dve.tensor_tensor(hot, hot, rank4, ALU.mult))
                link(dve.tensor_reduce(total, hot, AX.X, ALU.max))
                link(dve.tensor_tensor(hot, hot, wide(total, pg), ALU.is_equal))
            choose(plane(2, pg), best, plane(3, pg))
            link(dve.scalar_tensor_tensor(out=plane(6, pg), in0=plane(3, pg), scalar=-2.0, in1=plane(2, pg),
                                          op0=ALU.mult, op1=ALU.add))
            choose(plane(6, pg), second, plane(4, pg))
            link(dve.tensor_tensor(total, best, second, ALU.add))
            link(dve.tensor_scalar(total, total, 1e-8, None, ALU.add))
            link(dve.reciprocal(inv, total))
            link(dve.tensor_tensor(c1, best, inv, ALU.mult))
            link(dve.tensor_tensor(c2, second, inv, ALU.mult))
            for k in range(2):
                dve.tensor_tensor(oh8[:, k, :, 0:pg], plane(3 + k, pg), wide(in1st, pg), ALU.mult)
                link(dve.tensor_tensor(oh8[:, k, :, pg:], plane(3 + k, pg), wide(in2nd, pg), ALU.mult))
            link(dve.tensor_tensor(mask16[:, :, :], oh8[:, 0, :, :], oh8[:, 1, :, :], ALU.add))
            link(dve.memset(before[:, 0, :], 0.0))
            for t in range(T):
                link(dve.tensor_tensor(before[:, t + 1, :], before[:, t, :], mask16[:, t, :], ALU.add))
            dve.nop().then_inc(rank_in, 1)
            dve.memset(cntT[:, :], S_H)
            link(dve.tensor_scalar(thr[:, :], iop[0:P, 0:JW + 1], 128.0, None, ALU.mult))
            dve.nop().then_inc(const2_ok, 1)

            dve.wait_ge(rank_ps, 1)
            taken = rt[:, 7, :, :].rearrange("p t e -> p (t e)").rearrange("p (e k) -> p e k", e=EXPERTS)
            link(dve.tensor_tensor(
                taken, ps[0:P, 6, 128:136].rearrange("p (e k) -> p e k", k=1).broadcast_to((P, EXPERTS, T)),
                thr[:, 0:T].rearrange("p (e k) -> p e k", e=1).broadcast_to((P, EXPERTS, T)), ALU.is_gt))
            n_e, incl, start_e, ones8 = rt[:, 8, 0, :], rt[:, 8, 1, :], rt[:, 8, 2, :], rt[:, 8, 3, :]
            link(dve.tensor_reduce(n_e, taken, AX.X, ALU.add))
            link(dve.tensor_scalar(n_e, n_e, 1.0, None, ALU.max))
            link(dve.memset(ones8, 1.0))
            link(dve.tensor_tensor_scan(incl, ones8, n_e, 0.0, ALU.mult, ALU.add))
            link(dve.tensor_tensor(start_e, incl, n_e, ALU.subtract))
            eids = rt[0:1, 10:12, :, :].rearrange("p a t e -> p (a t e)")
            hits = ge16[0:1, 0:8, :].rearrange("p a b -> p (a b)")[:, 0:JW * (EXPERTS - 1)]\
                .rearrange("p (j e) -> p j e", j=JW)
            link(dve.tensor_tensor(
                hits, rt[0:1, 8, 2:3, 1:EXPERTS].broadcast_to((1, JW, EXPERTS - 1)),
                iop[0:1, 0:JW].rearrange("p (j e) -> p j e", e=1).broadcast_to((1, JW, EXPERTS - 1)), ALU.is_le))
            link(dve.tensor_reduce(eids[:, 0:JW], hits, AX.X, ALU.add))
            dve.tensor_copy(eidt[:, :], eids[:, 0:JW]).then_inc(eid_ok, 1)
            link(dve.tensor_scalar(rt[:, 8, 4, :], start_e, 128.0, None, ALU.mult))
            link(dve.tensor_tensor(plane(6), ps[0:P, 6, 0:T * EXPERTS].rearrange("p (t e) -> p t e", t=T),
                                   rt[:, 8, 4:5, :].broadcast_to((P, T, EXPERTS)), ALU.add))
            slot_f, j_f, p_f, lo_f = tk[:, 0, :], tk[:, 1, :], tk[:, 2, :], tk[:, 3, :]
            for k in range(2):
                link(dve.tensor_tensor(plane(7), oh8[:, k, :, :], plane(6), ALU.mult))
                link(dve.tensor_reduce(slot_f[:, k * T:(k + 1) * T], plane(7), AX.X, ALU.add))
            link(dve.tensor_tensor(ge16[:, :, :],
                                   slot_f.rearrange("p (n j) -> p n j", j=1).broadcast_to((P, 2 * T, JW + 1)),
                                   thr[:, :].rearrange("p (n j) -> p n j", n=1).broadcast_to((P, 2 * T, JW + 1)),
                                   ALU.is_ge))
            link(dve.tensor_reduce(j_f, ge16[:, :, 1:], AX.X, ALU.add))
            link(dve.scalar_tensor_tensor(out=p_f, in0=j_f, scalar=-128.0, in1=slot_f, op0=ALU.mult, op1=ALU.add))
            dve.tensor_tensor(hot_p[:, :, :],
                              iop[0:P, :].rearrange("p (n j) -> p n j", n=1).broadcast_to((P, 2 * T, 128)),
                              p_f.rearrange("p (n j) -> p n j", j=1).broadcast_to((P, 2 * T, 128)), ALU.is_equal)
            link(dve.tensor_tensor(hot_j[:, :, 3, :], ge16[:, :, 0:JW], ge16[:, :, 1:], ALU.subtract))
            link(dve.tensor_copy(tk[:, 4, 0:T].rearrange("p (t o) -> p t o", o=1), c1))
            link(dve.tensor_copy(tk[:, 4, T:2 * T].rearrange("p (t o) -> p t o", o=1), c2))
            link(dve.tensor_copy(c16[:, :], tk[:, 4, :]))
            link(dve.tensor_tensor(lo_f, tk[:, 4, :], c16[:, :], ALU.subtract))

            def spread(ap):
                return ap.rearrange("p (n j) -> p n j", j=1).broadcast_to((P, 2 * T, JW))
            for k in range(2):
                half = slice(k * T, (k + 1) * T)
                dve.tensor_tensor(hot_j[:, half, 0, :], hot_j[:, half, 3, :],
                                  node_id[:, :].rearrange("p (n j) -> p n j", j=1).broadcast_to((P, T, JW)), ALU.mult)
            dve.tensor_tensor(hot_j[:, :, 1, :], hot_j[:, :, 3, :], spread(c16[:, :]), ALU.mult)
            dve.tensor_tensor(hot_j[:, :, 2, :], hot_j[:, :, 3, :], spread(lo_f), ALU.mult).then_inc(hots_ok, 1)
            dve.wait_ge(slot_ps, 1)
            node_s, whi_s, wlo_s, full_s = (ps[:, 7, JW * k:JW * (k + 1)] for k in range(4))
            dve.tensor_copy(gidx[:, :], node_s)
            link(dve.tensor_scalar(wsl[:, :], wlo_s, 1 / (S_H * S_W), None, ALU.mult))
            link(dve.scalar_tensor_tensor(out=wsl[:, :], in0=whi_s, scalar=1 / (S_H * S_W), in1=wsl[:, :],
                                          op0=ALU.mult, op1=ALU.add))
            link(dve.tensor_scalar(padw[:, 0:JW], full_s, -1.0, 1.0, ALU.mult, ALU.add))
            dve.scalar_tensor_tensor(out=sidx[:, :], in0=padw[:, 0:JW], scalar=pad_row[:, :], in1=node_s,
                                     op0=ALU.mult, op1=ALU.add).then_inc(slots_ok, 1)

            def sin(u, first):
                split_lo(U_EXP + 2 + u, 2 + u)
                for m2 in range(2):
                    for c, (at, w) in enumerate(COLS):
                        n = 3 * m2 + c
                        dve.wait_ge(si_sil, 6 * u + n + 1)
                        if not first or n >= 2:
                            dve.wait_ge(si_lo, 6 * u + n - 1)
                        dve.scalar_tensor_tensor(out=h32_s[:, n % 2, 0:w], in0=ps[:, 2 * c + 1, 0:w],
                                                 scalar=S_H / (S_F * S_W), in1=sil_s[:, n % 2, 0:w],
                                                 op0=ALU.mult, op1=ALU.mult).then_inc(si_mul, 1)
            sin(0, True)
            with dve.Fori(1, 4) as u:
                sin(u, False)
            for u in range(6, 2 * EXPERTS - LATE):
                split_lo(U_EXP + u, u)

            dve.wait_ge(si_lo, 24)

            def sout(i):
                for b in range(2):
                    t = 2 * i + b
                    dve.wait_ge(so_ps, t + 1)
                    if later(i, b):
                        dve.wait_ge(acc_out, 16 * t)
                    dve.scalar_tensor_tensor(out=acc[:, b, :], in0=ps[0:P, 6 + b, :], scalar=1 / (S_H * S_W),
                                             in1=x_sb[:, t, :], op0=ALU.mult, op1=ALU.add).then_inc(so_done, 1)
            tiles(dve, sout)

            def turned_lo(i, b):
                j = 2 * i + b
                dve.wait_ge(tr_ps, j + 1)
                if later(i, b, 2):
                    dve.wait_ge(ex_ps, j - 1)
                dve.tensor_copy(heT[:, b, 1, :, :], ps16[:, 5 + 2 * b, :].rearrange("p (h n) -> p h n", h=HB))\
                   .then_inc(ht_lo, 1)

            def routed(i, units):
                for b in range(2):
                    turned_lo(i, 1) if b == 0 else turned_lo(i + 1, 0)
                    if units:
                        split_lo(2 * i + (U_LATE + b), 2 * i + (SLOT_LATE + b), (U_LATE + b) % 2)
            turned_lo(0, 0)
            routed(0, True)
            with dve.Fori(1, LATE // 2) as i:
                routed(i, True)
            with dve.Fori(LATE // 2, MAX_TILES // 2) as i:
                routed(i, False)

        @block.tensor
        def _(pe):
            def product(out_ap, left, right, blocks, start=True, stop=True):
                for k in range(blocks):
                    for lh, rh in ((0, 0), (0, 1), (1, 0)):
                        ins = pe.matmul(out_ap, left(lh, k), right(rh, k), start=start and k + lh + rh == 0,
                                        stop=stop and k == blocks - 1 and lh == 1)
                return ins

            def weight(slot, h, k, at=0, n=512):
                return wslots[:, slot, h, k * 512 + at:k * 512 + at + n] if isinstance(at, int) else \
                    wslots[:, slot, h, bass.ds(at + k * 512, n)]

            pe.wait_ge(diag_ok, 1)
            pe.matmul(ps[0:T, 6, 0:4 * HALF], ones[0:HALF, 0:T], diag[:, :, :], start=True, stop=True)\
              .then_inc(rows_ps, 1)
            pe.wait_ge(range_ok, 1)
            pe.matmul(ps[0:1, 7, 0:T + 1], rs16[:, 1:2], tri[0:T, 0:T + 1], start=True, stop=True)
            pe.matmul(ps[0:1, 7, 16:16 + T], rs16[:, 0:1], ident[0:T, 0:T], start=True, stop=True)\
              .then_inc(tab_ps, 1)
            pe.wait_ge(tab_ok, 1)

            def turn(t, b, reused):
                pe.wait_ge(a_copied, t + 1)
                if reused:
                    pe.wait_ge(adj_out, t)
                for s in range(T):
                    ins = pe.transpose(ps16[0:P, 6 + s // 5, (s % 5) * 128:(s % 5) * 128 + P],
                                       a_row[:, b, s * P:(s + 1) * P], ident[0:P, 0:P])
                ins.then_inc(a_turned, 1)

            def count(i):
                for b in range(2):
                    t = 2 * i + b
                    pe.wait_ge(self_hot, t + 1)
                    if later(i, b, 2):
                        pe.wait_ge(a_copied, t - 1)
                    for c in range(3):
                        ins = pe.matmul(ps[0:P, 3 * b + c, 0:417], ident[0:P, 0:P], hot_self[:, c * 417:(c + 1) * 417],
                                        start=True, stop=True)
                    ins.then_inc(self_used, 1)
                    if not later(i, b):
                        pe.sem_inc(hot_used, 2)
                    first = pe.value_load(tabs[0:1, bass.ds(t, 1)], min_val=0, max_val=T * (HALF + 1))
                    end = pe.value_load(tabs[0:1, bass.ds(t + 1, 1)], min_val=1, max_val=T * (HALF + 1))
                    with pe.Fori(first, end) as v:
                        pe.wait_ge(hot_ready, v + 1)
                        for q in range(2):
                            slot = (v % 2) * 2 + q
                            for c in range(3):
                                ins = pe.matmul(ps[0:P, 3 * b + c, 0:417], hot_dst[:, slot, 0:P],
                                                hot_src[:, slot, c * 417:(c + 1) * 417], start=False, stop=True,
                                                skip_group_check=True)
                        ins.then_inc(hot_used, 1)
                    if later(i, b):
                        turn(t - 1, 1 - b, later(i, b, 2))
            tiles(pe, count)
            turn(T - 1, 1, True)

            def xcol(t, first=False):
                pe.wait_ge(xn_lo, t + 1)
                if not first:
                    pe.wait_ge(xcol_out, t)
                for h in range(2):
                    for k in range(KB):
                        ins = pe.matmul(ps[:, 6 + h, k * P:(k + 1) * P], xn[:, h, t, k * 128:(k + 1) * 128],
                                        ident[0:P, 0:P], start=True, stop=True)
                ins.then_inc(xcol_ps, 1)

            def state(t, b, first, last):
                pe.wait_ge(k_done, t + 1)
                pe.wait_ge(v_done, t + 1)
                for a in range(KB):
                    k = kbuf[:, b, a * 128:(a + 1) * 128]
                    pe.matmul(ps[:, 4, a * 128:(a + 1) * 128], k, vbuf[:, b, a * 128:(a + 1) * 128],
                              start=first and a == 0, stop=True, skip_group_check=True)
                    ins = pe.matmul(ps[:, 5, 2 * a:2 * a + 2], k, onesf[0:P, :], start=first and a == 0, stop=True,
                                    skip_group_check=True)
                ins.then_inc(kv_used, 1)

            def keys(i, last=False):
                for b in range(2):
                    t = 2 * i + b
                    if not (last and b == 1):
                        xcol(t + 1)
                    pe.wait_ge(xcol_out, t + 1)
                    for bank, s, done, free in ((2 * b, SLOT_WK, k_ps, k_act), (2 * b + 1, SLOT_WV, v_ps, v_done)):
                        if later(i, b, 2):
                            pe.wait_ge(free, t - 1)
                        product(ps[0:P, bank, :], lambda h, k: xnT[:, h, k, bass.ds(t * P, P)],
                                lambda h, k: weight(s, h, k), KB).then_inc(done, 1)
                    if later(i, b):
                        state(t - 1, 1 - b, isinstance(i, int) and i == 0 and b == 1, False)
            pe.wait_ge(adj_out, T)
            pe.wait_ge(a_copied, T)
            pe.wait_ge(w_lo, U_WV + 1)
            xcol(0, first=True)
            keys(0)
            with pe.Fori(1, T // 2 - 1) as i:
                keys(i)
            keys(T // 2 - 1, last=True)
            state(T - 1, 1, False, True)

            pe.wait_ge(k_act, T)
            pe.wait_ge(v_done, T)
            pe.wait_ge(w_lo, U_WQ + 1)
            for m in range(KB):
                for c, (at, w) in enumerate(COLS):
                    n = 3 * m + c
                    if n >= 6:
                        pe.wait_ge(q_act, n - 5)
                    product(ps[:, [0, 1, 2, 3, 6, 7][n % 6], 0:w],
                            lambda h, k: weight(SLOT_WQ, h, k, m * 128, 128),
                            lambda h, k: xnT[:, h, k, at:at + w], KB).then_inc(q_ps, 1)

            pe.wait_ge(q_done, 12)
            pe.wait_ge(kvd_ok, 1)
            for t in range(T):
                if t >= 2:
                    pe.wait_ge(o_done, t - 1)
                for a in range(KB):
                    ins = pe.matmul(ps[0:P, 2 * (t % 2) + a // 2, (a % 2) * 130:(a % 2) * 130 + 130],
                                    qT[:, a, t * P:(t + 1) * P], kvd[:, a, :], start=True, stop=True)
                ins.then_inc(o_ps, 1)

            pe.wait_ge(q_act, 12)
            for m in range(KB):
                banks = [4, 5, 6, 7, 0, 1][3 * (m % 2):3 * (m % 2) + 3]
                if m == 1:
                    pe.wait_ge(o_done, T)
                if m >= 2:
                    pe.wait_ge(n_lo, 3 * (m - 1))
                for s in range(T):
                    for h in range(2):
                        for c, (at, w) in enumerate(COLS):
                            ins = pe.matmul(ps[:, banks[c], 0:w], xn[:, h, s, m * 128:(m + 1) * 128],
                                            adjT[:, s, at:at + w], start=s + h == 0, stop=s == T - 1 and h == 1)
                ins.then_inc(n_ps, 1)

            pe.wait_ge(n_lo, 12)
            pe.wait_ge(w_lo, U_W2 + 1)
            for m in range(KB):
                for c, (at, w) in enumerate(COLS):
                    n = 3 * m + c
                    if n >= 6:
                        pe.wait_ge(g_act, n - 5)
                    product(ps[:, 2 + n % 6, 0:w], lambda h, k: weight(SLOT_W1, h, k, m * 128, 128),
                            lambda h, k: h1T[:, h, k, at:at + w], KB).then_inc(f1_ps, 1)

            pe.wait_ge(g_lo, 12)
            pe.wait_ge(identf_ok, 1)
            pe.wait_ge(g_act, 12)

            def turn2(t, b, reused):
                pe.wait_ge(z_ok, T + t + 1)
                if reused:
                    pe.wait_ge(ft_act, t)
                for k in range(KB):
                    ins = pe.transpose(ps[:, 6, k * P:(k + 1) * P], z2[:, b, k * 128:(k + 1) * 128],
                                       identf[0:P, 0:P])
                ins.then_inc(zt_ps, 1)

            def gates(t, b, reused):
                pe.wait_ge(ft_act, t + 1)
                if reused:
                    pe.wait_ge(lg_done, t)
                for k in range(KB):
                    ins = pe.matmul(ps[0:P, 7, 0:GATES], ft[:, b, k, :], gw[:, k, :], start=k == 0,
                                    stop=k == KB - 1)
                ins.then_inc(gate_ps, 1)

            def ein(t, reused):
                pe.wait_ge(f_lo, t + 1)
                for j in range(2):
                    if reused:
                        pe.wait_ge(ei_mul, 2 * t + j - 1)
                    for half in range(2):
                        ins = product(ps[0:P, 2 * j + half, :],
                                      lambda h, k: fT[:, h, k, bass.ds(t * P, P)],
                                      lambda h, k: weight(SLOT_EIN + 2 * half + j, h, k), KB)
                    ins.then_inc(ei_ps, 1)

            def norm2(i):
                for b in range(2):
                    t = 2 * i + b
                    if later(i, b, 2):
                        pe.wait_ge(x1_done, t - 1)
                    product(ps[0:P, 4 + b, :], lambda h, k: r1T[:, h, k, bass.ds(t * P, P)],
                            lambda h, k: weight(SLOT_W2, h, k), KB).then_inc(w2_ps, 1)
                    if later(i, b):
                        gates(t - 1, 1 - b, later(i, b, 2))
                        ein(t - 1, later(i, b, 2))
                    turn2(t, b, later(i, b))
            tiles(pe, norm2, peeled=2)
            gates(T - 1, 1, True)
            ein(T - 1, True)

            pe.wait_ge(ei_mul, 2 * T)
            pe.wait_ge(rank_in, 1)
            pe.matmul(ps[0:P, 6, 0:T * EXPERTS], ones[0:P, 0:P], before[:, 0:T, :], start=True, stop=False)
            pe.matmul(ps[0:P, 6, 0:T * EXPERTS], tri[0:P, 0:P], mask16[:, :, :], start=False, stop=True)
            pe.matmul(ps[0:P, 6, 128:128 + EXPERTS], ones[0:P, 0:P], before[:, T, :], start=True, stop=True)\
              .then_inc(rank_ps, 1)
            pe.wait_ge(hots_ok, 1)
            for n in range(2 * T):
                ins = pe.matmul(ps[:, 7, 0:4 * JW], hot_p[:, n, :], hot_j[:, n, :, :], start=n == 0,
                                stop=n == 2 * T - 1)
            ins.then_inc(slot_ps, 1)

            pe.wait_ge(w_lo, U_SIN + 4)

            def sin(u, first):
                for m2 in range(2):
                    for c, (at, w) in enumerate(COLS):
                        n = 3 * m2 + c
                        if not first or n >= 3:
                            pe.wait_ge(si_mul, 6 * u + n - 2)
                        for half in range(2):
                            ins = product(
                                ps[:, 2 * c + half, 0:w],
                                lambda h, k: wslots[:, SLOT_SIN + u, h,
                                                    ((m2 * 2 + half) * KB + k) * 128:((m2 * 2 + half) * KB + k + 1) * 128],
                                lambda h, k: fT[:, h, k, at:at + w], KB)
                        ins.then_inc(si_ps, 1)
            sin(0, True)
            with pe.Fori(1, 4) as u:
                sin(u, False)

            pe.wait_ge(slots_ok, 1)
            pe.wait_ge(si_mul, 24)
            for t in range(T):
                ins = pe.matmul(ps[0:EXPERTS, [6, 7, 0][t // 4], (t % 4) * P:(t % 4 + 1) * P], mask16[:, t, :],
                                ident[0:P, 0:P], start=True, stop=True)
            ins.then_inc(cnt_ps, 1)

            pe.wait_ge(cnt_ok, 3)
            pe.wait_ge(si_lo, 24)
            pe.wait_ge(w_lo, U_SOUT + 2)

            def sout(i):
                for b in range(2):
                    t = 2 * i + b
                    if later(i, b, 2):
                        pe.wait_ge(so_done, t - 1)
                    out_ap = ps[0:P, 6 + b, :]
                    for h in range(2):
                        pe.matmul(out_ap, cntT[:, bass.ds(t * P, P)], bias9[:, h, :], start=h == 0, stop=False)
                    product(out_ap, lambda h, k: (hsl if h else hsh)[:, k, bass.ds(t * P, P)],
                            lambda h, k: weight(SLOT_SOUT + k // 4, h, k % 4), HB, start=False).then_inc(so_ps, 1)
            tiles(pe, sout)

            def turn_rows(i, b):
                j = 2 * i + b
                pe.wait_ge(got_ok[b], 16 * i + 16)
                if later(i, b, 2):
                    pe.wait_ge(ht_hi, j - 1)
                    pe.wait_ge(ht_lo, j - 1)
                for h in range(2):
                    for k in range(HB):
                        ins = pe.transpose(ps16[:, 4 + 2 * b + h, k * 128:(k + 1) * 128],
                                           got[:, b, h * HID + k * 128:h * HID + (k + 1) * 128], ident[:, :])
                ins.then_inc(tr_ps, 1)

            def expert(i, b):
                j = 2 * i + b
                e = pe.value_load(eidt[0:1, bass.ds(j, 1)], min_val=0, max_val=EXPERTS - 1)
                pe.wait_ge(ht_hi, j + 1)
                pe.wait_ge(ht_lo, j + 1)
                if later(i, b, 2):
                    pe.wait_ge(y_ok, j - 1)
                pe.wait_ge(w_lo, e * 2 + U_EXP + 2)
                product(ps[:, b, :], lambda h, k: heT[:, b, h, k, :],
                        lambda h, k: weight(e * 2 + k // 4, h, k % 4), HB).then_inc(ex_ps, 1)

            pe.wait_ge(eid_ok, 1)
            pe.wait_ge(so_done, T)
            turn_rows(0, 0)

            def routed(i):
                turn_rows(i, 1)
                expert(i, 0)
                turn_rows(i + 1, 0)
                expert(i, 1)
            routed(0)
            with pe.Fori(1, MAX_TILES // 2) as i:
                routed(i)
            expert(MAX_TILES // 2, 0)


_OUT_ROWS = N_NODES + 128


def kernel(**inputs):
    import numpy as _np
    import concourse.bacc as _bacc
    from concourse import mybir as _mybir
    from concourse.bass_utils import run_bass_kernel_spmd as _run

    a = {k: _np.asarray(v) for k, v in inputs.items()}

    def units(w):
        n_in, n_out = w.shape
        w = w.reshape(n_in // 512, 4, 128, n_out // 512, 512)
        return w.transpose(3, 0, 2, 1, 4).reshape(-1, 128, UNIT)

    def paired(w):
        w = w.reshape(KB, 128, 2, 4, 2, 128)
        return w.transpose(3, 1, 4, 2, 0, 5).reshape(4, 128, UNIT)

    kv = a["L0_mix_Wkv"].T
    weights = [units(kv[:, :D]), units(kv[:, D:]), units(a["L0_mix_Wq"].T), units(a["L0_gnn_W1"]),
               units(a["L0_gnn_W2"]), units(a["L0_ffn_expert_in_w"].T), paired(a["L0_ffn_shared_in_w"].T),
               units(a["L0_ffn_shared_out_w"].T)]
    weights += [units(a["L0_ffn_expert_out_weight"][e].T) for e in range(EXPERTS)]
    gate = _np.concatenate([a["L0_ffn_group_gate_w"], a["L0_ffn_expert_gate_w"]])
    arrays = {
        "x": a["x"],
        "dst_rows": a["dst"].reshape(2, HALF, P).transpose(1, 0, 2),
        "dst_cols": a["dst"].reshape(CHUNKS, P).T,
        "src_cols": a["src"].reshape(CHUNKS, P).T,
        "weights": _np.concatenate(weights),
        "b1": a["L0_gnn_b1"].reshape(KB, 128).T,
        "b2": a["L0_gnn_b2"].reshape(1, D),
        "ln_scale": a["L0_ffn_ln_scale"].reshape(KB, 128).T,
        "ln_bias": a["L0_ffn_ln_bias"].reshape(KB, 128).T,
        "gate_w": gate.T.reshape(KB, 128, GATES).transpose(1, 0, 2),
        "gate_b": _np.concatenate([a["L0_ffn_group_bias"], a["L0_ffn_expert_bias"]]).reshape(1, GATES),
        "expert_b": a["L0_ffn_expert_out_bias"],
        "shared_b": a["L0_ffn_shared_out_b"].reshape(1, D),
    }
    arrays = {k: _np.ascontiguousarray(v) for k, v in arrays.items()}
    nc = _bacc.Bacc("TRN2", target_bir_lowering=False, num_devices=1)
    dram = {k: nc.dram_tensor(k, v.shape, _mybir.dt.from_np(v.dtype), kind="ExternalInput").ap()
            for k, v in arrays.items()}
    out = nc.dram_tensor("out", (_OUT_ROWS, D), F32, kind="ExternalOutput").ap()
    hid = nc.dram_tensor("hid", (N_NODES, 2 * HID), F16, kind="Internal").ap()
    gps_layer(nc, dram, out, hid)
    r = _run(nc, [arrays], core_ids=[0])
    return r.results[0]["out"][:N_NODES]
```

```python
from contextlib import ExitStack

import numpy as np

import concourse.bass as bass
from concourse import mybir

F32 = mybir.dt.float32
F16 = mybir.dt.float16
I32 = mybir.dt.int32
U32 = mybir.dt.uint32
ALU = mybir.AluOpType
ACT = mybir.ActivationFunctionType
AX = mybir.AxisListType

N_NODES, D, HEADS, HID = 1250, 512, 8, 1024
N_EDGES = 21250
P = 125
T = N_NODES // P
KB = D // 128
HB = HID // 128
EXPERTS, GROUPS, PER_GROUP = 8, 2, 4
GATES = GROUPS + EXPERTS
CHUNKS = N_EDGES // P
HALF = CHUNKS // 2
RING = 4
COLS = [(0, 417), (417, 417), (834, 416)]
WIDE = 3 * 417
UNIT = 2048
MAX_TILES = (2 * N_NODES + EXPERTS * 127) // 128
JW = 32

U_WK, U_WV, U_WQ, U_W1, U_W2, U_EIN, U_SIN, U_SOUT, U_EXP = 0, 1, 2, 3, 4, 5, 9, 13, 15
N_UNITS = U_EXP + 2 * EXPERTS
LATE = 8
U_LATE = N_UNITS - LATE
SLOT_WK, SLOT_WV, SLOT_WQ, SLOT_W1, SLOT_W2 = 4, 5, 6, 14, 15
SLOT_EIN, SLOT_SIN, SLOT_SOUT, SLOT_LATE = 0, 4, 11, 16 - LATE

S_X = 2.0 ** 8
S_F = 2.0 ** 6
S_W = 2.0 ** 8
S_G = 2.0 ** -4
S_H = 2.0 ** 4
LN_EPS = 1e-5
ATT_EPS = 1e-6
IN_RANGE = "the tables of the chunk search stay within the chunks"
CO_SHIFT = 4096


class Region:

    def __init__(self, nc, start, size):
        self.nc, self.at, self.end = nc, start, start + size

    def put(self, name, shape, dt):
        size = int(np.prod(shape[1:])) * (2 if dt == F16 else 4)
        t = self.nc.alloc_sbuf_tensor_at(name, list(shape), dt, offset=self.at, align_bytes=4)
        self.at += (size + 3) // 4 * 4
        assert self.at <= self.end, (name, self.at, self.end)
        return t


def gps_layer(nc, d, out, hid_dram):
    with ExitStack() as ctx:
        base = (nc.sbuf_base + 31) // 32 * 32
        slot_bytes = 2 * UNIT * 2

        def region(start, size):
            return Region(nc, start, size)

        def slots(first, n=1):
            return region(base + first * slot_bytes, n * slot_bytes)

        top = base + 16 * slot_bytes
        r_x = region(top, T * D * 4)
        r_stage = region(r_x.end, 2 * UNIT * 4)
        r_f = region(r_stage.end, T * D * 4)
        r_g = region(r_f.end, 20000)
        small = region(r_g.end, nc.sbuf_usable_end - r_g.end)

        wslots = slots(0, 16).put("wslots", [128, 16, 2, UNIT], F16)
        x_sb = r_x.put("x_sb", [P, T, D], F32)
        stage = r_stage.put("stage", [128, 2, UNIT], F32)

        def again(r):
            return region(r.end - size_of[r], size_of[r])

        size_of = {r_f: T * D * 4, r_g: 20000}
        xn = r_f.put("xn", [P, 2, T, D], F16)
        xnT = r_g.put("xnT", [128, 2, KB, N_NODES], F16)
        h1T = again(r_g).put("h1T", [128, 2, KB, N_NODES], F16)
        r = slots(0, 4)
        hot_dst = r.put("hot_dst", [P, 2 * RING, P + 1], F16)
        a_row = r.put("a_row", [P, WIDE + 1], F16)
        band = r.put("band", [P, N_NODES - P + WIDE + 1], F16)
        z1 = r.put("z1", [P, 2, D], F32)
        ekey = r.put("ekey", [P, 2, D], F32)
        ksum = r.put("ksum", [P, D], F32)
        bias_in = r.put("bias_in", [EXPERTS + 1, D], F32)
        srci = r.put("srci", [P, CHUNKS], I32)
        dsti = r.put("dsti", [P, CHUNKS], I32)
        srcf = r.put("srcf", [P, CHUNKS + 2], F32)
        dstf = r.put("dstf", [P, CHUNKS + 2], F32)
        dst2 = r.put("dst2", [HALF, 2, P], I32)
        diag = r.put("diag", [HALF, 4, HALF], F16)
        mnmx = r.put("mnmx", [HALF, 4], F32)
        rngf = r.put("rngf", [T, 4, CHUNKS], F32)
        cup = r.put("cup", [T, 2, CHUNKS], F32)
        rsm = r.put("rsm", [T, 8], F32)
        rs16 = r.put("rs16", [T, 2], F16)
        even = r.put("even", [T, HALF], F32)
        st1 = r.put("st1", [P, T, 6], F32)
        mv1 = r.put("mv1", [P, T, 2], F32)
        r1 = r.put("r1", [P, 8, T], F32)
        r = slots(8, 3)
        hot_src = r.put("hot_src", [P, 2 * RING, WIDE + 1], F16)
        iota = r.put("iota", [P, WIDE + 1], F16)
        r = slots(7)
        kbuf = r.put("kbuf", [P, 2, D], F32)
        vbuf = r.put("vbuf", [P, 2, D], F32)
        r = slots(7)
        kvd = r.put("kvd", [128, KB, 130], F32)
        b2b = r.put("b2b", [P, D], F32)
        r_q = slots(8, 3)
        qT = r_q.put("qT", [128, KB, N_NODES], F32)
        spare = (r_q.at, r_q.end - 424 - r_q.at)
        r1T = slots(8, 3).put("r1T", [128, 2, KB, N_NODES], F16)
        ebuf = region(*spare).put("ebuf", [128, 2, D], F32)
        att = region(*spare).put("att", [P, 2, D], F32)
        rbuf = region(*spare).put("rbuf", [128, 2, 417], F32)
        adjT = region(r_q.end - 424, 3 * slot_bytes + 424).put("adjT", [P, T, N_NODES], F16)
        fT = again(r_f).put("fT", [128, 2, KB, N_NODES], F16)
        r = again(r_g)
        z2 = r.put("z2", [P, 2, D], F32)
        ft = r.put("ft", [128, 2, KB, P], F32)
        hot_p = r.put("hot_p", [P, 2 * T, 128], F16)
        hot_j = r.put("hot_j", [P, 2 * T, 4, JW], F16)
        lg = r.put("lg", [P, T, GATES], F32)
        identf = r.put("identf", [128, 128], F32)
        r = region(*spare)
        cntT = r.put("cntT", [EXPERTS + 1, N_NODES], F16)
        mask16 = r.put("mask16", [P, T, EXPERTS], F16)
        before = r.put("before", [P, T + 1, EXPERTS], F16)
        oh8 = r.put("oh8", [P, 2, T, EXPERTS], F32)
        tk = r.put("tk", [P, 8, 2 * T], F32)
        r = slots(14)
        sil = r.put("sil", [P, 2, D], F32)
        h32 = r.put("h32", [P, 2, D], F32)
        r = slots(8, 2)
        rt = r.put("rt", [P, 12, T, EXPERTS], F32)
        iop = r.put("iop", [128, 128], F32)
        thr = r.put("thr", [P, JW + 1], F32)
        ge16 = r.put("ge16", [P, 2 * T, JW + 1], F16)
        c16 = r.put("c16", [P, 2 * T], F16)
        padw = r.put("padw", [128, JW], F32)
        he = slots(13).put("he", [P, 2, 2, HID], F16)
        r = slots(13)
        sil_s = r.put("sil_s", [128, 2, 417], F32)
        h32_s = r.put("h32_s", [128, 2, 417], F32)
        acc = slots(13).put("acc", [P, 2, D], F32)
        hsh = slots(8, 3).put("hsh", [128, HB, N_NODES], F16)
        hsl = again(r_g).put("hsl", [128, HB, N_NODES], F16)
        r = again(r_f)
        got = r.put("got", [128, 2, 2 * HID], F16)
        y = r.put("y", [128, 2, D], F32)
        pad0 = r.put("pad0", [128, D], F32)
        heT = again(r_g).put("heT", [128, 2, 2, HB, 128], F16)

        ident = small.put("ident", [128, 128], F16)
        tri = small.put("tri", [128, 128], F16)
        ones = small.put("ones", [128, 128], F16)
        onesf = small.put("onesf", [128, 2], F32)
        b1 = small.put("b1", [128, KB], F32)
        b1s = small.put("b1s", [128, KB], F32)
        lnp = small.put("lnp", [128, 2, KB], F32)
        lns = small.put("lns", [128, 2, KB], F32)
        gw = small.put("gw", [128, KB, GATES], F32)
        gb = small.put("gb", [P, GATES], F32)
        tabs = small.put("tabs", [1, 32], I32)
        tabf = small.put("tabf", [1, 32], F32)
        st6 = small.put("st6", [P, 2, 6], F32)
        mv = small.put("mv", [P, 2, 2], F32)
        ve = small.put("ve", [P, 2, 1], F32)
        sd = small.put("sd", [P, 2, 1], F32)
        rst = small.put("rst", [P, 2, 4], F32)
        den = small.put("den", [P, 2, 2, HEADS], F32)
        node_id = small.put("node_id", [P, T], F32)
        tlo = small.put("tlo", [T, 2], F32)
        pad_row = small.put("pad_row", [128, 1], F32)
        bias9 = small.put("bias9", [EXPERTS + 1, 2, D], F16)
        eidt = small.put("eidt", [1, JW], I32)
        gidx = small.put("gidx", [128, JW], U32)
        sidx = small.put("sidx", [128, JW], U32)
        wsl = small.put("wsl", [128, JW], F32)
        gcur = small.put("gcur", [128, 2], U32)
        scur = small.put("scur", [128, 2], U32)

        ps = ctx.enter_context(nc.psum_tensor("ps", [128, 8, 512], F32))
        ps16 = ps[:, :, :].bitcast(F16)

        def sem(name):
            return ctx.enter_context(nc.semaphore(name))

        edge_in, x_in, small_in, stage_in = sem("edge_in"), sem("x_in"), sem("small_in"), sem("stage_in")
        b2_in, hid_out, acc_out, pad_out = sem("b2_in"), sem("hid_out"), sem("acc_out"), sem("pad_out")
        const_ok, const2_ok = sem("const_ok"), sem("const2_ok")
        w_scaled = sem("w_scaled")
        w_hi, w_lo = sem("w_hi"), sem("w_lo")
        bias_hi, bias_lo, par_ok = sem("bias_hi"), sem("bias_lo"), sem("par_ok")
        dve_c = sem("dve_c")
        edges_f, diag_ok, rows_ps, range_ok, tab_ps, tab_ok = (
            sem("edges_f"), sem("diag_ok"), sem("rows_ps"), sem("range_ok"), sem("tab_ps"), sem("tab_ok"))
        hot_ready, hot_used, ksum_c, ksum_ps = (
            sem("hot_ready"), sem("hot_used"), sem("ksum_c"), sem("ksum_ps"))
        a_copied, a_turned, adj_out = sem("a_copied"), sem("a_turned"), sem("adj_out")
        ln_bn, ln_mv, ln_ve, ln_sd, ln_r, z_ok = (
            sem("ln_bn"), sem("ln_mv"), sem("ln_ve"), sem("ln_sd"), sem("ln_r"), sem("z_ok"))
        var_ok, root_ok, scale_ok, z1_ok = sem("var_ok"), sem("root_ok"), sem("scale_ok"), sem("z1_ok")
        xn_hi, xn_lo = sem("xn_hi"), sem("xn_lo")
        xcol_ps, xcol_out = sem("xcol_ps"), sem("xcol_out")
        k_ps, v_ps, k_act, k_done, v_done, kv_used = (
            sem("k_ps"), sem("v_ps"), sem("k_act"), sem("k_done"), sem("v_done"), sem("kv_used"))
        k_neg, q_neg = sem("k_neg"), sem("q_neg")
        q_ps, q_act, q_done = sem("q_ps"), sem("q_act"), sem("q_done")
        kvd_ok, o_ps, den_c, o_done, att_added = (
            sem("kvd_ok"), sem("o_ps"), sem("den_c"), sem("o_done"), sem("att_added"))
        n_ps, n_hi, n_lo = sem("n_ps"), sem("n_hi"), sem("n_lo")
        f1_ps, g_act, g_lo = sem("f1_ps"), sem("g_act"), sem("g_lo")
        w2_ps, x1_done, zt_ps, ft_act, f_hi, f_lo, gate_ps, lg_done = (
            sem("w2_ps"), sem("x1_done"), sem("zt_ps"), sem("ft_act"), sem("f_hi"), sem("f_lo"),
            sem("gate_ps"), sem("lg_done"))
        ei_ps, ei_sil, ei_mul, ei_hi, ei_lo = (
            sem("ei_ps"), sem("ei_sil"), sem("ei_mul"), sem("ei_hi"), sem("ei_lo"))
        rank_in, rank_ps, hots_ok, slot_ps, slots_ok, cnt_ps, cnt_ok, eid_ok = (
            sem("rank_in"), sem("rank_ps"), sem("hots_ok"), sem("slot_ps"), sem("slots_ok"),
            sem("cnt_ps"), sem("cnt_ok"), sem("eid_ok"))
        si_ps, si_sil, si_mul, si_hi, si_lo = (
            sem("si_ps"), sem("si_sil"), sem("si_mul"), sem("si_hi"), sem("si_lo"))
        so_ps, so_done = sem("so_ps"), sem("so_done")
        pad_ok, idx_ok, got_ok, tr_ps, ht_hi, ht_lo, ex_ps, y_ok = (
            sem("pad_ok"), sem("idx_ok"), [sem("got_ok0"), sem("got_ok1")], sem("tr_ps"),
            sem("ht_hi"), sem("ht_lo"), sem("ex_ps"), sem("y_ok"))
        passed = sem("passed")
        sel_ok, sel_exp, identf_ok = sem("sel_ok"), sem("sel_exp"), sem("identf_ok")
        idx2_ok, added = sem("idx2_ok"), sem("added")

        n_small = 7 * 16
        block = ctx.enter_context(nc.Block())

        def tiles(eng, step, peeled=1):
            for i in range(peeled):
                step(i)
            with eng.Fori(peeled, T // 2) as i:
                step(i)

        first_units = [(U_WK, SLOT_WK), (U_WV, SLOT_WV), (U_WQ, SLOT_WQ), (U_W1, SLOT_W1), (U_W2, SLOT_W2)]

        def later(i, b, n=1):
            return not isinstance(i, int) or 2 * i + b >= n

        @block.sync
        def _(sp):
            sp.dma_start(dst2[:, :, :], d["dst_rows"]).then_inc(edge_in, 16)
            sp.dma_start(dsti[:, :], d["dst_cols"]).then_inc(edge_in, 16)
            sp.dma_start(srci[:, :], d["src_cols"]).then_inc(edge_in, 16)
            xv = d["x"].rearrange("(t p) c -> p t c", p=P)
            sp.dma_start(x_sb[0:112, :, :], xv[0:112]).then_inc(x_in, 16)
            sp.dma_start(x_sb[112:P, :, :], xv[112:P]).then_inc(x_in, 16)
            sp.dma_start(stage[:, 0, :], d["weights"][0]).then_inc(stage_in, 16)
            sp.dma_start(b1[:, :], d["b1"]).then_inc(small_in, 16)
            sp.dma_start(lnp[:, 0, :], d["ln_scale"]).then_inc(small_in, 16)
            sp.dma_start(lnp[:, 1, :], d["ln_bias"]).then_inc(small_in, 16)
            sp.dma_start(gw[:, :, :], d["gate_w"]).then_inc(small_in, 16)
            sp.dma_start(gb[:, :], d["gate_b"].broadcast_to((P, GATES))).then_inc(small_in, 16)
            sp.dma_start(bias_in[0:EXPERTS, :], d["expert_b"]).then_inc(small_in, 16)
            sp.dma_start(bias_in[EXPERTS:EXPERTS + 1, :], d["shared_b"]).then_inc(small_in, 16)
            sp.wait_ge(stage_in, 16)
            sp.dma_start(stage[:, 1, :], d["weights"][1]).then_inc(stage_in, 16)
            with sp.Fori(2, N_UNITS) as u:
                sp.wait_ge(stage_in, 16 * u)
                sp.sem_inc(passed, 1)
                sp.wait_ge(w_lo, u - 1)
                sp.sem_inc(passed, 1)
                sp.dma_start(stage[:, u % 2, :], d["weights"][u]).then_inc(stage_in, 16)

        @block.gpsimd
        def _(pool):
            pool.memset(ident[:, :], 0.0).then_inc(const_ok, 1)
            pool.memset(ones[:, :], 1.0).then_inc(const_ok, 1)
            pool.wait_ge(const_ok, 2)
            pool.affine_select(out=ident[:, :], in_=ident[:, :], compare_op=ALU.not_equal, fill=1.0,
                               base=0, pattern=[[-1, 128]], channel_multiplier=1).then_inc(const_ok, 1)
            pool.affine_select(out=tri[:, :], in_=ones[:, :], compare_op=ALU.is_gt, fill=0.0,
                               base=0, pattern=[[1, 128]], channel_multiplier=-1).then_inc(const_ok, 1)
            exact = {"allow_small_or_imprecise_dtypes": True}
            pool.iota(cup[:, 0, :], [[1, CHUNKS]], base=1, channel_multiplier=0, **exact).then_inc(const_ok, 1)
            pool.iota(cup[:, 1, :], [[-1, CHUNKS]], base=CHUNKS, channel_multiplier=0, **exact).then_inc(const_ok, 1)
            pool.iota(even[:, :], [[2, HALF]], base=0, channel_multiplier=0, **exact).then_inc(const_ok, 1)
            pool.iota(tlo[:, :], [[P, 2]], base=0, channel_multiplier=P, **exact).then_inc(const_ok, 1)
            pool.iota(iota[:, :], [[1, WIDE + 1]], base=0, channel_multiplier=0, **exact).then_inc(const_ok, 1)
            pool.iota(node_id[:, :], [[P, T]], base=0, channel_multiplier=1, **exact).then_inc(const_ok, 1)
            pool.memset(onesf[:, :], 1.0).then_inc(const_ok, 1)
            pool.iota(pad_row[:, :], [[1, 1]], base=N_NODES, channel_multiplier=1, **exact).then_inc(const_ok, 1)
            pool.memset(srcf[:, CHUNKS:], -1.0).then_inc(const_ok, 1)
            pool.memset(dstf[:, CHUNKS:], -1.0).then_inc(const_ok, 1)
            pool.memset(ksum[:, :], 0.0).then_inc(const_ok, 1)
            pool.memset(band[:, :], 0.0).then_inc(const_ok, 1)
            pool.wait_ge(const_ok, 16)
            pool.affine_select(out=band[:, :], in_=band[:, :], compare_op=ALU.not_equal, fill=1.0,
                               base=N_NODES - P, pattern=[[-1, N_NODES - P + WIDE + 1]],
                               channel_multiplier=1).then_inc(const_ok, 1)

            def low_part(u, slot):
                pool.wait_ge(w_hi, u + 1)
                pool.tensor_tensor(wslots[:, slot, 1, :], stage[:, u % 2, :], wslots[:, slot, 0, :],
                                   ALU.subtract).then_inc(w_lo, 1)

            def node_low(t, b):
                pool.wait_ge(xn_hi, t + 1)
                pool.sem_inc(passed, 1)
                pool.tensor_tensor(xn[:, 1, t, :], z1[:, b, :], xn[:, 0, t, :], ALU.subtract).then_inc(xn_lo, 1)

            def nodes(i, last=False):
                for b in range(2):
                    t = 2 * i + b
                    if not (last and b == 1):
                        node_low(t + 1, 1 - b)
                    pool.wait_ge(k_act, t + 1)
                    pool.sem_inc(passed, 1)
                    pool.tensor_tensor(kbuf[:, b, :], ekey[:, b, :], kbuf[:, b, :], ALU.add).then_inc(k_done, 1)
                    pool.wait_ge(k_done, t + 1)
                    pool.sem_inc(passed, 1)
                    pool.tensor_tensor(ksum[:, :], ksum[:, :], kbuf[:, b, :], ALU.add).then_inc(ksum_c, 1)
                    if isinstance(i, int) and i < 2 and t >= 1:
                        low_part(*first_units[t + 1])
            low_part(*first_units[0])
            node_low(0, 0)
            low_part(*first_units[1])
            nodes(0)
            nodes(1)
            with pool.Fori(2, T // 2 - 1) as i:
                nodes(i)
            nodes(T // 2 - 1, last=True)

            pool.wait_ge(b2_in, 16)

            def add_att(i):
                for b in range(2):
                    t = 2 * i + b
                    pool.tensor_tensor(x_sb[:, t, :], x_sb[:, t, :], b2b[:, :], ALU.add).then_inc(att_added, 1)
                    pool.wait_ge(att_added, 2 * t + 1)
                    pool.wait_ge(o_done, t + 1)
                    pool.sem_inc(passed, 1)
                    pool.tensor_tensor(x_sb[:, t, :], x_sb[:, t, :], att[:, b, :], ALU.add)\
                        .then_inc(att_added, 1)
            tiles(pool, add_att)

            def ein_low(i):
                for b in range(2):
                    for j in range(2):
                        n = 2 * (2 * i + b) + j
                        pool.wait_ge(ei_hi, n + 1)
                        pool.tensor_tensor(he[:, b, 1, j * 512:(j + 1) * 512], h32[:, j, :],
                                           he[:, b, 0, j * 512:(j + 1) * 512], ALU.subtract).then_inc(ei_lo, 1)
            tiles(pool, ein_low)
            pool.wait_ge(w2_ps, T)
            pool.iota(iop[:, :], [[1, 128]], base=0, channel_multiplier=0, **exact).then_inc(const2_ok, 1)

            def sin_low(u):
                for m2 in range(2):
                    for c, (at, w) in enumerate(COLS):
                        n = 3 * m2 + c
                        pool.wait_ge(si_hi, 6 * u + n + 1)
                        pool.tensor_tensor(hsl[:, 2 * u + m2, at:at + w], h32_s[:, n % 2, 0:w],
                                           hsh[:, 2 * u + m2, at:at + w], ALU.subtract).then_inc(si_lo, 1)
            pool.wait_ge(slots_ok, 1)
            with pool.Fori(0, 4) as u:
                sin_low(u)

            pool.wait_ge(si_ps, 24)
            pool.memset(pad0[:, :], 0.0).then_inc(pad_ok, 1)
            pool.wait_ge(hid_out, 16 * T)
            pool.wait_ge(slots_ok, 1)

            def fetch(i, b):
                j = 2 * i + b
                pool.tensor_copy(gcur[:, b:b + 1], gidx[:, bass.ds(j, 1)]).then_inc(idx_ok, 1)
                pool.wait_ge(idx_ok, j + 1)
                pool.sem_inc(passed, 1)
                pool.indirect_dma_start(
                    out=got[:, b, :], out_offset=None, in_=hid_dram[:, :],
                    in_offset=bass.IndirectOffsetOnAxis(ap=gcur[:, b:b + 1], axis=0)).then_inc(got_ok[b], 16)

            def put(i, b):
                j = 2 * i + b
                pool.tensor_copy(scur[:, b:b + 1], sidx[:, bass.ds(j, 1)]).then_inc(idx2_ok, 1)
                pool.wait_ge(idx2_ok, j + 1)
                pool.wait_ge(y_ok, j + 1)
                if later(i, b):
                    pool.wait_ge(added, 16 * j)
                pool.sem_inc(passed, 1)
                pool.indirect_dma_start(
                    out=out[:, :], out_offset=bass.IndirectOffsetOnAxis(ap=scur[:, b:b + 1], axis=0),
                    in_=y[:, b, :], in_offset=None, compute_op=ALU.add).then_inc(added, 16)

            fetch(0, 0)
            fetch(0, 1)
            pool.wait_ge(acc_out, 16 * T)
            pool.wait_ge(pad_out, 16)

            def step(i):
                for b in range(2):
                    pool.wait_ge(tr_ps, 2 * i + b + 1)
                    if not (isinstance(i, int) and 2 * i + b + 2 >= MAX_TILES):
                        fetch(i + 1, b)
                    put(i, b)
            n_pairs = MAX_TILES // 2
            step(0)
            with pool.Fori(1, n_pairs - 1) as i:
                step(i)
            step(n_pairs - 1)
            put(n_pairs, 0)
            pool.wait_ge(added, 16 * MAX_TILES)

        @block.scalar
        def _(act):
            def split_hi(u, slot, half=None):
                half = u % 2 if half is None else half
                act.wait_ge(stage_in, 16 * (u + 1))
                act.activation(wslots[:, slot, 0, :], stage[:, half, :], ACT.Copy, scale=S_W).then_inc(w_hi, 1)

            def scale_and_split_hi(u, slot):
                act.wait_ge(stage_in, 16 * (u + 1))
                act.activation(stage[:, u % 2, :], stage[:, u % 2, :], ACT.Copy, scale=S_W).then_inc(w_scaled, 1)
                act.wait_ge(w_scaled, u + 1)
                act.activation(wslots[:, slot, 0, :], stage[:, u % 2, :], ACT.Copy).then_inc(w_hi, 1)

            act.wait_ge(edge_in, 48)
            act.activation(dstf[:, 0:CHUNKS], dsti[:, :], ACT.Copy).then_inc(edges_f, 1)
            act.activation(srcf[:, 0:CHUNKS], srci[:, :], ACT.Copy).then_inc(edges_f, 1)
            act.wait_ge(small_in, n_small)
            act.activation(bias9[:, 0, :], bias_in[:, :], ACT.Copy, scale=S_W).then_inc(bias_hi, 1)
            act.activation(b1s[:, :], b1[:, :], ACT.Copy, scale=S_G).then_inc(par_ok, 1)
            act.activation(lns[:, :, :], lnp[:, :, :], ACT.Copy, scale=S_F).then_inc(par_ok, 1)

            act.wait_ge(var_ok, 1)
            act.activation(r1[:, 1, :], r1[:, 0, :], ACT.Sqrt).then_inc(root_ok, 1)
            act.wait_ge(scale_ok, 1)

            def normal(t, b, reused):
                if reused:
                    act.wait_ge(xn_lo, t - 1)
                act.activation(z1[:, b, :], x_sb[:, t, :], ACT.Identity, scale=r1[:, 6, bass.ds(t, 1)],
                               bias=r1[:, 7, bass.ds(t, 1)]).then_inc(z1_ok, 1)
                act.wait_ge(z1_ok, t + 1)
                act.activation(xn[:, 0, t, :], z1[:, b, :], ACT.Copy).then_inc(xn_hi, 1)

            def nodes(i, last=False):
                for b in range(2):
                    t = 2 * i + b
                    if not (last and b == 1):
                        normal(t + 1, 1 - b, later(i, b))
                    end = act.value_load(tabs[0:1, bass.ds(t + 1, 1)], min_val=1, max_val=T * (HALF + 1))
                    act.wait_ge(hot_used, end + RING)
                    if later(i, b):
                        act.wait_ge(a_turned, t)
                    act.activation(a_row[:, 0:WIDE].rearrange("p (c w) -> p c w", c=3),
                                   ps[0:P, 0:3, 0:417], ACT.Copy).then_inc(a_copied, 1)
                    act.wait_ge(xcol_ps, t + 1)
                    act.activation(xnT[:, :, :, bass.ds(t * P, P)],
                                   ps[:, 6:8, 0:4 * P].rearrange("p a (k n) -> p a k n", k=KB),
                                   ACT.Copy).then_inc(xcol_out, 1)
                    act.wait_ge(k_ps, t + 1)
                    if later(i, b, 2):
                        act.wait_ge(ksum_c, t - 1)
                        act.wait_ge(kv_used, t - 1)
                    act.activation(ekey[:, b, :], ps[0:P, 3, :], ACT.Relu,
                                   scale=-1 / (S_X * S_W)).then_inc(k_neg, 1)
                    act.activation(kbuf[:, b, :], ps[0:P, 3, :], ACT.Relu, scale=1 / (S_X * S_W))
                    act.wait_ge(k_neg, t + 1)
                    act.activation(ekey[:, b, :], ekey[:, b, :], ACT.Exp, scale=-1.0).then_inc(k_act, 1)
                    act.wait_ge(v_ps, t + 1)
                    act.activation(vbuf[:, b, :], ps[0:P, 4, :], ACT.Copy,
                                   scale=1 / (S_X * S_W * N_NODES)).then_inc(v_done, 1)
                    act.wait_ge(a_turned, t + 1)
                    v = ps16[0:P, 6:8, 0:640].rearrange("p a (s c) -> p a s c", c=128)[:, :, :, 0:P]
                    o = adjT[:, :, bass.ds(t * P, P)].rearrange("p (a s) c -> p a s c", a=2)
                    act.activation(o, v, ACT.Copy).then_inc(adj_out, 1)
                    if isinstance(i, int) and i < 2 and t >= 1:
                        scale_and_split_hi(*first_units[t + 1])
            scale_and_split_hi(*first_units[0])
            normal(0, 0, False)
            scale_and_split_hi(*first_units[1])
            nodes(0)
            nodes(1)
            with act.Fori(2, T // 2 - 1) as i:
                nodes(i)
            nodes(T // 2 - 1, last=True)


            def queries(i):
                for m2 in range(2):
                    for c, (at, w) in enumerate(COLS):
                        n = 3 * m2 + c
                        bank = [0, 1, 2, 3, 6, 7][n]
                        act.wait_ge(q_ps, 6 * i + n + 1)
                        if not isinstance(i, int) or i or n >= 2:
                            act.wait_ge(q_done, 6 * i + n - 1)
                        act.activation(ebuf[:, n % 2, 0:w], ps[:, bank, 0:w], ACT.Relu,
                                       scale=-1 / (S_X * S_W)).then_inc(q_neg, 1)
                        act.activation(qT[:, 2 * i + m2, at:at + w], ps[:, bank, 0:w], ACT.Relu,
                                       scale=1 / (S_X * S_W))
                        act.wait_ge(q_neg, 6 * i + n + 1)
                        act.activation(ebuf[:, n % 2, 0:w], ebuf[:, n % 2, 0:w], ACT.Exp,
                                       scale=-1.0).then_inc(q_act, 1)
            queries(0)
            queries(1)
            act.wait_ge(kv_used, T)
            act.wait_ge(ksum_c, T)
            act.dma_start(b2b[:, :], d["b2"].broadcast_to((P, D))).then_inc(b2_in, 16)

            act.wait_ge(ksum_ps, 1)
            act.wait_ge(bias_lo, 1)

            for m in range(KB):
                act.wait_ge(n_ps, m + 1)
                for c, (at, w) in enumerate(COLS):
                    bank = [4, 5, 6, 7, 0, 1][3 * (m % 2) + c]
                    act.activation(h1T[:, 0, m, at:at + w], ps[:, bank, 0:w], ACT.Copy,
                                   scale=S_G / S_X).then_inc(n_hi, 1)
                split_hi(U_EIN + m, SLOT_EIN + m)
            act.wait_ge(att_added, 2 * T)
            act.wait_ge(o_ps, T)

            act.wait_ge(par_ok, 2)
            for m in range(KB):
                for c, (at, w) in enumerate(COLS):
                    n = 3 * m + c
                    act.wait_ge(f1_ps, n + 1)
                    if n >= 2:
                        act.wait_ge(g_lo, n - 1)
                    act.activation(rbuf[:, n % 2, 0:w], ps[:, 2 + n % 6, 0:w], ACT.Relu,
                                   scale=1 / S_W, bias=b1s[:, m:m + 1])
                    act.activation(r1T[:, 0, m, at:at + w], ps[:, 2 + n % 6, 0:w], ACT.Relu,
                                   scale=1 / S_W, bias=b1s[:, m:m + 1]).then_inc(g_act, 1)
                split_hi(U_SIN + m, SLOT_SIN + m)

            def columns2(t, b, reused):
                act.wait_ge(zt_ps, t + 1)
                if reused:
                    act.wait_ge(gate_ps, t - 1)
                    act.wait_ge(f_lo, t - 1)
                for k in range(KB):
                    ins = act.activation(ft[:, b, k, :], ps[:, 6, k * P:(k + 1) * P], ACT.Identity,
                                         scale=lns[:, 0, k:k + 1], bias=lns[:, 1, k:k + 1])
                ins.then_inc(ft_act, 1)
                act.wait_ge(ft_act, t + 1)
                act.activation(fT[:, 0, :, bass.ds(t * P, P)], ft[:, b, :, :], ACT.Copy).then_inc(f_hi, 1)

            def store_hidden(t, b):
                act.wait_ge(ei_lo, 2 * t + 2)
                act.dma_start(hid_dram[bass.ds(t * P, P), :].rearrange("p (h c) -> p h c", h=2),
                              he[:, b, :, :]).then_inc(hid_out, 16)

            def ein_silu(t, b, j, reused):
                act.wait_ge(ei_ps, 2 * t + j + 1)
                if reused:
                    act.wait_ge(ei_mul, 2 * t + j - 1)
                act.activation(sil[:, j, :], ps[0:P, 2 * j, :], ACT.Silu,
                               scale=1 / (S_F * S_W)).then_inc(ei_sil, 1)

            def ein_high(t, b, j):
                act.wait_ge(ei_mul, 2 * t + j + 1)
                act.activation(he[:, b, 0, j * 512:(j + 1) * 512], h32[:, j, :], ACT.Copy).then_inc(ei_hi, 1)

            def norm2(i):
                for b in range(2):
                    t = 2 * i + b
                    act.wait_ge(ln_ve, t + 1)
                    act.activation(sd[:, b, :], ve[:, b, :], ACT.Sqrt).then_inc(ln_sd, 1)
                    if later(i, b):
                        ein_silu(t - 1, 1 - b, 0, later(i, b, 2))
                        if later(i, b, 3):
                            act.wait_ge(hid_out, 16 * (t - 2))
                        if later(i, b, 2):
                            store_hidden(t - 2, b)
                        ein_high(t - 1, 1 - b, 0)
                        ein_silu(t - 1, 1 - b, 1, later(i, b, 2))
                    columns2(t, b, later(i, b, 2))
                    if later(i, b):
                        ein_high(t - 1, 1 - b, 1)
                    if isinstance(i, int) and i == 0:
                        split_hi(U_SOUT + b, SLOT_SOUT + b)
            tiles(act, norm2, peeled=2)
            ein_silu(T - 1, 1, 0, True)
            act.wait_ge(hid_out, 16 * (T - 2))
            store_hidden(T - 2, 0)
            ein_high(T - 1, 1, 0)
            ein_silu(T - 1, 1, 1, True)
            ein_high(T - 1, 1, 1)
            for u in range(2):
                split_hi(U_EXP + u, u)
            store_hidden(T - 1, 1)

            act.wait_ge(sel_ok, 1)
            act.activation(rt[:, 2, :, 0:PER_GROUP], rt[:, 1, :, 0:PER_GROUP], ACT.Exp).then_inc(sel_exp, 1)
            act.wait_ge(hid_out, 16 * T)
            act.wait_ge(slots_ok, 1)
            act.wait_ge(eid_ok, 1)

            def sin(u, first):
                split_hi(U_EXP + 2 + u, 2 + u)
                for m2 in range(2):
                    for c, (at, w) in enumerate(COLS):
                        n = 3 * m2 + c
                        act.wait_ge(si_ps, 6 * u + n + 1)
                        if not first or n >= 2:
                            act.wait_ge(si_mul, 6 * u + n - 1)
                        act.activation(sil_s[:, n % 2, 0:w], ps[:, 2 * c, 0:w], ACT.Silu,
                                       scale=1 / (S_F * S_W)).then_inc(si_sil, 1)
                        act.wait_ge(si_mul, 6 * u + n + 1)
                        act.activation(hsh[:, 2 * u + m2, at:at + w], h32_s[:, n % 2, 0:w], ACT.Copy)\
                            .then_inc(si_hi, 1)
            sin(0, True)
            with act.Fori(1, 4) as u:
                sin(u, False)

            act.wait_ge(cnt_ps, 1)
            for g, n in ((0, 4), (1, 4), (2, 2)):
                act.activation(cntT[0:EXPERTS, g * 500:g * 500 + n * P], ps[0:EXPERTS, [6, 7, 0][g], 0:n * P],
                               ACT.Copy, scale=S_H).then_inc(cnt_ok, 1)

            act.wait_ge(pad_ok, 1)
            act.dma_start(out[N_NODES:N_NODES + 128, :], pad0[:, :]).then_inc(pad_out, 16)

            for u in range(6, 2 * EXPERTS - LATE):
                split_hi(U_EXP + u, u)

            def sout(i):
                for b in range(2):
                    t = 2 * i + b
                    act.wait_ge(so_done, t + 1)
                    act.dma_start(out[bass.ds(t * P, P), :], acc[:, b, :]).then_inc(acc_out, 16)
            with act.Fori(0, T // 2) as i:
                sout(i)

            act.wait_ge(acc_out, 16 * T)

            def turned_hi(i, b):
                j = 2 * i + b
                act.wait_ge(tr_ps, j + 1)
                if later(i, b, 2):
                    act.wait_ge(ex_ps, j - 1)
                act.activation(heT[:, b, 0, :, :], ps16[:, 4 + 2 * b, :].rearrange("p (h n) -> p h n", h=HB),
                               ACT.Copy).then_inc(ht_hi, 1)

            def weighted(i, b):
                j = 2 * i + b
                act.wait_ge(ex_ps, j + 1)
                if later(i, b, 2):
                    act.wait_ge(added, 16 * (j - 1))
                act.activation(y[:, b, :], ps[:, b, :], ACT.Copy, scale=wsl[:, bass.ds(j, 1)]).then_inc(y_ok, 1)

            def routed(i, units):
                for b in range(2):
                    turned_hi(i, 1) if b == 0 else turned_hi(i + 1, 0)
                    if units:
                        split_hi(2 * i + (U_LATE + b), 2 * i + (SLOT_LATE + b), (U_LATE + b) % 2)
                    weighted(i, b)
            turned_hi(0, 0)
            routed(0, True)
            with act.Fori(1, LATE // 2) as i:
                routed(i, True)
            with act.Fori(LATE // 2, MAX_TILES // 2) as i:
                routed(i, False)
            weighted(MAX_TILES // 2, 0)

        @block.vector
        def _(dve):
            steps = [0]

            def link(ins):
                steps[0] += 1
                ins.then_inc(dve_c, 1)
                dve.wait_ge(dve_c, steps[0])

            def split_lo(u, slot, half=None):
                half = u % 2 if half is None else half
                dve.wait_ge(w_hi, u + 1)
                dve.scalar_tensor_tensor(out=wslots[:, slot, 1, :], in0=stage[:, half, :], scalar=S_W,
                                         in1=wslots[:, slot, 0, :], op0=ALU.mult, op1=ALU.subtract)\
                   .then_inc(w_lo, 1)

            def stats(n, b, src, scale, add):
                dve.sem_inc(passed, 1)
                dve.bn_stats(st6[:, b, :], src).then_inc(ln_bn, 1)
                dve.wait_ge(ln_bn, n + 1)
                dve.sem_inc(passed, 1)
                dve.bn_aggr(mv[:, b, :], st6[:, b, :]).then_inc(ln_mv, 1)
                dve.wait_ge(ln_mv, n + 1)
                dve.tensor_scalar(ve[:, b, :], mv[:, b, 1:2], scale, add, ALU.mult, ALU.add).then_inc(ln_ve, 1)

            def normalise(n, b, src, dst, scale):
                dve.wait_ge(ln_sd, n + 1)
                dve.reciprocal(rst[:, b, 0:1], sd[:, b, :]).then_inc(ln_r, 1)
                dve.wait_ge(ln_r, 4 * n + 1)
                dve.tensor_scalar(rst[:, b, 1:2], ve[:, b, :], rst[:, b, 0:1], rst[:, b, 0:1],
                                  ALU.mult, ALU.mult).then_inc(ln_r, 1)
                dve.wait_ge(ln_r, 4 * n + 2)
                dve.tensor_scalar(rst[:, b, 2:3], rst[:, b, 1:2], -0.5, 1.5, ALU.mult, ALU.add).then_inc(ln_r, 1)
                dve.wait_ge(ln_r, 4 * n + 3)
                dve.tensor_scalar(rst[:, b, 3:4], rst[:, b, 2:3], rst[:, b, 0:1], scale,
                                  ALU.mult, ALU.mult).then_inc(ln_r, 1)
                dve.wait_ge(ln_r, 4 * n + 4)
                dve.tensor_scalar(dst, src, mv[:, b, 0:1], rst[:, b, 3:4],
                                  ALU.subtract, ALU.mult).then_inc(z_ok, 1)

            dve.wait_ge(edge_in, 48)
            dve.tensor_reduce(mnmx[:, 0:2], dst2[:, :, :], AX.X, ALU.max)
            link(dve.tensor_reduce(mnmx[:, 2:4], dst2[:, :, :], AX.X, ALU.min))
            dve.wait_ge(const_ok, 14)
            for q in range(4):
                ins = dve.tensor_scalar(diag[:, q, :], ident[0:HALF, 0:HALF], mnmx[:, q:q + 1], None, ALU.mult)
            ins.then_inc(diag_ok, 1)
            dve.wait_ge(rows_ps, 1)
            link(dve.tensor_scalar(rngf[:, 0, :], ps[0:T, 6, 0:CHUNKS], tlo[:, 0:1], None, ALU.is_ge))
            link(dve.scalar_tensor_tensor(out=rngf[:, 1, :], in0=ps[0:T, 6, CHUNKS:2 * CHUNKS], scalar=tlo[:, 1:2],
                                          in1=rngf[:, 0, :], op0=ALU.is_lt, op1=ALU.mult))
            link(dve.tensor_tensor(rngf[:, 2:4, :], rngf[:, 1:2, :].broadcast_to((T, 2, CHUNKS)), cup[:, :, :],
                                   ALU.mult))
            link(dve.tensor_reduce(rsm[:, 0:2], rngf[:, 2:4, :], AX.X, ALU.max))
            link(dve.tensor_scalar(rsm[:, 2:3], rsm[:, 0:1], 1.0, None, ALU.max))
            link(dve.tensor_scalar(rsm[:, 3:4], rsm[:, 2:3], -1.0, None, ALU.add))
            link(dve.tensor_scalar(rsm[:, 4:5], rsm[:, 1:2], -1.0, float(CHUNKS), ALU.mult, ALU.add))
            link(dve.tensor_tensor(rsm[:, 5:6], rsm[:, 4:5], rsm[:, 3:4], ALU.min))
            link(dve.tensor_tensor(rsm[:, 6:7], rsm[:, 2:3], rsm[:, 5:6], ALU.subtract))
            link(dve.tensor_scalar(rngf[:, 0, 0:HALF], even[:, :], rsm[:, 6:7], None, ALU.is_lt, ALU.add,
                                   accum_out=rsm[:, 7:8]))
            dve.tensor_copy(rs16[:, 0:1], rsm[:, 5:6])
            dve.tensor_copy(rs16[:, 1:2], rsm[:, 7:8]).then_inc(range_ok, 1)
            dve.wait_ge(tab_ps, 1)
            link(dve.tensor_copy(tabf[0:1, 0:T + 1], ps[0:1, 7, 0:T + 1]))
            link(dve.scalar_tensor_tensor(out=tabf[0:1, 16:16 + T], in0=tabf[0:1, 0:T], scalar=-2.0,
                                          in1=ps[0:1, 7, 16:16 + T], op0=ALU.mult, op1=ALU.add))
            dve.tensor_scalar(tabs[0:1, 16:16 + T], tabf[0:1, 16:16 + T], float(CO_SHIFT), None, ALU.add)
            link(dve.tensor_copy(tabs[0:1, 0:T + 1], tabf[0:1, 0:T + 1]))
            dve.nop().then_inc(tab_ok, 1)

            dve.wait_ge(x_in, 32)
            for t in range(T):
                ins = dve.bn_stats(st1[:, t, :], x_sb[:, t, :])
            link(ins)
            for t in range(T):
                ins = dve.bn_aggr(mv1[:, t, :], st1[:, t, :])
            link(ins)
            var, root, inv1, tmp = r1[:, 0, :], r1[:, 1, :], r1[:, 2, :], r1[:, 3, :]
            fix, inv2, rs, shift = r1[:, 4, :], r1[:, 5, :], r1[:, 6, :], r1[:, 7, :]
            by_tile = "p (t o) -> p t o"
            dve.tensor_scalar(var.rearrange(by_tile, o=1), mv1[:, :, 1:2], LN_EPS, None, ALU.add).then_inc(var_ok, 1)
            dve.wait_ge(root_ok, 1)
            link(dve.reciprocal(inv1, root))
            link(dve.tensor_tensor(tmp, inv1, inv1, ALU.mult))
            link(dve.tensor_tensor(fix, tmp, var, ALU.mult))
            link(dve.tensor_scalar(inv2, fix, -0.5 * S_X, 1.5 * S_X, ALU.mult, ALU.add))
            link(dve.tensor_tensor(rs, inv2, inv1, ALU.mult))
            dve.scalar_tensor_tensor(out=shift.rearrange(by_tile, o=1), in0=mv1[:, :, 0:1], scalar=-1.0,
                                     in1=rs.rearrange(by_tile, o=1), op0=ALU.mult, op1=ALU.mult).then_inc(scale_ok, 1)

            dve.wait_ge(edges_f, 2)

            def count_edges(i):
                for b in range(2):
                    t = 2 * i + b
                    first = dve.value_load(tabs[0:1, bass.ds(t, 1)], min_val=0, max_val=T * (HALF + 1))
                    end = dve.value_load(tabs[0:1, bass.ds(t + 1, 1)], min_val=1, max_val=T * (HALF + 1))
                    off = dve.value_load(tabs[0:1, bass.ds(16 + t, 1)], min_val=0, max_val=2 * CO_SHIFT)
                    with dve.Fori(first, end) as v:
                        dve.wait_ge(hot_used, v + 1)
                        pair = nc.s_assert_within(v * 2 + off - CO_SHIFT, 0, CHUNKS,
                                                  skip_runtime_bounds_check_because=IN_RANGE)
                        for q in range(2):
                            chunk = pair + q
                            place = (v % RING) * 2 + q
                            dve.tensor_scalar(hot_src[:, place, 0:WIDE], iota[:, 0:WIDE],
                                              srcf[:, bass.ds(chunk, 1)], None, ALU.is_equal)
                            ins = dve.tensor_scalar(hot_dst[:, place, 0:P], iota[:, bass.ds(t * P, P)],
                                                    dstf[:, bass.ds(chunk, 1)], None, ALU.is_equal)
                        ins.then_inc(hot_ready, 1)
            tiles(dve, count_edges)
            dve.wait_ge(bias_hi, 1)
            dve.scalar_tensor_tensor(out=bias9[:, 1, :], in0=bias_in[:, :], scalar=S_W, in1=bias9[:, 0, :],
                                     op0=ALU.mult, op1=ALU.subtract).then_inc(bias_lo, 1)

            def queries(i):
                for m2 in range(2):
                    for c, (at, w) in enumerate(COLS):
                        n = 3 * m2 + c
                        dve.wait_ge(q_act, 6 * i + n + 1)
                        o = qT[:, 2 * i + m2, at:at + w]
                        dve.tensor_tensor(o, ebuf[:, n % 2, 0:w], o, ALU.add).then_inc(q_done, 1)
            queries(0)
            queries(1)

            dve.wait_ge(ksum_ps, 1)
            dve.wait_ge(ksum_c, T)
            link(dve.memset(kvd[:, :, :], 0.0))
            for h, lo in ((0, 0), (1, 64)):
                rows = slice(lo, lo + 64)
                dve.tensor_scalar(kvd[rows, :, lo:lo + 64],
                                  ps[rows, 5, :].rearrange("p (a c) -> p a c", a=KB)[:, :, lo:lo + 64],
                                  float(N_NODES), None, ALU.mult)
                ins = dve.tensor_copy(kvd[rows, :, 128 + h:129 + h],
                                      ps[rows, 4, 0:8].rearrange("p (a c) -> p a c", a=KB)[:, :, 0:1])
            ins.then_inc(kvd_ok, 1)
            dve.wait_ge(q_done, 12)

            def attend(i):
                for b in range(2):
                    t = 2 * i + b
                    dve.wait_ge(o_ps, t + 1)
                    banks = ps[0:P, 2 * b:2 * b + 2, 0:260].rearrange("p a (q c) -> p a q c", q=2)
                    dve.tensor_scalar(den[:, b, 0, :].rearrange("p (a q h) -> p a q h", a=2, q=2),
                                      banks[:, :, :, 128:130], ATT_EPS, None, ALU.add).then_inc(den_c, 1)
                    dve.wait_ge(den_c, 2 * t + 1)
                    dve.reciprocal(den[:, b, 1, :], den[:, b, 0, :]).then_inc(den_c, 1)
                    dve.wait_ge(den_c, 2 * t + 2)
                    if later(i, b, 2):
                        dve.wait_ge(att_added, 2 * t - 2)
                    for g in range(2):
                        o = att[:, b, 256 * g:256 * g + 256].rearrange("p (q h c) -> p q h c", q=2, h=2)
                        s = ps[0:P, 2 * b + g, 0:260].rearrange("p (q c) -> p q c", q=2)[:, :, 0:128]\
                            .rearrange("p q (h c) -> p q h c", h=2)
                        z = den[:, b, 1, 4 * g:4 * g + 4].rearrange("p (q h c) -> p q h c", q=2, c=1)\
                            .broadcast_to((P, 2, 2, 64))
                        ins = dve.tensor_tensor(o, s, z, ALU.mult)
                    ins.then_inc(o_done, 1)
            tiles(dve, attend)

            for m in range(KB):
                for c, (at, w) in enumerate(COLS):
                    bank = [4, 5, 6, 7, 0, 1][3 * (m % 2) + c]
                    dve.wait_ge(n_hi, 3 * m + c + 1)
                    dve.scalar_tensor_tensor(out=h1T[:, 1, m, at:at + w], in0=ps[:, bank, 0:w], scalar=S_G / S_X,
                                             in1=h1T[:, 0, m, at:at + w], op0=ALU.mult, op1=ALU.subtract)\
                       .then_inc(n_lo, 1)
                split_lo(U_EIN + m, SLOT_EIN + m)

            for m in range(KB):
                for c, (at, w) in enumerate(COLS):
                    n = 3 * m + c
                    dve.wait_ge(g_act, n + 1)
                    dve.tensor_tensor(r1T[:, 1, m, at:at + w], rbuf[:, n % 2, 0:w], r1T[:, 0, m, at:at + w],
                                      ALU.subtract).then_inc(g_lo, 1)
                split_lo(U_SIN + m, SLOT_SIN + m)

            dve.wait_ge(att_added, 2 * T)
            dve.wait_ge(f1_ps, 12)
            dve.tensor_copy(identf[:, :], ident[:, :]).then_inc(identf_ok, 1)

            def ein_product(t, b, j, reused):
                dve.wait_ge(ei_sil, 2 * t + j + 1)
                if reused:
                    dve.wait_ge(ei_lo, 2 * t + j - 1)
                dve.scalar_tensor_tensor(out=h32[:, j, :], in0=ps[0:P, 2 * j + 1, :],
                                         scalar=S_H / (S_F * S_W), in1=sil[:, j, :],
                                         op0=ALU.mult, op1=ALU.mult).then_inc(ei_mul, 1)

            def logits(t):
                dve.wait_ge(gate_ps, t + 1)
                dve.scalar_tensor_tensor(out=lg[:, t, :], in0=ps[0:P, 7, 0:GATES], scalar=1 / S_F,
                                         in1=gb[:, :], op0=ALU.mult, op1=ALU.add).then_inc(lg_done, 1)

            def norm2(i):
                for b in range(2):
                    t = 2 * i + b
                    dve.wait_ge(w2_ps, t + 1)
                    dve.scalar_tensor_tensor(out=x_sb[:, t, :], in0=ps[0:P, 4 + b, :], scalar=1 / (S_G * S_W),
                                             in1=x_sb[:, t, :], op0=ALU.mult, op1=ALU.add).then_inc(x1_done, 1)
                    dve.wait_ge(x1_done, t + 1)
                    stats(t, b, x_sb[:, t, :], 1.0 + LN_EPS, LN_EPS * LN_EPS)
                    if later(i, b):
                        logits(t - 1)
                    if later(i, b, 2):
                        dve.wait_ge(zt_ps, t - 1)
                    normalise(t, b, x_sb[:, t, :], z2[:, b, :], 1.0)
                    if later(i, b):
                        for j in range(2):
                            ein_product(t - 1, 1 - b, j, later(i, b, 2))
                    dve.wait_ge(f_hi, t + 1)
                    dve.tensor_tensor(fT[:, 1, :, bass.ds(t * P, P)], ft[:, b, :, :],
                                      fT[:, 0, :, bass.ds(t * P, P)], ALU.subtract).then_inc(f_lo, 1)
                    if isinstance(i, int) and i == 0:
                        split_lo(U_SOUT + b, SLOT_SOUT + b)
            tiles(dve, norm2, peeled=2)
            logits(T - 1)
            for j in range(2):
                ein_product(T - 1, 1, j, True)
            for u in range(2):
                split_lo(U_EXP + u, u)

            dve.wait_ge(const2_ok, 1)
            dve.wait_ge(lg_done, T)

            def plane(k, n=EXPERTS):
                return rt[:, k, :, 0:n]

            def wide(ap, n):
                return ap.broadcast_to((P, T, n))

            pg = PER_GROUP
            in1st, in2nd, best = rt[:, 0, :, 0:1], rt[:, 0, :, 1:2], rt[:, 0, :, 2:3]
            second, total, inv = rt[:, 0, :, 3:4], rt[:, 0, :, 4:5], rt[:, 0, :, 5:6]
            c1, c2 = rt[:, 0, :, 6:7], rt[:, 0, :, 7:8]
            link(dve.tensor_tensor(in2nd, lg[:, :, 1:2], lg[:, :, 0:1], ALU.is_gt))
            link(dve.tensor_scalar(in1st, in2nd, -1.0, 1.0, ALU.mult, ALU.add))
            link(dve.tensor_tensor(plane(3, pg), lg[:, :, 2:2 + pg], wide(in1st, pg), ALU.mult))
            link(dve.tensor_tensor(plane(4, pg), lg[:, :, 2 + pg:2 + 2 * pg], wide(in2nd, pg), ALU.mult))
            link(dve.tensor_tensor(plane(3, pg), plane(3, pg), plane(4, pg), ALU.add))
            link(dve.tensor_reduce(best, plane(3, pg), AX.X, ALU.max))
            dve.tensor_tensor(plane(1, pg), plane(3, pg), wide(best, pg), ALU.subtract).then_inc(sel_ok, 1)
            link(dve.tensor_scalar(rt[:, 5, 0, 0:pg], iop[0:P, 0:pg], -1.0, float(pg), ALU.mult, ALU.add))
            rank4 = rt[:, 5, 0:1, 0:pg].broadcast_to((P, T, pg))
            dve.wait_ge(sel_exp, 1)
            link(dve.tensor_reduce(total, plane(2, pg), AX.X, ALU.add))
            link(dve.reciprocal(inv, total))
            link(dve.tensor_tensor(plane(2, pg), plane(2, pg), wide(inv, pg), ALU.mult))

            def choose(probs, value, hot):
                link(dve.tensor_reduce(value, probs, AX.X, ALU.max))
                link(dve.tensor_tensor(hot, probs, wide(value, pg), ALU.is_equal))
                link(dve.tensor_tensor(hot, hot, rank4, ALU.mult))
                link(dve.tensor_reduce(total, hot, AX.X, ALU.max))
                link(dve.tensor_tensor(hot, hot, wide(total, pg), ALU.is_equal))
            choose(plane(2, pg), best, plane(3, pg))
            link(dve.scalar_tensor_tensor(out=plane(6, pg), in0=plane(3, pg), scalar=-2.0, in1=plane(2, pg),
                                          op0=ALU.mult, op1=ALU.add))
            choose(plane(6, pg), second, plane(4, pg))
            link(dve.tensor_tensor(total, best, second, ALU.add))
            link(dve.tensor_scalar(total, total, 1e-8, None, ALU.add))
            link(dve.reciprocal(inv, total))
            link(dve.tensor_tensor(c1, best, inv, ALU.mult))
            link(dve.tensor_tensor(c2, second, inv, ALU.mult))
            for k in range(2):
                dve.tensor_tensor(oh8[:, k, :, 0:pg], plane(3 + k, pg), wide(in1st, pg), ALU.mult)
                link(dve.tensor_tensor(oh8[:, k, :, pg:], plane(3 + k, pg), wide(in2nd, pg), ALU.mult))
            link(dve.tensor_tensor(mask16[:, :, :], oh8[:, 0, :, :], oh8[:, 1, :, :], ALU.add))
            link(dve.memset(before[:, 0, :], 0.0))
            for t in range(T):
                link(dve.tensor_tensor(before[:, t + 1, :], before[:, t, :], mask16[:, t, :], ALU.add))
            dve.nop().then_inc(rank_in, 1)
            dve.memset(cntT[:, :], S_H)
            link(dve.tensor_scalar(thr[:, :], iop[0:P, 0:JW + 1], 128.0, None, ALU.mult))
            dve.nop().then_inc(const2_ok, 1)

            dve.wait_ge(rank_ps, 1)
            taken = rt[:, 7, :, :].rearrange("p t e -> p (t e)").rearrange("p (e k) -> p e k", e=EXPERTS)
            link(dve.tensor_tensor(
                taken, ps[0:P, 6, 128:136].rearrange("p (e k) -> p e k", k=1).broadcast_to((P, EXPERTS, T)),
                thr[:, 0:T].rearrange("p (e k) -> p e k", e=1).broadcast_to((P, EXPERTS, T)), ALU.is_gt))
            n_e, incl, start_e, ones8 = rt[:, 8, 0, :], rt[:, 8, 1, :], rt[:, 8, 2, :], rt[:, 8, 3, :]
            link(dve.tensor_reduce(n_e, taken, AX.X, ALU.add))
            link(dve.tensor_scalar(n_e, n_e, 1.0, None, ALU.max))
            link(dve.memset(ones8, 1.0))
            link(dve.tensor_tensor_scan(incl, ones8, n_e, 0.0, ALU.mult, ALU.add))
            link(dve.tensor_tensor(start_e, incl, n_e, ALU.subtract))
            eids = rt[0:1, 10:12, :, :].rearrange("p a t e -> p (a t e)")
            hits = ge16[0:1, 0:8, :].rearrange("p a b -> p (a b)")[:, 0:JW * (EXPERTS - 1)]\
                .rearrange("p (j e) -> p j e", j=JW)
            link(dve.tensor_tensor(
                hits, rt[0:1, 8, 2:3, 1:EXPERTS].broadcast_to((1, JW, EXPERTS - 1)),
                iop[0:1, 0:JW].rearrange("p (j e) -> p j e", e=1).broadcast_to((1, JW, EXPERTS - 1)), ALU.is_le))
            link(dve.tensor_reduce(eids[:, 0:JW], hits, AX.X, ALU.add))
            dve.tensor_copy(eidt[:, :], eids[:, 0:JW]).then_inc(eid_ok, 1)
            link(dve.tensor_scalar(rt[:, 8, 4, :], start_e, 128.0, None, ALU.mult))
            link(dve.tensor_tensor(plane(6), ps[0:P, 6, 0:T * EXPERTS].rearrange("p (t e) -> p t e", t=T),
                                   rt[:, 8, 4:5, :].broadcast_to((P, T, EXPERTS)), ALU.add))
            slot_f, j_f, p_f, lo_f = tk[:, 0, :], tk[:, 1, :], tk[:, 2, :], tk[:, 3, :]
            for k in range(2):
                link(dve.tensor_tensor(plane(7), oh8[:, k, :, :], plane(6), ALU.mult))
                link(dve.tensor_reduce(slot_f[:, k * T:(k + 1) * T], plane(7), AX.X, ALU.add))
            link(dve.tensor_tensor(ge16[:, :, :],
                                   slot_f.rearrange("p (n j) -> p n j", j=1).broadcast_to((P, 2 * T, JW + 1)),
                                   thr[:, :].rearrange("p (n j) -> p n j", n=1).broadcast_to((P, 2 * T, JW + 1)),
                                   ALU.is_ge))
            link(dve.tensor_reduce(j_f, ge16[:, :, 1:], AX.X, ALU.add))
            link(dve.scalar_tensor_tensor(out=p_f, in0=j_f, scalar=-128.0, in1=slot_f, op0=ALU.mult, op1=ALU.add))
            dve.tensor_tensor(hot_p[:, :, :],
                              iop[0:P, :].rearrange("p (n j) -> p n j", n=1).broadcast_to((P, 2 * T, 128)),
                              p_f.rearrange("p (n j) -> p n j", j=1).broadcast_to((P, 2 * T, 128)), ALU.is_equal)
            link(dve.tensor_tensor(hot_j[:, :, 3, :], ge16[:, :, 0:JW], ge16[:, :, 1:], ALU.subtract))
            link(dve.tensor_copy(tk[:, 4, 0:T].rearrange("p (t o) -> p t o", o=1), c1))
            link(dve.tensor_copy(tk[:, 4, T:2 * T].rearrange("p (t o) -> p t o", o=1), c2))
            link(dve.tensor_copy(c16[:, :], tk[:, 4, :]))
            link(dve.tensor_tensor(lo_f, tk[:, 4, :], c16[:, :], ALU.subtract))

            def spread(ap):
                return ap.rearrange("p (n j) -> p n j", j=1).broadcast_to((P, 2 * T, JW))
            for k in range(2):
                half = slice(k * T, (k + 1) * T)
                dve.tensor_tensor(hot_j[:, half, 0, :], hot_j[:, half, 3, :],
                                  node_id[:, :].rearrange("p (n j) -> p n j", j=1).broadcast_to((P, T, JW)), ALU.mult)
            dve.tensor_tensor(hot_j[:, :, 1, :], hot_j[:, :, 3, :], spread(c16[:, :]), ALU.mult)
            dve.tensor_tensor(hot_j[:, :, 2, :], hot_j[:, :, 3, :], spread(lo_f), ALU.mult).then_inc(hots_ok, 1)
            dve.wait_ge(slot_ps, 1)
            node_s, whi_s, wlo_s, full_s = (ps[:, 7, JW * k:JW * (k + 1)] for k in range(4))
            dve.tensor_copy(gidx[:, :], node_s)
            link(dve.tensor_scalar(wsl[:, :], wlo_s, 1 / (S_H * S_W), None, ALU.mult))
            link(dve.scalar_tensor_tensor(out=wsl[:, :], in0=whi_s, scalar=1 / (S_H * S_W), in1=wsl[:, :],
                                          op0=ALU.mult, op1=ALU.add))
            link(dve.tensor_scalar(padw[:, 0:JW], full_s, -1.0, 1.0, ALU.mult, ALU.add))
            dve.scalar_tensor_tensor(out=sidx[:, :], in0=padw[:, 0:JW], scalar=pad_row[:, :], in1=node_s,
                                     op0=ALU.mult, op1=ALU.add).then_inc(slots_ok, 1)

            def sin(u, first):
                split_lo(U_EXP + 2 + u, 2 + u)
                for m2 in range(2):
                    for c, (at, w) in enumerate(COLS):
                        n = 3 * m2 + c
                        dve.wait_ge(si_sil, 6 * u + n + 1)
                        if not first or n >= 2:
                            dve.wait_ge(si_lo, 6 * u + n - 1)
                        dve.scalar_tensor_tensor(out=h32_s[:, n % 2, 0:w], in0=ps[:, 2 * c + 1, 0:w],
                                                 scalar=S_H / (S_F * S_W), in1=sil_s[:, n % 2, 0:w],
                                                 op0=ALU.mult, op1=ALU.mult).then_inc(si_mul, 1)
            sin(0, True)
            with dve.Fori(1, 4) as u:
                sin(u, False)
            for u in range(6, 2 * EXPERTS - LATE):
                split_lo(U_EXP + u, u)

            dve.wait_ge(si_lo, 24)

            def sout(i):
                for b in range(2):
                    t = 2 * i + b
                    dve.wait_ge(so_ps, t + 1)
                    if later(i, b):
                        dve.wait_ge(acc_out, 16 * t)
                    dve.scalar_tensor_tensor(out=acc[:, b, :], in0=ps[0:P, 6 + b, :], scalar=1 / (S_H * S_W),
                                             in1=x_sb[:, t, :], op0=ALU.mult, op1=ALU.add).then_inc(so_done, 1)
            tiles(dve, sout)

            def turned_lo(i, b):
                j = 2 * i + b
                dve.wait_ge(tr_ps, j + 1)
                if later(i, b, 2):
                    dve.wait_ge(ex_ps, j - 1)
                dve.tensor_copy(heT[:, b, 1, :, :], ps16[:, 5 + 2 * b, :].rearrange("p (h n) -> p h n", h=HB))\
                   .then_inc(ht_lo, 1)

            def routed(i, units):
                for b in range(2):
                    turned_lo(i, 1) if b == 0 else turned_lo(i + 1, 0)
                    if units:
                        split_lo(2 * i + (U_LATE + b), 2 * i + (SLOT_LATE + b), (U_LATE + b) % 2)
            turned_lo(0, 0)
            routed(0, True)
            with dve.Fori(1, LATE // 2) as i:
                routed(i, True)
            with dve.Fori(LATE // 2, MAX_TILES // 2) as i:
                routed(i, False)

        @block.tensor
        def _(pe):
            def product(out_ap, left, right, blocks, start=True, stop=True):
                for k in range(blocks):
                    for lh, rh in ((0, 0), (0, 1), (1, 0)):
                        ins = pe.matmul(out_ap, left(lh, k), right(rh, k), start=start and k + lh + rh == 0,
                                        stop=stop and k == blocks - 1 and lh == 1)
                return ins

            def weight(slot, h, k, at=0, n=512):
                return wslots[:, slot, h, k * 512 + at:k * 512 + at + n] if isinstance(at, int) else \
                    wslots[:, slot, h, bass.ds(at + k * 512, n)]

            pe.wait_ge(diag_ok, 1)
            pe.matmul(ps[0:T, 6, 0:4 * HALF], ones[0:HALF, 0:T], diag[:, :, :], start=True, stop=True)\
              .then_inc(rows_ps, 1)
            pe.wait_ge(range_ok, 1)
            pe.matmul(ps[0:1, 7, 0:T + 1], rs16[:, 1:2], tri[0:T, 0:T + 1], start=True, stop=True)
            pe.matmul(ps[0:1, 7, 16:16 + T], rs16[:, 0:1], ident[0:T, 0:T], start=True, stop=True)\
              .then_inc(tab_ps, 1)
            pe.wait_ge(tab_ok, 1)

            def state(t, b, first):
                pe.wait_ge(k_done, t + 1)
                pe.wait_ge(v_done, t + 1)
                for a in range(KB):
                    ins = pe.matmul(ps[:, 5, a * 128:(a + 1) * 128], kbuf[:, b, a * 128:(a + 1) * 128],
                                    vbuf[:, b, a * 128:(a + 1) * 128], start=first and a == 0, stop=True,
                                    skip_group_check=True)
                ins.then_inc(kv_used, 1)

            def nodes(i):
                for b in range(2):
                    t = 2 * i + b
                    if later(i, b):
                        pe.wait_ge(a_copied, t)
                    for c in range(3):
                        at = N_NODES - P + c * 417
                        pe.matmul(ps[0:P, c, 0:417], ident[0:P, 0:P], band[:, bass.ds(at - t * P, 417)],
                                  start=True, stop=True)
                    first = pe.value_load(tabs[0:1, bass.ds(t, 1)], min_val=0, max_val=T * (HALF + 1))
                    end = pe.value_load(tabs[0:1, bass.ds(t + 1, 1)], min_val=1, max_val=T * (HALF + 1))
                    with pe.Fori(first, end) as v:
                        pe.wait_ge(hot_ready, v + 1)
                        for q in range(2):
                            place = (v % RING) * 2 + q
                            for c in range(3):
                                ins = pe.matmul(ps[0:P, c, 0:417], hot_dst[:, place, 0:P],
                                                hot_src[:, place, c * 417:(c + 1) * 417], start=False, stop=True,
                                                skip_group_check=True)
                        ins.then_inc(hot_used, 1)
                    pe.wait_ge(xn_lo, t + 1)
                    if later(i, b):
                        pe.wait_ge(adj_out, t)
                    for h in range(2):
                        for k in range(KB):
                            ins = pe.matmul(ps[:, 6 + h, k * P:(k + 1) * P], xn[:, h, t, k * 128:(k + 1) * 128],
                                            ident[0:P, 0:P], start=True, stop=True)
                    ins.then_inc(xcol_ps, 1)
                    if later(i, b):
                        state(t - 1, 1 - b, isinstance(i, int) and t == 1)
                    pe.wait_ge(xcol_out, t + 1)
                    for bank, s, done, free in ((3, SLOT_WK, k_ps, k_act), (4, SLOT_WV, v_ps, v_done)):
                        if not later(i, b):
                            pe.wait_ge(w_lo, (U_WK if s == SLOT_WK else U_WV) + 1)
                        else:
                            pe.wait_ge(free, t)
                        product(ps[0:P, bank, :], lambda h, k: xnT[:, h, k, bass.ds(t * P, P)],
                                lambda h, k: weight(s, h, k), KB).then_inc(done, 1)
                    pe.wait_ge(a_copied, t + 1)
                    for s in range(T):
                        ins = pe.transpose(ps16[0:P, 6 + s // 5, (s % 5) * 128:(s % 5) * 128 + P],
                                           a_row[:, s * P:(s + 1) * P], ident[0:P, 0:P])
                    ins.then_inc(a_turned, 1)
            pe.wait_ge(const_ok, 17)
            pe.sem_inc(hot_used, RING)
            tiles(pe, nodes)
            state(T - 1, 1, False)
            pe.wait_ge(ksum_c, T)
            for a in range(KB):
                ins = pe.matmul(ps[:, 4, 2 * a:2 * a + 2], ksum[:, a * 128:(a + 1) * 128], onesf[0:P, :],
                                start=True, stop=True)
            ins.then_inc(ksum_ps, 1)
            pe.wait_ge(adj_out, T)

            pe.wait_ge(k_act, T)
            pe.wait_ge(v_done, T)
            pe.wait_ge(w_lo, U_WQ + 1)
            for m in range(KB):
                for c, (at, w) in enumerate(COLS):
                    n = 3 * m + c
                    if n >= 6:
                        pe.wait_ge(q_act, n - 5)
                    product(ps[:, [0, 1, 2, 3, 6, 7][n % 6], 0:w],
                            lambda h, k: weight(SLOT_WQ, h, k, m * 128, 128),
                            lambda h, k: xnT[:, h, k, at:at + w], KB).then_inc(q_ps, 1)

            pe.wait_ge(q_done, 12)
            pe.wait_ge(kvd_ok, 1)
            for t in range(T):
                if t >= 2:
                    pe.wait_ge(o_done, t - 1)
                for a in range(KB):
                    ins = pe.matmul(ps[0:P, 2 * (t % 2) + a // 2, (a % 2) * 130:(a % 2) * 130 + 130],
                                    qT[:, a, t * P:(t + 1) * P], kvd[:, a, :], start=True, stop=True)
                ins.then_inc(o_ps, 1)

            pe.wait_ge(q_act, 12)
            for m in range(KB):
                banks = [4, 5, 6, 7, 0, 1][3 * (m % 2):3 * (m % 2) + 3]
                if m == 1:
                    pe.wait_ge(o_done, T)
                if m >= 2:
                    pe.wait_ge(n_lo, 3 * (m - 1))
                for s in range(T):
                    for h in range(2):
                        for c, (at, w) in enumerate(COLS):
                            ins = pe.matmul(ps[:, banks[c], 0:w], xn[:, h, s, m * 128:(m + 1) * 128],
                                            adjT[:, s, at:at + w], start=s + h == 0, stop=s == T - 1 and h == 1)
                ins.then_inc(n_ps, 1)

            pe.wait_ge(n_lo, 12)
            pe.wait_ge(w_lo, U_W2 + 1)
            for m in range(KB):
                for c, (at, w) in enumerate(COLS):
                    n = 3 * m + c
                    if n >= 6:
                        pe.wait_ge(g_act, n - 5)
                    product(ps[:, 2 + n % 6, 0:w], lambda h, k: weight(SLOT_W1, h, k, m * 128, 128),
                            lambda h, k: h1T[:, h, k, at:at + w], KB).then_inc(f1_ps, 1)

            pe.wait_ge(g_lo, 12)
            pe.wait_ge(identf_ok, 1)
            pe.wait_ge(g_act, 12)

            def turn2(t, b, reused):
                pe.wait_ge(z_ok, t + 1)
                if reused:
                    pe.wait_ge(ft_act, t)
                for k in range(KB):
                    ins = pe.transpose(ps[:, 6, k * P:(k + 1) * P], z2[:, b, k * 128:(k + 1) * 128],
                                       identf[0:P, 0:P])
                ins.then_inc(zt_ps, 1)

            def gates(t, b, reused):
                pe.wait_ge(ft_act, t + 1)
                if reused:
                    pe.wait_ge(lg_done, t)
                for k in range(KB):
                    ins = pe.matmul(ps[0:P, 7, 0:GATES], ft[:, b, k, :], gw[:, k, :], start=k == 0,
                                    stop=k == KB - 1)
                ins.then_inc(gate_ps, 1)

            def ein(t, reused):
                pe.wait_ge(f_lo, t + 1)
                for j in range(2):
                    if reused:
                        pe.wait_ge(ei_mul, 2 * t + j - 1)
                    for half in range(2):
                        ins = product(ps[0:P, 2 * j + half, :],
                                      lambda h, k: fT[:, h, k, bass.ds(t * P, P)],
                                      lambda h, k: weight(SLOT_EIN + 2 * half + j, h, k), KB)
                    ins.then_inc(ei_ps, 1)

            def norm2(i):
                for b in range(2):
                    t = 2 * i + b
                    if later(i, b, 2):
                        pe.wait_ge(x1_done, t - 1)
                    product(ps[0:P, 4 + b, :], lambda h, k: r1T[:, h, k, bass.ds(t * P, P)],
                            lambda h, k: weight(SLOT_W2, h, k), KB).then_inc(w2_ps, 1)
                    if later(i, b):
                        gates(t - 1, 1 - b, later(i, b, 2))
                        ein(t - 1, later(i, b, 2))
                    turn2(t, b, later(i, b))
            tiles(pe, norm2, peeled=2)
            gates(T - 1, 1, True)
            ein(T - 1, True)

            pe.wait_ge(ei_mul, 2 * T)
            pe.wait_ge(rank_in, 1)
            pe.matmul(ps[0:P, 6, 0:T * EXPERTS], ones[0:P, 0:P], before[:, 0:T, :], start=True, stop=False)
            pe.matmul(ps[0:P, 6, 0:T * EXPERTS], tri[0:P, 0:P], mask16[:, :, :], start=False, stop=True)
            pe.matmul(ps[0:P, 6, 128:128 + EXPERTS], ones[0:P, 0:P], before[:, T, :], start=True, stop=True)\
              .then_inc(rank_ps, 1)
            pe.wait_ge(hots_ok, 1)
            for n in range(2 * T):
                ins = pe.matmul(ps[:, 7, 0:4 * JW], hot_p[:, n, :], hot_j[:, n, :, :], start=n == 0,
                                stop=n == 2 * T - 1)
            ins.then_inc(slot_ps, 1)

            pe.wait_ge(w_lo, U_SIN + 4)

            def sin(u, first):
                for m2 in range(2):
                    for c, (at, w) in enumerate(COLS):
                        n = 3 * m2 + c
                        if not first or n >= 3:
                            pe.wait_ge(si_mul, 6 * u + n - 2)
                        for half in range(2):
                            ins = product(
                                ps[:, 2 * c + half, 0:w],
                                lambda h, k: wslots[:, SLOT_SIN + u, h,
                                                    ((m2 * 2 + half) * KB + k) * 128:((m2 * 2 + half) * KB + k + 1) * 128],
                                lambda h, k: fT[:, h, k, at:at + w], KB)
                        ins.then_inc(si_ps, 1)
            sin(0, True)
            with pe.Fori(1, 4) as u:
                sin(u, False)

            pe.wait_ge(slots_ok, 1)
            pe.wait_ge(si_mul, 24)
            for t in range(T):
                ins = pe.matmul(ps[0:EXPERTS, [6, 7, 0][t // 4], (t % 4) * P:(t % 4 + 1) * P], mask16[:, t, :],
                                ident[0:P, 0:P], start=True, stop=True)
            ins.then_inc(cnt_ps, 1)

            pe.wait_ge(cnt_ok, 3)
            pe.wait_ge(si_lo, 24)
            pe.wait_ge(w_lo, U_SOUT + 2)

            def sout(i):
                for b in range(2):
                    t = 2 * i + b
                    if later(i, b, 2):
                        pe.wait_ge(so_done, t - 1)
                    out_ap = ps[0:P, 6 + b, :]
                    for h in range(2):
                        pe.matmul(out_ap, cntT[:, bass.ds(t * P, P)], bias9[:, h, :], start=h == 0, stop=False)
                    product(out_ap, lambda h, k: (hsl if h else hsh)[:, k, bass.ds(t * P, P)],
                            lambda h, k: weight(SLOT_SOUT + k // 4, h, k % 4), HB, start=False).then_inc(so_ps, 1)
            tiles(pe, sout)

            def turn_rows(i, b):
                j = 2 * i + b
                pe.wait_ge(got_ok[b], 16 * i + 16)
                if later(i, b, 2):
                    pe.wait_ge(ht_hi, j - 1)
                    pe.wait_ge(ht_lo, j - 1)
                for h in range(2):
                    for k in range(HB):
                        ins = pe.transpose(ps16[:, 4 + 2 * b + h, k * 128:(k + 1) * 128],
                                           got[:, b, h * HID + k * 128:h * HID + (k + 1) * 128], ident[:, :])
                ins.then_inc(tr_ps, 1)

            def expert(i, b):
                j = 2 * i + b
                e = pe.value_load(eidt[0:1, bass.ds(j, 1)], min_val=0, max_val=EXPERTS - 1)
                pe.wait_ge(ht_hi, j + 1)
                pe.wait_ge(ht_lo, j + 1)
                if later(i, b, 2):
                    pe.wait_ge(y_ok, j - 1)
                pe.wait_ge(w_lo, e * 2 + U_EXP + 2)
                product(ps[:, b, :], lambda h, k: heT[:, b, h, k, :],
                        lambda h, k: weight(e * 2 + k // 4, h, k % 4), HB).then_inc(ex_ps, 1)

            pe.wait_ge(eid_ok, 1)
            pe.wait_ge(so_done, T)
            turn_rows(0, 0)

            def routed(i):
                turn_rows(i, 1)
                expert(i, 0)
                turn_rows(i + 1, 0)
                expert(i, 1)
            routed(0)
            with pe.Fori(1, MAX_TILES // 2) as i:
                routed(i)
            expert(MAX_TILES // 2, 0)


_OUT_ROWS = N_NODES + 128


def kernel(**inputs):
    import numpy as _np
    import concourse.bacc as _bacc
    from concourse import mybir as _mybir
    from concourse.bass_utils import run_bass_kernel_spmd as _run

    a = {k: _np.asarray(v) for k, v in inputs.items()}

    def units(w):
        n_in, n_out = w.shape
        w = w.reshape(n_in // 512, 4, 128, n_out // 512, 512)
        return w.transpose(3, 0, 2, 1, 4).reshape(-1, 128, UNIT)

    def paired(w):
        w = w.reshape(KB, 128, 2, 4, 2, 128)
        return w.transpose(3, 1, 4, 2, 0, 5).reshape(4, 128, UNIT)

    kv = a["L0_mix_Wkv"].T
    weights = [units(kv[:, :D]), units(kv[:, D:]), units(a["L0_mix_Wq"].T), units(a["L0_gnn_W1"]),
               units(a["L0_gnn_W2"]), units(a["L0_ffn_expert_in_w"].T), paired(a["L0_ffn_shared_in_w"].T),
               units(a["L0_ffn_shared_out_w"].T)]
    weights += [units(a["L0_ffn_expert_out_weight"][e].T) for e in range(EXPERTS)]
    gate = _np.concatenate([a["L0_ffn_group_gate_w"], a["L0_ffn_expert_gate_w"]])
    arrays = {
        "x": a["x"],
        "dst_rows": a["dst"].reshape(2, HALF, P).transpose(1, 0, 2),
        "dst_cols": a["dst"].reshape(CHUNKS, P).T,
        "src_cols": a["src"].reshape(CHUNKS, P).T,
        "weights": _np.concatenate(weights),
        "b1": a["L0_gnn_b1"].reshape(KB, 128).T,
        "b2": a["L0_gnn_b2"].reshape(1, D),
        "ln_scale": a["L0_ffn_ln_scale"].reshape(KB, 128).T,
        "ln_bias": a["L0_ffn_ln_bias"].reshape(KB, 128).T,
        "gate_w": gate.T.reshape(KB, 128, GATES).transpose(1, 0, 2),
        "gate_b": _np.concatenate([a["L0_ffn_group_bias"], a["L0_ffn_expert_bias"]]).reshape(1, GATES),
        "expert_b": a["L0_ffn_expert_out_bias"],
        "shared_b": a["L0_ffn_shared_out_b"].reshape(1, D),
    }
    arrays = {k: _np.ascontiguousarray(v) for k, v in arrays.items()}
    nc = _bacc.Bacc("TRN2", target_bir_lowering=False, num_devices=1)
    dram = {k: nc.dram_tensor(k, v.shape, _mybir.dt.from_np(v.dtype), kind="ExternalInput").ap()
            for k, v in arrays.items()}
    out = nc.dram_tensor("out", (_OUT_ROWS, D), F32, kind="ExternalOutput").ap()
    hid = nc.dram_tensor("hid", (N_NODES, 2 * HID), F16, kind="Internal").ap()
    gps_layer(nc, dram, out, hid)
    r = _run(nc, [arrays], core_ids=[0])
    return r.results[0]["out"][:N_NODES]
```

```python
from contextlib import ExitStack

import numpy as np

import concourse.bass as bass
from concourse import mybir

F32 = mybir.dt.float32
F16 = mybir.dt.float16
I32 = mybir.dt.int32
U32 = mybir.dt.uint32
ALU = mybir.AluOpType
ACT = mybir.ActivationFunctionType
AX = mybir.AxisListType

N_NODES, D, HEADS, HID = 1250, 512, 8, 1024
N_EDGES = 21250
P = 125
T = N_NODES // P
KB = D // 128
HB = HID // 128
EXPERTS, GROUPS, PER_GROUP = 8, 2, 4
GATES = GROUPS + EXPERTS
CHUNKS = N_EDGES // P
HALF = CHUNKS // 2
GROUP = 3
STEPS = -(-CHUNKS // GROUP)
RING = 3
COLS = [(0, 417), (417, 417), (834, 416)]
WIDE = 3 * 417
UNIT = 2048
MAX_TILES = (2 * N_NODES + EXPERTS * 127) // 128
JW = 32

U_WK, U_WV, U_WQ, U_W1, U_W2, U_EIN, U_SIN, U_SOUT, U_EXP = 0, 1, 2, 3, 4, 5, 9, 13, 15
N_UNITS = U_EXP + 2 * EXPERTS
LATE = 8
U_LATE = N_UNITS - LATE
SLOT_WK, SLOT_WV, SLOT_WQ, SLOT_W1, SLOT_W2 = 4, 5, 6, 14, 15
SLOT_EIN, SLOT_SIN, SLOT_SOUT, SLOT_LATE = 0, 4, 11, 16 - LATE

S_X = 2.0 ** 8
S_F = 2.0 ** 6
S_W = 2.0 ** 8
S_G = 2.0 ** -4
S_H = 2.0 ** 4
LN_EPS = 1e-5
ATT_EPS = 1e-6
IN_RANGE = "the tables of the chunk search stay within the chunks"
CO_SHIFT = 4096


class Region:

    def __init__(self, nc, start, size):
        self.nc, self.at, self.end = nc, start, start + size

    def put(self, name, shape, dt):
        size = int(np.prod(shape[1:])) * (2 if dt == F16 else 4)
        t = self.nc.alloc_sbuf_tensor_at(name, list(shape), dt, offset=self.at, align_bytes=4)
        self.at += (size + 3) // 4 * 4
        assert self.at <= self.end, (name, self.at, self.end)
        return t


def gps_layer(nc, d, out, hid_dram):
    with ExitStack() as ctx:
        base = (nc.sbuf_base + 31) // 32 * 32
        slot_bytes = 2 * UNIT * 2

        def region(start, size):
            return Region(nc, start, size)

        def slots(first, n=1):
            return region(base + first * slot_bytes, n * slot_bytes)

        top = base + 16 * slot_bytes
        r_x = region(top, T * D * 4)
        r_stage = region(r_x.end, 2 * UNIT * 4)
        r_f = region(r_stage.end, T * D * 4)
        r_g = region(r_f.end, 20000)
        small = region(r_g.end, nc.sbuf_usable_end - r_g.end)

        wslots = slots(0, 16).put("wslots", [128, 16, 2, UNIT], F16)
        x_sb = r_x.put("x_sb", [P, T, D], F32)
        stage = r_stage.put("stage", [128, 2, UNIT], F32)

        def again(r):
            return region(r.end - size_of[r], size_of[r])

        size_of = {r_f: T * D * 4, r_g: 20000}
        xn = r_f.put("xn", [P, 2, T, D], F16)
        xnT = r_g.put("xnT", [128, 2, KB, N_NODES], F16)
        h1T = again(r_g).put("h1T", [128, 2, KB, N_NODES], F16)
        r = slots(0, 4)
        hot_dst = r.put("hot_dst", [P, GROUP * RING, P + 1], F16)
        a_row = r.put("a_row", [P, WIDE + 1], F16)
        band = r.put("band", [P, N_NODES - P + WIDE + 1], F16)
        iota = r.put("iota", [P, WIDE + 1], F16)
        search = region(r.at, 2 * 2 * D * 4)
        z1 = r.put("z1", [P, 2, D], F32)
        ekey = r.put("ekey", [P, 2, D], F32)
        ksum = r.put("ksum", [P, D], F32)
        bias_in = r.put("bias_in", [EXPERTS + 1, D], F32)
        b1 = r.put("b1", [128, KB], F32)
        lnp = r.put("lnp", [128, 2, KB], F32)
        srci = r.put("srci", [P, CHUNKS], I32)
        dsti = r.put("dsti", [P, CHUNKS], I32)
        srcf = r.put("srcf", [P, CHUNKS + GROUP], F32)
        dstf = r.put("dstf", [P, CHUNKS + GROUP], F32)
        dst2 = search.put("dst2", [HALF, 2, P], I32)
        diag = search.put("diag", [HALF, 4, HALF], F16)
        mnmx = search.put("mnmx", [HALF, 4], F32)
        rngf = search.put("rngf", [T, 4, CHUNKS], F32)
        cup = search.put("cup", [T, 2, CHUNKS], F32)
        rsm = search.put("rsm", [T, 8], F32)
        rs16 = search.put("rs16", [T, 2], F16)
        step_at = search.put("step_at", [T, STEPS], F32)
        st1 = r.put("st1", [P, T, 6], F32)
        mv1 = r.put("mv1", [P, T, 2], F32)
        r1 = r.put("r1", [P, 8, T], F32)
        r = slots(8, 3)
        hot_src = r.put("hot_src", [P, GROUP * RING, WIDE + 1], F16)
        r = slots(7)
        kbuf = r.put("kbuf", [P, 2, D], F32)
        vbuf = r.put("vbuf", [P, 2, D], F32)
        r = slots(7)
        kvd = r.put("kvd", [128, KB, 130], F32)
        b2b = r.put("b2b", [P, D], F32)
        r_q = slots(8, 3)
        qT = r_q.put("qT", [128, KB, N_NODES], F32)
        spare = (r_q.at, r_q.end - 424 - r_q.at)
        r1T = slots(8, 3).put("r1T", [128, 2, KB, N_NODES], F16)
        ebuf = region(*spare).put("ebuf", [128, 2, D], F32)
        att = region(*spare).put("att", [P, 2, D], F32)
        rbuf = region(*spare).put("rbuf", [128, 2, 417], F32)
        adjT = region(r_q.end - 424, 3 * slot_bytes + 424).put("adjT", [P, T, N_NODES], F16)
        r = again(r_f)
        fT = r.put("fT", [128, 2, KB, N_NODES], F16)
        lg = r.put("lg", [P, T, GATES], F32)
        r = again(r_g)
        z2 = r.put("z2", [P, 2, D], F32)
        ft = r.put("ft", [128, 2, KB, P], F32)
        identf = r.put("identf", [128, 128], F32)
        r = region(*spare)
        cntT = r.put("cntT", [EXPERTS + 1, N_NODES], F16)
        mask16 = r.put("mask16", [P, T, EXPERTS], F16)
        before = r.put("before", [P, T + 1, EXPERTS], F16)
        oh8 = r.put("oh8", [P, 2, T, EXPERTS], F32)
        tk = r.put("tk", [P, 8, 2 * T], F32)
        r = slots(14)
        sil = r.put("sil", [P, 2, D], F32)
        h32 = r.put("h32", [P, 2, D], F32)
        r = slots(14, 2)
        rt = r.put("rt", [P, 12, T, EXPERTS], F32)
        iop = r.put("iop", [128, 128], F32)
        thr = r.put("thr", [P, JW + 1], F32)
        ge16 = r.put("ge16", [P, 2 * T, JW + 1], F16)
        c16 = r.put("c16", [P, 2 * T], F16)
        padw = r.put("padw", [128, JW], F32)
        hot_p = r.put("hot_p", [P, 2 * T, 128], F16)
        hot_j = r.put("hot_j", [P, 2 * T, 4, JW], F16)
        he = slots(13).put("he", [P, 2, 2, HID], F16)
        r = slots(13)
        sil_s = r.put("sil_s", [128, 2, 417], F32)
        h32_s = r.put("h32_s", [128, 2, 417], F32)
        acc = slots(13).put("acc", [P, 2, D], F32)
        hsh = slots(8, 3).put("hsh", [128, HB, N_NODES], F16)
        hsl = again(r_g).put("hsl", [128, HB, N_NODES], F16)
        r = again(r_f)
        got = r.put("got", [128, 2, 2 * HID], F16)
        y = r.put("y", [128, 2, D], F32)
        pad0 = r.put("pad0", [128, D], F32)
        heT = [r.put("heT0", [128, 2, HB, 128], F16), again(r_g).put("heT1", [128, 2, HB, 128], F16)]

        ident = small.put("ident", [128, 128], F16)
        tri = small.put("tri", [128, 128], F16)
        ones = small.put("ones", [128, 128], F16)
        onesf = small.put("onesf", [128, 2], F32)
        b1s = small.put("b1s", [128, KB], F32)
        lns = small.put("lns", [128, 2, KB], F32)
        gw = small.put("gw", [128, KB, GATES], F32)
        gb = small.put("gb", [P, GATES], F32)
        tabs = small.put("tabs", [1, 32], I32)
        tabf = small.put("tabf", [1, 32], F32)
        st6 = small.put("st6", [P, 2, 6], F32)
        mv = small.put("mv", [P, 2, 2], F32)
        ve = small.put("ve", [P, 2, 1], F32)
        sd = small.put("sd", [P, 2, 1], F32)
        rst = small.put("rst", [P, 2, 4], F32)
        den = small.put("den", [P, 2, 2, HEADS], F32)
        node_id = small.put("node_id", [P, T], F32)
        tlo = small.put("tlo", [T, 2], F32)
        pad_row = small.put("pad_row", [128, 1], F32)
        bias9 = small.put("bias9", [EXPERTS + 1, 2, D], F16)
        eidt = small.put("eidt", [1, JW], I32)
        gidx = small.put("gidx", [128, JW], U32)
        sidx = small.put("sidx", [128, JW], U32)
        wsl = small.put("wsl", [128, JW], F32)
        gcur = small.put("gcur", [128, 2], U32)
        scur = small.put("scur", [128, 2], U32)

        ps = ctx.enter_context(nc.psum_tensor("ps", [128, 8, 512], F32))
        ps16 = ps[:, :, :].bitcast(F16)

        def sem(name):
            return ctx.enter_context(nc.semaphore(name))

        x0_in = sem("x0_in")
        edge_in, x_in, small_in, stage_in = sem("edge_in"), sem("x_in"), sem("small_in"), sem("stage_in")
        b2_in, hid_out, acc_out, pad_out = sem("b2_in"), sem("hid_out"), sem("acc_out"), sem("pad_out")
        const_ok, const2_ok = sem("const_ok"), sem("const2_ok")
        w_scaled = sem("w_scaled")
        w_hi, w_lo = sem("w_hi"), sem("w_lo")
        bias_hi, bias_lo, par_ok = sem("bias_hi"), sem("bias_lo"), sem("par_ok")
        dve_c = sem("dve_c")
        edges_f, diag_ok, rows_ps, range_ok, tab_ps, tab_ok = (
            sem("edges_f"), sem("diag_ok"), sem("rows_ps"), sem("range_ok"), sem("tab_ps"), sem("tab_ok"))
        hot_ready, hot_used, ksum_c, ksum_ps = (
            sem("hot_ready"), sem("hot_used"), sem("ksum_c"), sem("ksum_ps"))
        a_copied, a_turned, adj_out = sem("a_copied"), sem("a_turned"), sem("adj_out")
        ln_bn, ln_mv, ln_ve, ln_sd, ln_r, z_ok = (
            sem("ln_bn"), sem("ln_mv"), sem("ln_ve"), sem("ln_sd"), sem("ln_r"), sem("z_ok"))
        var_ok, root_ok, scale_ok, z1_ok = sem("var_ok"), sem("root_ok"), sem("scale_ok"), sem("z1_ok")
        xn_hi, xn_lo = sem("xn_hi"), sem("xn_lo")
        xcol_ps, xcol_out = sem("xcol_ps"), sem("xcol_out")
        k_ps, v_ps, k_act, k_done, v_done, kv_used = (
            sem("k_ps"), sem("v_ps"), sem("k_act"), sem("k_done"), sem("v_done"), sem("kv_used"))
        k_neg, q_neg = sem("k_neg"), sem("q_neg")
        q_ps, q_act, q_done = sem("q_ps"), sem("q_act"), sem("q_done")
        kvd_ok, o_ps, den_c, o_done, att_added = (
            sem("kvd_ok"), sem("o_ps"), sem("den_c"), sem("o_done"), sem("att_added"))
        n_ps, n_hi, n_lo = sem("n_ps"), sem("n_hi"), sem("n_lo")
        f1_ps, g_act, g_lo = sem("f1_ps"), sem("g_act"), sem("g_lo")
        w2_ps, x1_done, zt_ps, ft_act, f_hi, f_lo, gate_ps, lg_done = (
            sem("w2_ps"), sem("x1_done"), sem("zt_ps"), sem("ft_act"), sem("f_hi"), sem("f_lo"),
            sem("gate_ps"), sem("lg_done"))
        ei_ps, ei_sil, ei_mul, ei_hi, ei_lo = (
            sem("ei_ps"), sem("ei_sil"), sem("ei_mul"), sem("ei_hi"), sem("ei_lo"))
        rank_in, rank_ps, hots_ok, slot_ps, slots_ok, cnt_ps, cnt_ok, eid_ok = (
            sem("rank_in"), sem("rank_ps"), sem("hots_ok"), sem("slot_ps"), sem("slots_ok"),
            sem("cnt_ps"), sem("cnt_ok"), sem("eid_ok"))
        si_ps, si_sil, si_mul, si_hi, si_lo = (
            sem("si_ps"), sem("si_sil"), sem("si_mul"), sem("si_hi"), sem("si_lo"))
        so_ps, so_done = sem("so_ps"), sem("so_done")
        pad_ok, idx_ok, got_ok, tr_ps, ht_hi, ht_lo, ex_ps, y_ok = (
            sem("pad_ok"), sem("idx_ok"), [sem("got_ok0"), sem("got_ok1")], sem("tr_ps"),
            sem("ht_hi"), sem("ht_lo"), sem("ex_ps"), sem("y_ok"))
        passed = sem("passed")
        sel_ok, sel_exp, identf_ok = sem("sel_ok"), sem("sel_exp"), sem("identf_ok")
        idx2_ok, added = sem("idx2_ok"), sem("added")

        n_small = 7 * 16
        block = ctx.enter_context(nc.Block())

        def tiles(eng, step, peeled=1):
            for i in range(peeled):
                step(i)
            with eng.Fori(peeled, T // 2) as i:
                step(i)

        first_units = [(U_WK, SLOT_WK), (U_WV, SLOT_WV), (U_WQ, SLOT_WQ), (U_W1, SLOT_W1), (U_W2, SLOT_W2)]

        late_units = [(U_SIN + 3, SLOT_SIN + 3), (U_SOUT, SLOT_SOUT), (U_SOUT + 1, SLOT_SOUT + 1)]

        def later(i, b, n=1):
            return not isinstance(i, int) or 2 * i + b >= n

        @block.sync
        def _(sp):
            sp.dma_start(dst2[:, :, :], d["dst_rows"]).then_inc(edge_in, 16)
            sp.dma_start(dsti[:, :], d["dst_cols"]).then_inc(edge_in, 16)
            sp.dma_start(srci[:, :], d["src_cols"]).then_inc(edge_in, 16)
            xv = d["x"].rearrange("(t p) c -> p t c", p=P)
            for landed, at in ((x0_in, slice(0, 2)), (x_in, slice(2, T))):
                sp.dma_start(x_sb[0:112, at, :], xv[0:112, at]).then_inc(landed, 16)
                sp.dma_start(x_sb[112:P, at, :], xv[112:P, at]).then_inc(landed, 16)
            sp.dma_start(stage[:, 0, :], d["weights"][0]).then_inc(stage_in, 16)
            sp.dma_start(b1[:, :], d["b1"]).then_inc(small_in, 16)
            sp.dma_start(lnp[:, 0, :], d["ln_scale"]).then_inc(small_in, 16)
            sp.dma_start(lnp[:, 1, :], d["ln_bias"]).then_inc(small_in, 16)
            sp.dma_start(gw[:, :, :], d["gate_w"]).then_inc(small_in, 16)
            sp.dma_start(gb[:, :], d["gate_b"].broadcast_to((P, GATES))).then_inc(small_in, 16)
            sp.dma_start(bias_in[0:EXPERTS, :], d["expert_b"]).then_inc(small_in, 16)
            sp.dma_start(bias_in[EXPERTS:EXPERTS + 1, :], d["shared_b"]).then_inc(small_in, 16)
            sp.wait_ge(stage_in, 16)
            sp.dma_start(stage[:, 1, :], d["weights"][1]).then_inc(stage_in, 16)
            with sp.Fori(2, N_UNITS) as u:
                sp.wait_ge(stage_in, 16 * u)
                sp.sem_inc(passed, 1)
                sp.wait_ge(w_lo, u - 1)
                sp.sem_inc(passed, 1)
                sp.dma_start(stage[:, u % 2, :], d["weights"][u]).then_inc(stage_in, 16)

        @block.gpsimd
        def _(pool):
            pool.memset(ident[:, :], 0.0).then_inc(const_ok, 1)
            pool.memset(ones[:, :], 1.0).then_inc(const_ok, 1)
            pool.wait_ge(const_ok, 2)
            pool.affine_select(out=ident[:, :], in_=ident[:, :], compare_op=ALU.not_equal, fill=1.0,
                               base=0, pattern=[[-1, 128]], channel_multiplier=1).then_inc(const_ok, 1)
            pool.affine_select(out=tri[:, :], in_=ones[:, :], compare_op=ALU.is_gt, fill=0.0,
                               base=0, pattern=[[1, 128]], channel_multiplier=-1).then_inc(const_ok, 1)
            exact = {"allow_small_or_imprecise_dtypes": True}
            pool.iota(cup[:, 0, :], [[1, CHUNKS]], base=1, channel_multiplier=0, **exact).then_inc(const_ok, 1)
            pool.iota(cup[:, 1, :], [[-1, CHUNKS]], base=CHUNKS, channel_multiplier=0, **exact).then_inc(const_ok, 1)
            pool.iota(step_at[:, :], [[GROUP, STEPS]], base=0, channel_multiplier=0, **exact).then_inc(const_ok, 1)
            pool.iota(tlo[:, :], [[P, 2]], base=0, channel_multiplier=P, **exact).then_inc(const_ok, 1)
            pool.iota(iota[:, :], [[1, WIDE + 1]], base=0, channel_multiplier=0, **exact).then_inc(const_ok, 1)
            pool.iota(node_id[:, :], [[P, T]], base=0, channel_multiplier=1, **exact).then_inc(const_ok, 1)
            pool.memset(onesf[:, :], 1.0).then_inc(const_ok, 1)
            pool.iota(pad_row[:, :], [[1, 1]], base=N_NODES, channel_multiplier=1, **exact).then_inc(const_ok, 1)
            pool.memset(srcf[:, CHUNKS:], -1.0).then_inc(const_ok, 1)
            pool.memset(dstf[:, CHUNKS:], -1.0).then_inc(const_ok, 1)
            pool.memset(ksum[:, :], 0.0).then_inc(const_ok, 1)
            pool.memset(band[:, :], 0.0).then_inc(const_ok, 1)
            pool.wait_ge(const_ok, 16)
            pool.affine_select(out=band[:, :], in_=band[:, :], compare_op=ALU.not_equal, fill=1.0,
                               base=N_NODES - P, pattern=[[-1, N_NODES - P + WIDE + 1]],
                               channel_multiplier=1).then_inc(const_ok, 1)

            def low_part(u, slot):
                pool.wait_ge(w_hi, u + 1)
                pool.tensor_tensor(wslots[:, slot, 1, :], stage[:, u % 2, :], wslots[:, slot, 0, :],
                                   ALU.subtract).then_inc(w_lo, 1)

            def node_low(t, b):
                pool.wait_ge(xn_hi, t + 1)
                pool.sem_inc(passed, 1)
                pool.tensor_tensor(xn[:, 1, t, :], z1[:, b, :], xn[:, 0, t, :], ALU.subtract).then_inc(xn_lo, 1)

            def nodes(i, last=False):
                for b in range(2):
                    t = 2 * i + b
                    if not (last and b == 1):
                        node_low(t + 1, 1 - b)
                    pool.wait_ge(k_act, t + 1)
                    pool.sem_inc(passed, 1)
                    pool.tensor_tensor(kbuf[:, b, :], ekey[:, b, :], kbuf[:, b, :], ALU.add).then_inc(k_done, 1)
                    pool.wait_ge(k_done, t + 1)
                    pool.sem_inc(passed, 1)
                    pool.tensor_tensor(ksum[:, :], ksum[:, :], kbuf[:, b, :], ALU.add).then_inc(ksum_c, 1)
                    if isinstance(i, int) and i < 2 and t >= 1:
                        low_part(*first_units[t + 1])
            node_low(0, 0)
            low_part(*first_units[0])
            low_part(*first_units[1])
            nodes(0)
            nodes(1)
            with pool.Fori(2, T // 2 - 1) as i:
                nodes(i)
            nodes(T // 2 - 1, last=True)

            pool.wait_ge(b2_in, 16)

            def add_att(i):
                for b in range(2):
                    t = 2 * i + b
                    pool.tensor_tensor(x_sb[:, t, :], x_sb[:, t, :], b2b[:, :], ALU.add).then_inc(att_added, 1)
                    pool.wait_ge(att_added, 2 * t + 1)
                    pool.wait_ge(o_done, t + 1)
                    pool.sem_inc(passed, 1)
                    pool.tensor_tensor(x_sb[:, t, :], x_sb[:, t, :], att[:, b, :], ALU.add)\
                        .then_inc(att_added, 1)
            tiles(pool, add_att)

            def ein_low(i):
                for b in range(2):
                    for j in range(2):
                        n = 2 * (2 * i + b) + j
                        pool.wait_ge(ei_hi, n + 1)
                        pool.tensor_tensor(he[:, b, 1, j * 512:(j + 1) * 512], h32[:, j, :],
                                           he[:, b, 0, j * 512:(j + 1) * 512], ALU.subtract).then_inc(ei_lo, 1)
            tiles(pool, ein_low)
            pool.wait_ge(ei_lo, 2 * T)
            pool.iota(iop[:, :], [[1, 128]], base=0, channel_multiplier=0, **exact).then_inc(const2_ok, 1)

            def sin_low(u):
                for m2 in range(2):
                    for c, (at, w) in enumerate(COLS):
                        n = 3 * m2 + c
                        pool.wait_ge(si_hi, 6 * u + n + 1)
                        pool.tensor_tensor(hsl[:, 2 * u + m2, at:at + w], h32_s[:, n % 2, 0:w],
                                           hsh[:, 2 * u + m2, at:at + w], ALU.subtract).then_inc(si_lo, 1)
            with pool.Fori(0, 4) as u:
                sin_low(u)

            pool.wait_ge(si_ps, 24)
            pool.memset(pad0[:, :], 0.0).then_inc(pad_ok, 1)
            pool.wait_ge(hid_out, 16 * T)
            pool.wait_ge(slots_ok, 1)

            def fetch(i, b):
                j = 2 * i + b
                pool.tensor_copy(gcur[:, b:b + 1], gidx[:, bass.ds(j, 1)]).then_inc(idx_ok, 1)
                pool.wait_ge(idx_ok, j + 1)
                pool.sem_inc(passed, 1)
                pool.indirect_dma_start(
                    out=got[:, b, :], out_offset=None, in_=hid_dram[:, :],
                    in_offset=bass.IndirectOffsetOnAxis(ap=gcur[:, b:b + 1], axis=0)).then_inc(got_ok[b], 16)

            def put(i, b):
                j = 2 * i + b
                pool.tensor_copy(scur[:, b:b + 1], sidx[:, bass.ds(j, 1)]).then_inc(idx2_ok, 1)
                pool.wait_ge(idx2_ok, j + 1)
                pool.wait_ge(y_ok, j + 1)
                if later(i, b):
                    pool.wait_ge(added, 16 * j)
                pool.sem_inc(passed, 1)
                pool.indirect_dma_start(
                    out=out[:, :], out_offset=bass.IndirectOffsetOnAxis(ap=scur[:, b:b + 1], axis=0),
                    in_=y[:, b, :], in_offset=None, compute_op=ALU.add).then_inc(added, 16)

            fetch(0, 0)
            fetch(0, 1)
            pool.wait_ge(tr_ps, 1)
            fetch(1, 0)
            pool.wait_ge(acc_out, 16 * T)
            pool.wait_ge(pad_out, 16)

            def step(i, ahead=True):
                for b in range(2):
                    if ahead:
                        pool.wait_ge(tr_ps, 2 * i + b + 2)
                        fetch(i + 1 + b, 1 - b)
                    put(i, b)
            n_pairs = MAX_TILES // 2
            step(0)
            with pool.Fori(1, n_pairs - 1) as i:
                step(i)
            step(n_pairs - 1, ahead=False)
            put(n_pairs, 0)
            pool.wait_ge(added, 16 * MAX_TILES)

        @block.scalar
        def _(act):
            def split_hi(u, slot, half=None):
                half = u % 2 if half is None else half
                act.wait_ge(stage_in, 16 * (u + 1))
                act.activation(wslots[:, slot, 0, :], stage[:, half, :], ACT.Copy, scale=S_W).then_inc(w_hi, 1)

            def scale_and_split_hi(u, slot):
                act.wait_ge(stage_in, 16 * (u + 1))
                act.activation(stage[:, u % 2, :], stage[:, u % 2, :], ACT.Copy, scale=S_W).then_inc(w_scaled, 1)
                act.wait_ge(w_scaled, u + 1)
                act.activation(wslots[:, slot, 0, :], stage[:, u % 2, :], ACT.Copy).then_inc(w_hi, 1)

            act.wait_ge(edge_in, 48)
            act.activation(dstf[:, 0:CHUNKS], dsti[:, :], ACT.Copy).then_inc(edges_f, 1)
            act.activation(srcf[:, 0:CHUNKS], srci[:, :], ACT.Copy).then_inc(edges_f, 1)

            def roots(n, lo, hi):
                act.wait_ge(var_ok, n + 1)
                act.activation(r1[:, 1, lo:hi], r1[:, 0, lo:hi], ACT.Sqrt).then_inc(root_ok, 1)
                act.wait_ge(scale_ok, n + 1)
            roots(0, 0, 2)

            def normal(t, b, reused):
                if reused:
                    act.wait_ge(xn_lo, t - 1)
                act.activation(z1[:, b, :], x_sb[:, t, :], ACT.Identity, scale=r1[:, 6, bass.ds(t, 1)],
                               bias=r1[:, 7, bass.ds(t, 1)]).then_inc(z1_ok, 1)
                act.wait_ge(z1_ok, t + 1)
                act.activation(xn[:, 0, t, :], z1[:, b, :], ACT.Copy).then_inc(xn_hi, 1)

            def values(t, b, reused):
                act.wait_ge(v_ps, t + 1)
                if reused:
                    act.wait_ge(kv_used, t - 1)
                act.activation(vbuf[:, b, :], ps[0:P, 4, :], ACT.Copy,
                               scale=1 / (S_X * S_W * N_NODES)).then_inc(v_done, 1)

            def node_columns(t):
                act.wait_ge(xcol_ps, t + 1)
                act.activation(xnT[:, :, :, bass.ds(t * P, P)],
                               ps[:, 6:8, 0:4 * P].rearrange("p a (k n) -> p a k n", k=KB),
                               ACT.Copy).then_inc(xcol_out, 1)

            def nodes(i, last=False):
                for b in range(2):
                    t = 2 * i + b
                    if not (last and b == 1):
                        normal(t + 1, 1 - b, later(i, b))
                    if later(i, b):
                        values(t - 1, 1 - b, later(i, b, 3))
                    node_columns(t)
                    end = act.value_load(tabs[0:1, bass.ds(t + 1, 1)], min_val=1, max_val=T * (STEPS + 1))
                    act.wait_ge(hot_used, end + RING)
                    if later(i, b):
                        act.wait_ge(a_turned, t)
                    act.activation(a_row[:, 0:WIDE].rearrange("p (c w) -> p c w", c=3),
                                   ps[0:P, 0:3, 0:417], ACT.Copy).then_inc(a_copied, 1)
                    if isinstance(i, int) and t == 0:
                        roots(1, 2, T)
                    act.wait_ge(k_ps, t + 1)
                    if later(i, b, 2):
                        act.wait_ge(ksum_c, t - 1)
                        act.wait_ge(kv_used, t - 1)
                    act.activation(ekey[:, b, :], ps[0:P, 3, :], ACT.Relu,
                                   scale=-1 / (S_X * S_W)).then_inc(k_neg, 1)
                    act.activation(kbuf[:, b, :], ps[0:P, 3, :], ACT.Relu, scale=1 / (S_X * S_W))
                    act.wait_ge(k_neg, t + 1)
                    act.activation(ekey[:, b, :], ekey[:, b, :], ACT.Exp, scale=-1.0).then_inc(k_act, 1)
                    act.wait_ge(a_turned, t + 1)
                    v = ps16[0:P, 6:8, 0:640].rearrange("p a (s c) -> p a s c", c=128)[:, :, :, 0:P]
                    o = adjT[:, :, bass.ds(t * P, P)].rearrange("p (a s) c -> p a s c", a=2)
                    act.activation(o, v, ACT.Copy).then_inc(adj_out, 1)
                    if isinstance(i, int) and i < 2 and t >= 1:
                        scale_and_split_hi(*first_units[t + 1])
            normal(0, 0, False)
            for unit in first_units[:2]:
                scale_and_split_hi(*unit)
            act.wait_ge(small_in, n_small)
            act.activation(bias9[:, 0, :], bias_in[:, :], ACT.Copy, scale=S_W).then_inc(bias_hi, 1)
            act.activation(b1s[:, :], b1[:, :], ACT.Copy, scale=S_G).then_inc(par_ok, 1)
            act.activation(lns[:, :, :], lnp[:, :, :], ACT.Copy, scale=S_F).then_inc(par_ok, 1)
            nodes(0)
            nodes(1)
            with act.Fori(2, T // 2 - 1) as i:
                nodes(i)
            nodes(T // 2 - 1, last=True)
            values(T - 1, 1, True)


            def queries(i):
                for m2 in range(2):
                    for c, (at, w) in enumerate(COLS):
                        n = 3 * m2 + c
                        bank = [0, 1, 2, 3, 6, 7][n]
                        act.wait_ge(q_ps, 6 * i + n + 1)
                        if not isinstance(i, int) or i or n >= 2:
                            act.wait_ge(q_done, 6 * i + n - 1)
                        act.activation(ebuf[:, n % 2, 0:w], ps[:, bank, 0:w], ACT.Relu,
                                       scale=-1 / (S_X * S_W)).then_inc(q_neg, 1)
                        act.activation(qT[:, 2 * i + m2, at:at + w], ps[:, bank, 0:w], ACT.Relu,
                                       scale=1 / (S_X * S_W))
                        act.wait_ge(q_neg, 6 * i + n + 1)
                        act.activation(ebuf[:, n % 2, 0:w], ebuf[:, n % 2, 0:w], ACT.Exp,
                                       scale=-1.0).then_inc(q_act, 1)
            queries(0)
            queries(1)
            act.wait_ge(kv_used, T)
            act.wait_ge(ksum_c, T)
            act.dma_start(b2b[:, :], d["b2"].broadcast_to((P, D))).then_inc(b2_in, 16)

            act.wait_ge(ksum_ps, 1)
            act.wait_ge(bias_lo, 1)

            for m in range(KB):
                act.wait_ge(n_ps, m + 1)
                for c, (at, w) in enumerate(COLS):
                    bank = [4, 5, 6, 7, 0, 1][3 * (m % 2) + c]
                    act.activation(h1T[:, 0, m, at:at + w], ps[:, bank, 0:w], ACT.Copy,
                                   scale=S_G / S_X).then_inc(n_hi, 1)
                split_hi(U_EIN + m, SLOT_EIN + m)
            act.wait_ge(att_added, 2 * T)
            act.wait_ge(o_ps, T)

            act.wait_ge(par_ok, 2)
            for m in range(KB):
                for c, (at, w) in enumerate(COLS):
                    n = 3 * m + c
                    act.wait_ge(f1_ps, n + 1)
                    if n >= 2:
                        act.wait_ge(g_lo, n - 1)
                    act.activation(rbuf[:, n % 2, 0:w], ps[:, 2 + n % 6, 0:w], ACT.Relu,
                                   scale=1 / S_W, bias=b1s[:, m:m + 1])
                    act.activation(r1T[:, 0, m, at:at + w], ps[:, 2 + n % 6, 0:w], ACT.Relu,
                                   scale=1 / S_W, bias=b1s[:, m:m + 1]).then_inc(g_act, 1)
                if m < KB - 1:
                    split_hi(U_SIN + m, SLOT_SIN + m)

            def columns2(t, b, reused):
                act.wait_ge(zt_ps, t + 1)
                if reused:
                    act.wait_ge(gate_ps, t - 1)
                    act.wait_ge(f_lo, t - 1)
                for k in range(KB):
                    ins = act.activation(ft[:, b, k, :], ps[:, 6, k * P:(k + 1) * P], ACT.Identity,
                                         scale=lns[:, 0, k:k + 1], bias=lns[:, 1, k:k + 1])
                ins.then_inc(ft_act, 1)
                act.wait_ge(ft_act, t + 1)
                act.activation(fT[:, 0, :, bass.ds(t * P, P)], ft[:, b, :, :], ACT.Copy).then_inc(f_hi, 1)

            def store_hidden(t, b):
                act.wait_ge(ei_lo, 2 * t + 2)
                act.dma_start(hid_dram[bass.ds(t * P, P), :].rearrange("p (h c) -> p h c", h=2),
                              he[:, b, :, :]).then_inc(hid_out, 16)

            def ein_silu(t, b, j, reused):
                act.wait_ge(ei_ps, 2 * t + j + 1)
                if reused:
                    act.wait_ge(ei_mul, 2 * t + j - 1)
                act.activation(sil[:, j, :], ps[0:P, 2 * j, :], ACT.Silu,
                               scale=1 / (S_F * S_W)).then_inc(ei_sil, 1)

            def ein_high(t, b, j):
                act.wait_ge(ei_mul, 2 * t + j + 1)
                act.activation(he[:, b, 0, j * 512:(j + 1) * 512], h32[:, j, :], ACT.Copy).then_inc(ei_hi, 1)

            def norm2(i):
                for b in range(2):
                    t = 2 * i + b
                    act.wait_ge(ln_ve, t + 1)
                    act.activation(sd[:, b, :], ve[:, b, :], ACT.Sqrt).then_inc(ln_sd, 1)
                    if later(i, b):
                        ein_silu(t - 1, 1 - b, 0, later(i, b, 2))
                        if later(i, b, 3):
                            act.wait_ge(hid_out, 16 * (t - 2))
                        if later(i, b, 2):
                            store_hidden(t - 2, b)
                        ein_high(t - 1, 1 - b, 0)
                    columns2(t, b, later(i, b, 2))
                    if later(i, b):
                        ein_silu(t - 1, 1 - b, 1, later(i, b, 2))
                        ein_high(t - 1, 1 - b, 1)
                    if isinstance(i, int) and t < 3:
                        split_hi(*late_units[t])
            tiles(act, norm2, peeled=2)
            ein_silu(T - 1, 1, 0, True)
            act.wait_ge(hid_out, 16 * (T - 2))
            store_hidden(T - 2, 0)
            ein_high(T - 1, 1, 0)
            ein_silu(T - 1, 1, 1, True)
            ein_high(T - 1, 1, 1)
            store_hidden(T - 1, 1)
            act.wait_ge(hid_out, 16 * T)

            def expert_units(u, n):
                for q in range(n):
                    split_hi(2 * u + (U_EXP + q), 2 * u + q, (U_EXP + q) % 2)

            def sin(u, m2, c):
                at, w = COLS[c]
                n = 3 * m2 + c
                act.wait_ge(si_ps, 6 * u + n + 1)
                if not isinstance(u, int) or u or n >= 2:
                    act.wait_ge(si_mul, 6 * u + n - 1)
                act.activation(sil_s[:, n % 2, 0:w], ps[:, 2 * c, 0:w], ACT.Silu,
                               scale=1 / (S_F * S_W)).then_inc(si_sil, 1)
                act.wait_ge(si_mul, 6 * u + n + 1)
                act.activation(hsh[:, 2 * u + m2, at:at + w], h32_s[:, n % 2, 0:w], ACT.Copy).then_inc(si_hi, 1)

            sin(0, 0, 0)
            act.wait_ge(sel_ok, 1)
            act.activation(rt[:, 2, :, 0:PER_GROUP], rt[:, 1, :, 0:PER_GROUP], ACT.Exp).then_inc(sel_exp, 1)
            sin(0, 0, 1)
            sin(0, 0, 2)
            expert_units(0, 2)
            for c in range(3):
                sin(0, 1, c)
            with act.Fori(1, 3) as u:
                expert_units(u, 2)
                for n in range(6):
                    sin(u, n // 3, n % 3)
            expert_units(3, 1)
            sin(3, 0, 0)
            act.wait_ge(cnt_ps, 1)
            for g, n in ((0, 8), (1, 2)):
                act.activation(cntT[0:EXPERTS, g * 8 * P:(g * 8 + n) * P].rearrange("p (t c) -> p t c", c=P),
                               ps16[0:EXPERTS, 6 + g, 0:n * 128].rearrange("p (t c) -> p t c", c=128)[:, :, 0:P],
                               ACT.Copy, scale=S_H).then_inc(cnt_ok, 1)
            for n in range(1, 6):
                sin(3, n // 3, n % 3)

            act.wait_ge(pad_ok, 1)
            act.dma_start(out[N_NODES:N_NODES + 128, :], pad0[:, :]).then_inc(pad_out, 16)

            for u in range(7, 2 * EXPERTS - LATE):
                split_hi(U_EXP + u, u)

            def sout(i):
                for b in range(2):
                    t = 2 * i + b
                    act.wait_ge(so_done, t + 1)
                    act.dma_start(out[bass.ds(t * P, P), :], acc[:, b, :]).then_inc(acc_out, 16)
            def turned_hi(i, b):
                j = 2 * i + b
                act.wait_ge(tr_ps, j + 1)
                if later(i, b, 2):
                    act.wait_ge(ex_ps, j - 1)
                act.activation(heT[b][:, 0, :, :], ps16[:, 4 + 2 * b, :].rearrange("p (h n) -> p h n", h=HB),
                               ACT.Copy).then_inc(ht_hi, 1)

            sout(0)
            turned_hi(0, 0)
            with act.Fori(1, T // 2) as i:
                sout(i)

            act.wait_ge(acc_out, 16 * T)
            act.wait_ge(slots_ok, 1)

            def weighted(i, b):
                j = 2 * i + b
                act.wait_ge(ex_ps, j + 1)
                if later(i, b, 2):
                    act.wait_ge(added, 16 * (j - 1))
                act.activation(y[:, b, :], ps[:, b, :], ACT.Copy, scale=wsl[:, bass.ds(j, 1)]).then_inc(y_ok, 1)

            def routed(i, units):
                for b in range(2):
                    turned_hi(i, 1) if b == 0 else turned_hi(i + 1, 0)
                    if units:
                        split_hi(2 * i + (U_LATE + b), 2 * i + (SLOT_LATE + b), (U_LATE + b) % 2)
                    weighted(i, b)
            routed(0, True)
            with act.Fori(1, LATE // 2) as i:
                routed(i, True)
            with act.Fori(LATE // 2, MAX_TILES // 2) as i:
                routed(i, False)
            weighted(MAX_TILES // 2, 0)

        @block.vector
        def _(dve):
            steps = [0]

            def link(ins):
                steps[0] += 1
                ins.then_inc(dve_c, 1)
                dve.wait_ge(dve_c, steps[0])

            def split_lo(u, slot, half=None):
                half = u % 2 if half is None else half
                dve.wait_ge(w_hi, u + 1)
                dve.scalar_tensor_tensor(out=wslots[:, slot, 1, :], in0=stage[:, half, :], scalar=S_W,
                                         in1=wslots[:, slot, 0, :], op0=ALU.mult, op1=ALU.subtract)\
                   .then_inc(w_lo, 1)

            def stats(n, b, src, scale, add):
                dve.sem_inc(passed, 1)
                dve.bn_stats(st6[:, b, :], src).then_inc(ln_bn, 1)
                dve.wait_ge(ln_bn, n + 1)
                dve.sem_inc(passed, 1)
                dve.bn_aggr(mv[:, b, :], st6[:, b, :]).then_inc(ln_mv, 1)
                dve.wait_ge(ln_mv, n + 1)
                dve.tensor_scalar(ve[:, b, :], mv[:, b, 1:2], scale, add, ALU.mult, ALU.add).then_inc(ln_ve, 1)

            def normalise(n, b, src, dst, scale):
                dve.wait_ge(ln_sd, n + 1)
                dve.reciprocal(rst[:, b, 0:1], sd[:, b, :]).then_inc(ln_r, 1)
                dve.wait_ge(ln_r, 4 * n + 1)
                dve.tensor_scalar(rst[:, b, 1:2], ve[:, b, :], rst[:, b, 0:1], rst[:, b, 0:1],
                                  ALU.mult, ALU.mult).then_inc(ln_r, 1)
                dve.wait_ge(ln_r, 4 * n + 2)
                dve.tensor_scalar(rst[:, b, 2:3], rst[:, b, 1:2], -0.5, 1.5, ALU.mult, ALU.add).then_inc(ln_r, 1)
                dve.wait_ge(ln_r, 4 * n + 3)
                dve.tensor_scalar(rst[:, b, 3:4], rst[:, b, 2:3], rst[:, b, 0:1], scale,
                                  ALU.mult, ALU.mult).then_inc(ln_r, 1)
                dve.wait_ge(ln_r, 4 * n + 4)
                dve.tensor_scalar(dst, src, mv[:, b, 0:1], rst[:, b, 3:4],
                                  ALU.subtract, ALU.mult).then_inc(z_ok, 1)

            by_tile = "p (t o) -> p t o"

            def variances(lo, hi):
                for t in range(lo, hi):
                    ins = dve.bn_stats(st1[:, t, :], x_sb[:, t, :])
                link(ins)
                for t in range(lo, hi):
                    ins = dve.bn_aggr(mv1[:, t, :], st1[:, t, :])
                link(ins)
                dve.tensor_scalar(r1[:, 0, lo:hi].rearrange(by_tile, o=1), mv1[:, lo:hi, 1:2], LN_EPS, None, ALU.add)\
                   .then_inc(var_ok, 1)

            def scales(n, lo, hi):
                var, root, inv1, tmp, fix, inv2, rs, shift = (r1[:, k, lo:hi] for k in range(8))
                dve.wait_ge(root_ok, n + 1)
                link(dve.reciprocal(inv1, root))
                link(dve.tensor_tensor(tmp, inv1, inv1, ALU.mult))
                link(dve.tensor_tensor(fix, tmp, var, ALU.mult))
                link(dve.tensor_scalar(inv2, fix, -0.5 * S_X, 1.5 * S_X, ALU.mult, ALU.add))
                link(dve.tensor_tensor(rs, inv2, inv1, ALU.mult))
                dve.scalar_tensor_tensor(out=shift.rearrange(by_tile, o=1), in0=mv1[:, lo:hi, 0:1], scalar=-1.0,
                                         in1=rs.rearrange(by_tile, o=1), op0=ALU.mult, op1=ALU.mult)\
                   .then_inc(scale_ok, 1)

            dve.wait_ge(edge_in, 48)
            dve.tensor_reduce(mnmx[:, 0:2], dst2[:, :, :], AX.X, ALU.max)
            link(dve.tensor_reduce(mnmx[:, 2:4], dst2[:, :, :], AX.X, ALU.min))
            dve.wait_ge(const_ok, 14)
            for q in range(4):
                ins = dve.tensor_scalar(diag[:, q, :], ident[0:HALF, 0:HALF], mnmx[:, q:q + 1], None, ALU.mult)
            ins.then_inc(diag_ok, 1)
            dve.wait_ge(x0_in, 32)
            variances(0, 2)
            dve.wait_ge(rows_ps, 1)
            link(dve.tensor_scalar(rngf[:, 0, :], ps[0:T, 6, 0:CHUNKS], tlo[:, 0:1], None, ALU.is_ge))
            link(dve.scalar_tensor_tensor(out=rngf[:, 1, :], in0=ps[0:T, 6, CHUNKS:2 * CHUNKS], scalar=tlo[:, 1:2],
                                          in1=rngf[:, 0, :], op0=ALU.is_lt, op1=ALU.mult))
            link(dve.tensor_tensor(rngf[:, 2:4, :], rngf[:, 1:2, :].broadcast_to((T, 2, CHUNKS)), cup[:, :, :],
                                   ALU.mult))
            link(dve.tensor_reduce(rsm[:, 0:2], rngf[:, 2:4, :], AX.X, ALU.max))
            link(dve.tensor_scalar(rsm[:, 2:3], rsm[:, 0:1], 1.0, None, ALU.max))
            link(dve.tensor_scalar(rsm[:, 3:4], rsm[:, 2:3], -1.0, None, ALU.add))
            link(dve.tensor_scalar(rsm[:, 4:5], rsm[:, 1:2], -1.0, float(CHUNKS), ALU.mult, ALU.add))
            link(dve.tensor_tensor(rsm[:, 5:6], rsm[:, 4:5], rsm[:, 3:4], ALU.min))
            link(dve.tensor_tensor(rsm[:, 6:7], rsm[:, 2:3], rsm[:, 5:6], ALU.subtract))
            link(dve.tensor_scalar(rngf[:, 0, 0:STEPS], step_at[:, :], rsm[:, 6:7], None, ALU.is_lt, ALU.add,
                                   accum_out=rsm[:, 7:8]))
            dve.tensor_copy(rs16[:, 0:1], rsm[:, 5:6])
            dve.tensor_copy(rs16[:, 1:2], rsm[:, 7:8]).then_inc(range_ok, 1)
            scales(0, 0, 2)
            dve.wait_ge(tab_ps, 1)
            link(dve.tensor_copy(tabf[0:1, 0:T + 1], ps[0:1, 7, 0:T + 1]))
            link(dve.scalar_tensor_tensor(out=tabf[0:1, 16:16 + T], in0=tabf[0:1, 0:T], scalar=float(-GROUP),
                                          in1=ps[0:1, 7, 16:16 + T], op0=ALU.mult, op1=ALU.add))
            dve.tensor_scalar(tabs[0:1, 16:16 + T], tabf[0:1, 16:16 + T], float(CO_SHIFT), None, ALU.add)
            link(dve.tensor_copy(tabs[0:1, 0:T + 1], tabf[0:1, 0:T + 1]))
            dve.nop().then_inc(tab_ok, 1)

            dve.wait_ge(edges_f, 2)

            def tile_edges(t):
                first = dve.value_load(tabs[0:1, bass.ds(t, 1)], min_val=0, max_val=T * (STEPS + 1))
                end = dve.value_load(tabs[0:1, bass.ds(t + 1, 1)], min_val=1, max_val=T * (STEPS + 1))
                off = dve.value_load(tabs[0:1, bass.ds(16 + t, 1)], min_val=0, max_val=2 * CO_SHIFT)
                with dve.Fori(first, end) as v:
                    dve.wait_ge(hot_used, v + 1)
                    chunk0 = nc.s_assert_within(v * GROUP + off - CO_SHIFT, 0, CHUNKS,
                                              skip_runtime_bounds_check_because=IN_RANGE)
                    for q in range(GROUP):
                        chunk = chunk0 + q
                        place = (v % RING) * GROUP + q
                        dve.tensor_scalar(hot_src[:, place, 0:WIDE], iota[:, 0:WIDE],
                                          srcf[:, bass.ds(chunk, 1)], None, ALU.is_equal)
                        ins = dve.tensor_scalar(hot_dst[:, place, 0:P], iota[:, bass.ds(t * P, P)],
                                                dstf[:, bass.ds(chunk, 1)], None, ALU.is_equal)
                    ins.then_inc(hot_ready, 1)

            tile_edges(0)
            dve.wait_ge(x_in, 32)
            variances(2, T)
            scales(1, 2, T)
            tile_edges(1)
            with dve.Fori(1, T // 2) as i:
                for b in range(2):
                    tile_edges(2 * i + b)
            dve.wait_ge(bias_hi, 1)
            dve.scalar_tensor_tensor(out=bias9[:, 1, :], in0=bias_in[:, :], scalar=S_W, in1=bias9[:, 0, :],
                                     op0=ALU.mult, op1=ALU.subtract).then_inc(bias_lo, 1)

            dve.wait_ge(ksum_ps, 1)
            dve.wait_ge(ksum_c, T)
            link(dve.memset(kvd[:, :, :], 0.0))
            for h, lo in ((0, 0), (1, 64)):
                rows = slice(lo, lo + 64)
                dve.tensor_scalar(kvd[rows, :, lo:lo + 64],
                                  ps[rows, 5, :].rearrange("p (a c) -> p a c", a=KB)[:, :, lo:lo + 64],
                                  float(N_NODES), None, ALU.mult)
                ins = dve.tensor_copy(kvd[rows, :, 128 + h:129 + h],
                                      ps[rows, 4, 0:8].rearrange("p (a c) -> p a c", a=KB)[:, :, 0:1])
            ins.then_inc(kvd_ok, 1)
            def queries(i):
                for m2 in range(2):
                    for c, (at, w) in enumerate(COLS):
                        n = 3 * m2 + c
                        dve.wait_ge(q_act, 6 * i + n + 1)
                        o = qT[:, 2 * i + m2, at:at + w]
                        dve.tensor_tensor(o, ebuf[:, n % 2, 0:w], o, ALU.add).then_inc(q_done, 1)
            queries(0)
            queries(1)

            dve.wait_ge(q_done, 12)

            def attend(i):
                for b in range(2):
                    t = 2 * i + b
                    dve.wait_ge(o_ps, t + 1)
                    banks = ps[0:P, 2 * b:2 * b + 2, 0:260].rearrange("p a (q c) -> p a q c", q=2)
                    dve.tensor_scalar(den[:, b, 0, :].rearrange("p (a q h) -> p a q h", a=2, q=2),
                                      banks[:, :, :, 128:130], ATT_EPS, None, ALU.add).then_inc(den_c, 1)
                    dve.wait_ge(den_c, 2 * t + 1)
                    dve.reciprocal(den[:, b, 1, :], den[:, b, 0, :]).then_inc(den_c, 1)
                    dve.wait_ge(den_c, 2 * t + 2)
                    if later(i, b, 2):
                        dve.wait_ge(att_added, 2 * t - 2)
                    for g in range(2):
                        o = att[:, b, 256 * g:256 * g + 256].rearrange("p (q h c) -> p q h c", q=2, h=2)
                        s = ps[0:P, 2 * b + g, 0:260].rearrange("p (q c) -> p q c", q=2)[:, :, 0:128]\
                            .rearrange("p q (h c) -> p q h c", h=2)
                        z = den[:, b, 1, 4 * g:4 * g + 4].rearrange("p (q h c) -> p q h c", q=2, c=1)\
                            .broadcast_to((P, 2, 2, 64))
                        ins = dve.tensor_tensor(o, s, z, ALU.mult)
                    ins.then_inc(o_done, 1)
            tiles(dve, attend)

            for m in range(KB):
                for c, (at, w) in enumerate(COLS):
                    bank = [4, 5, 6, 7, 0, 1][3 * (m % 2) + c]
                    dve.wait_ge(n_hi, 3 * m + c + 1)
                    dve.scalar_tensor_tensor(out=h1T[:, 1, m, at:at + w], in0=ps[:, bank, 0:w], scalar=S_G / S_X,
                                             in1=h1T[:, 0, m, at:at + w], op0=ALU.mult, op1=ALU.subtract)\
                       .then_inc(n_lo, 1)
                split_lo(U_EIN + m, SLOT_EIN + m)

            for m in range(KB):
                for c, (at, w) in enumerate(COLS):
                    n = 3 * m + c
                    dve.wait_ge(g_act, n + 1)
                    dve.tensor_tensor(r1T[:, 1, m, at:at + w], rbuf[:, n % 2, 0:w], r1T[:, 0, m, at:at + w],
                                      ALU.subtract).then_inc(g_lo, 1)
                if m < KB - 1:
                    split_lo(U_SIN + m, SLOT_SIN + m)

            dve.wait_ge(att_added, 2 * T)
            dve.wait_ge(f1_ps, 12)
            dve.tensor_copy(identf[:, :], ident[:, :]).then_inc(identf_ok, 1)

            def ein_product(t, b, j, reused):
                dve.wait_ge(ei_sil, 2 * t + j + 1)
                if reused:
                    dve.wait_ge(ei_lo, 2 * t + j - 1)
                dve.scalar_tensor_tensor(out=h32[:, j, :], in0=ps[0:P, 2 * j + 1, :],
                                         scalar=S_H / (S_F * S_W), in1=sil[:, j, :],
                                         op0=ALU.mult, op1=ALU.mult).then_inc(ei_mul, 1)

            def logits(t):
                dve.wait_ge(gate_ps, t + 1)
                dve.scalar_tensor_tensor(out=lg[:, t, :], in0=ps[0:P, 7, 0:GATES], scalar=1 / S_F,
                                         in1=gb[:, :], op0=ALU.mult, op1=ALU.add).then_inc(lg_done, 1)

            def norm2(i):
                for b in range(2):
                    t = 2 * i + b
                    dve.wait_ge(w2_ps, t + 1)
                    dve.scalar_tensor_tensor(out=x_sb[:, t, :], in0=ps[0:P, 4 + b, :], scalar=1 / (S_G * S_W),
                                             in1=x_sb[:, t, :], op0=ALU.mult, op1=ALU.add).then_inc(x1_done, 1)
                    dve.wait_ge(x1_done, t + 1)
                    stats(t, b, x_sb[:, t, :], 1.0 + LN_EPS, LN_EPS * LN_EPS)
                    if later(i, b):
                        logits(t - 1)
                    if later(i, b, 2):
                        dve.wait_ge(zt_ps, t - 1)
                    normalise(t, b, x_sb[:, t, :], z2[:, b, :], 1.0)
                    if later(i, b):
                        ein_product(t - 1, 1 - b, 0, later(i, b, 2))
                    dve.wait_ge(f_hi, t + 1)
                    dve.tensor_tensor(fT[:, 1, :, bass.ds(t * P, P)], ft[:, b, :, :],
                                      fT[:, 0, :, bass.ds(t * P, P)], ALU.subtract).then_inc(f_lo, 1)
                    if later(i, b):
                        ein_product(t - 1, 1 - b, 1, later(i, b, 2))
                    if isinstance(i, int) and t < 3:
                        split_lo(*late_units[t])
            tiles(dve, norm2, peeled=2)
            logits(T - 1)
            for j in range(2):
                ein_product(T - 1, 1, j, True)

            def plane(k, n=EXPERTS):
                return rt[:, k, :, 0:n]

            def wide(ap, n):
                return ap.broadcast_to((P, T, n))

            pg = PER_GROUP
            in1st, in2nd, best = rt[:, 0, :, 0:1], rt[:, 0, :, 1:2], rt[:, 0, :, 2:3]
            second, total, inv = rt[:, 0, :, 3:4], rt[:, 0, :, 4:5], rt[:, 0, :, 5:6]
            c1, c2 = rt[:, 0, :, 6:7], rt[:, 0, :, 7:8]
            rank4 = rt[:, 5, 0:1, 0:pg].broadcast_to((P, T, pg))
            slot_f, j_f, p_f, lo_f = tk[:, 0, :], tk[:, 1, :], tk[:, 2, :], tk[:, 3, :]

            def choose(probs, value, hot):
                link(dve.tensor_reduce(value, probs, AX.X, ALU.max))
                link(dve.tensor_tensor(hot, probs, wide(value, pg), ALU.is_equal))
                link(dve.tensor_tensor(hot, hot, rank4, ALU.mult))
                link(dve.tensor_reduce(total, hot, AX.X, ALU.max))
                link(dve.tensor_tensor(hot, hot, wide(total, pg), ALU.is_equal))

            def choose_group():
                dve.wait_ge(const2_ok, 1)
                dve.wait_ge(lg_done, T)
                dve.wait_ge(ei_mul, 2 * T)
                dve.wait_ge(w2_ps, T)
                link(dve.tensor_tensor(in2nd, lg[:, :, 1:2], lg[:, :, 0:1], ALU.is_gt))
                link(dve.tensor_scalar(in1st, in2nd, -1.0, 1.0, ALU.mult, ALU.add))
                link(dve.tensor_tensor(plane(3, pg), lg[:, :, 2:2 + pg], wide(in1st, pg), ALU.mult))
                link(dve.tensor_tensor(plane(4, pg), lg[:, :, 2 + pg:2 + 2 * pg], wide(in2nd, pg), ALU.mult))
                link(dve.tensor_tensor(plane(3, pg), plane(3, pg), plane(4, pg), ALU.add))
                link(dve.tensor_reduce(best, plane(3, pg), AX.X, ALU.max))
                dve.tensor_tensor(plane(1, pg), plane(3, pg), wide(best, pg), ALU.subtract).then_inc(sel_ok, 1)

            def choose_experts():
                link(dve.tensor_scalar(rt[:, 5, 0, 0:pg], iop[0:P, 0:pg], -1.0, float(pg), ALU.mult, ALU.add))
                dve.wait_ge(sel_exp, 1)
                link(dve.tensor_reduce(total, plane(2, pg), AX.X, ALU.add))
                link(dve.reciprocal(inv, total))
                link(dve.tensor_tensor(plane(2, pg), plane(2, pg), wide(inv, pg), ALU.mult))
                choose(plane(2, pg), best, plane(3, pg))
                link(dve.scalar_tensor_tensor(out=plane(6, pg), in0=plane(3, pg), scalar=-2.0, in1=plane(2, pg),
                                              op0=ALU.mult, op1=ALU.add))
                choose(plane(6, pg), second, plane(4, pg))
                link(dve.tensor_tensor(total, best, second, ALU.add))
                link(dve.tensor_scalar(total, total, 1e-8, None, ALU.add))
                link(dve.reciprocal(inv, total))
                link(dve.tensor_tensor(c1, best, inv, ALU.mult))
                link(dve.tensor_tensor(c2, second, inv, ALU.mult))
                for k in range(2):
                    dve.tensor_tensor(oh8[:, k, :, 0:pg], plane(3 + k, pg), wide(in1st, pg), ALU.mult)
                    link(dve.tensor_tensor(oh8[:, k, :, pg:], plane(3 + k, pg), wide(in2nd, pg), ALU.mult))
                link(dve.tensor_tensor(mask16[:, :, :], oh8[:, 0, :, :], oh8[:, 1, :, :], ALU.add))

            def count_choices():
                link(dve.memset(before[:, 0, :], 0.0))
                for t in range(T):
                    link(dve.tensor_tensor(before[:, t + 1, :], before[:, t, :], mask16[:, t, :], ALU.add))
                dve.nop().then_inc(rank_in, 1)
                dve.memset(cntT[:, :], S_H)
                link(dve.tensor_scalar(thr[:, :], iop[0:P, 0:JW + 1], 128.0, None, ALU.mult))
                dve.nop().then_inc(const2_ok, 1)

            def place_choices():
                dve.wait_ge(rank_ps, 1)
                taken = rt[:, 7, :, :].rearrange("p t e -> p (t e)").rearrange("p (e k) -> p e k", e=EXPERTS)
                link(dve.tensor_tensor(
                    taken, ps[0:P, 6, 128:136].rearrange("p (e k) -> p e k", k=1).broadcast_to((P, EXPERTS, T)),
                    thr[:, 0:T].rearrange("p (e k) -> p e k", e=1).broadcast_to((P, EXPERTS, T)), ALU.is_gt))
                n_e, incl, start_e, ones8 = rt[:, 8, 0, :], rt[:, 8, 1, :], rt[:, 8, 2, :], rt[:, 8, 3, :]
                link(dve.tensor_reduce(n_e, taken, AX.X, ALU.add))
                link(dve.tensor_scalar(n_e, n_e, 1.0, None, ALU.max))
                link(dve.memset(ones8, 1.0))
                link(dve.tensor_tensor_scan(incl, ones8, n_e, 0.0, ALU.mult, ALU.add))
                link(dve.tensor_tensor(start_e, incl, n_e, ALU.subtract))
                eids = rt[0:1, 10:12, :, :].rearrange("p a t e -> p (a t e)")
                hits = ge16[0:1, 0:8, :].rearrange("p a b -> p (a b)")[:, 0:JW * (EXPERTS - 1)]\
                    .rearrange("p (j e) -> p j e", j=JW)
                link(dve.tensor_tensor(
                    hits, rt[0:1, 8, 2:3, 1:EXPERTS].broadcast_to((1, JW, EXPERTS - 1)),
                    iop[0:1, 0:JW].rearrange("p (j e) -> p j e", e=1).broadcast_to((1, JW, EXPERTS - 1)), ALU.is_le))
                link(dve.tensor_reduce(eids[:, 0:JW], hits, AX.X, ALU.add))
                dve.tensor_copy(eidt[:, :], eids[:, 0:JW]).then_inc(eid_ok, 1)
                link(dve.tensor_scalar(rt[:, 8, 4, :], start_e, 128.0, None, ALU.mult))
                link(dve.tensor_tensor(plane(6), ps[0:P, 6, 0:T * EXPERTS].rearrange("p (t e) -> p t e", t=T),
                                       rt[:, 8, 4:5, :].broadcast_to((P, T, EXPERTS)), ALU.add))
                for k in range(2):
                    link(dve.tensor_tensor(plane(7), oh8[:, k, :, :], plane(6), ALU.mult))
                    link(dve.tensor_reduce(slot_f[:, k * T:(k + 1) * T], plane(7), AX.X, ALU.add))

            def slot_rows():
                link(dve.tensor_tensor(ge16[:, :, :],
                                       slot_f.rearrange("p (n j) -> p n j", j=1).broadcast_to((P, 2 * T, JW + 1)),
                                       thr[:, :].rearrange("p (n j) -> p n j", n=1).broadcast_to((P, 2 * T, JW + 1)),
                                       ALU.is_ge))
                link(dve.tensor_reduce(j_f, ge16[:, :, 1:], AX.X, ALU.add))
                link(dve.scalar_tensor_tensor(out=p_f, in0=j_f, scalar=-128.0, in1=slot_f, op0=ALU.mult, op1=ALU.add))
                dve.tensor_tensor(hot_p[:, :, :],
                                  iop[0:P, :].rearrange("p (n j) -> p n j", n=1).broadcast_to((P, 2 * T, 128)),
                                  p_f.rearrange("p (n j) -> p n j", j=1).broadcast_to((P, 2 * T, 128)), ALU.is_equal)

            def slot_columns():
                link(dve.tensor_tensor(hot_j[:, :, 3, :], ge16[:, :, 0:JW], ge16[:, :, 1:], ALU.subtract))
                link(dve.tensor_copy(tk[:, 4, 0:T].rearrange("p (t o) -> p t o", o=1), c1))
                link(dve.tensor_copy(tk[:, 4, T:2 * T].rearrange("p (t o) -> p t o", o=1), c2))
                link(dve.tensor_copy(c16[:, :], tk[:, 4, :]))
                link(dve.tensor_tensor(lo_f, tk[:, 4, :], c16[:, :], ALU.subtract))

                def spread(ap):
                    return ap.rearrange("p (n j) -> p n j", j=1).broadcast_to((P, 2 * T, JW))
                for k in range(2):
                    half = slice(k * T, (k + 1) * T)
                    dve.tensor_tensor(hot_j[:, half, 0, :], hot_j[:, half, 3, :],
                                      node_id[:, :].rearrange("p (n j) -> p n j", j=1).broadcast_to((P, T, JW)), ALU.mult)
                dve.tensor_tensor(hot_j[:, :, 1, :], hot_j[:, :, 3, :], spread(c16[:, :]), ALU.mult)
                dve.tensor_tensor(hot_j[:, :, 2, :], hot_j[:, :, 3, :], spread(lo_f), ALU.mult).then_inc(hots_ok, 1)

            def slot_tables():
                dve.wait_ge(slot_ps, 1)
                node_s, whi_s, wlo_s, full_s = (ps[:, 7, JW * k:JW * (k + 1)] for k in range(4))
                dve.tensor_copy(gidx[:, :], node_s)
                link(dve.tensor_scalar(wsl[:, :], wlo_s, 1 / (S_H * S_W), None, ALU.mult))
                link(dve.scalar_tensor_tensor(out=wsl[:, :], in0=whi_s, scalar=1 / (S_H * S_W), in1=wsl[:, :],
                                              op0=ALU.mult, op1=ALU.add))
                link(dve.tensor_scalar(padw[:, 0:JW], full_s, -1.0, 1.0, ALU.mult, ALU.add))
                dve.scalar_tensor_tensor(out=sidx[:, :], in0=padw[:, 0:JW], scalar=pad_row[:, :], in1=node_s,
                                         op0=ALU.mult, op1=ALU.add).then_inc(slots_ok, 1)

            def expert_units(u, n):
                for q in range(n):
                    split_lo(2 * u + (U_EXP + q), 2 * u + q, (U_EXP + q) % 2)

            def sin(u, m2, c):
                at, w = COLS[c]
                n = 3 * m2 + c
                dve.wait_ge(si_sil, 6 * u + n + 1)
                if not isinstance(u, int) or u or n >= 2:
                    dve.wait_ge(si_lo, 6 * u + n - 1)
                dve.scalar_tensor_tensor(out=h32_s[:, n % 2, 0:w], in0=ps[:, 2 * c + 1, 0:w],
                                         scalar=S_H / (S_F * S_W), in1=sil_s[:, n % 2, 0:w],
                                         op0=ALU.mult, op1=ALU.mult).then_inc(si_mul, 1)

            sin(0, 0, 0)
            choose_group()
            sin(0, 0, 1)
            choose_experts()
            sin(0, 0, 2)
            expert_units(0, 2)
            sin(0, 1, 0)
            count_choices()
            sin(0, 1, 1)
            sin(0, 1, 2)
            expert_units(1, 2)
            sin(1, 0, 0)
            place_choices()
            sin(1, 0, 1)
            slot_rows()
            sin(1, 0, 2)
            slot_columns()
            for c in range(3):
                sin(1, 1, c)
            expert_units(2, 2)
            sin(2, 0, 0)
            slot_tables()
            for n in range(1, 6):
                sin(2, n // 3, n % 3)
            expert_units(3, 1)
            for n in range(6):
                sin(3, n // 3, n % 3)
            for u in range(7, 2 * EXPERTS - LATE):
                split_lo(U_EXP + u, u)

            dve.wait_ge(si_lo, 24)

            def sout(i):
                for b in range(2):
                    t = 2 * i + b
                    dve.wait_ge(so_ps, t + 1)
                    if later(i, b):
                        dve.wait_ge(acc_out, 16 * t)
                    dve.scalar_tensor_tensor(out=acc[:, b, :], in0=ps[0:P, 6 + b, :], scalar=1 / (S_H * S_W),
                                             in1=x_sb[:, t, :], op0=ALU.mult, op1=ALU.add).then_inc(so_done, 1)
            def turned_lo(i, b):
                j = 2 * i + b
                dve.wait_ge(tr_ps, j + 1)
                if later(i, b, 2):
                    dve.wait_ge(ex_ps, j - 1)
                dve.tensor_copy(heT[b][:, 1, :, :], ps16[:, 5 + 2 * b, :].rearrange("p (h n) -> p h n", h=HB))\
                   .then_inc(ht_lo, 1)

            sout(0)
            turned_lo(0, 0)
            with dve.Fori(1, T // 2) as i:
                sout(i)

            def routed(i, units):
                for b in range(2):
                    turned_lo(i, 1) if b == 0 else turned_lo(i + 1, 0)
                    if units:
                        split_lo(2 * i + (U_LATE + b), 2 * i + (SLOT_LATE + b), (U_LATE + b) % 2)
            routed(0, True)
            with dve.Fori(1, LATE // 2) as i:
                routed(i, True)
            with dve.Fori(LATE // 2, MAX_TILES // 2) as i:
                routed(i, False)

        @block.tensor
        def _(pe):
            def product(out_ap, left, right, blocks, start=True, stop=True, before_last=None):
                for k in range(blocks):
                    if before_last and k == blocks - 1:
                        pe.wait_ge(*before_last)
                    for lh, rh in ((0, 0), (0, 1), (1, 0)):
                        ins = pe.matmul(out_ap, left(lh, k), right(rh, k), start=start and k + lh + rh == 0,
                                        stop=stop and k == blocks - 1 and lh == 1)
                return ins

            def weight(slot, h, k, at=0, n=512):
                return wslots[:, slot, h, k * 512 + at:k * 512 + at + n] if isinstance(at, int) else \
                    wslots[:, slot, h, bass.ds(at + k * 512, n)]

            pe.wait_ge(diag_ok, 1)
            pe.matmul(ps[0:T, 6, 0:4 * HALF], ones[0:HALF, 0:T], diag[:, :, :], start=True, stop=True)\
              .then_inc(rows_ps, 1)
            pe.wait_ge(range_ok, 1)
            pe.matmul(ps[0:1, 7, 0:T + 1], rs16[:, 1:2], tri[0:T, 0:T + 1], start=True, stop=True)
            pe.matmul(ps[0:1, 7, 16:16 + T], rs16[:, 0:1], ident[0:T, 0:T], start=True, stop=True)\
              .then_inc(tab_ps, 1)
            pe.wait_ge(tab_ok, 1)

            def state(t, b, first):
                pe.wait_ge(k_done, t + 1)
                pe.wait_ge(v_done, t + 1)
                for a in range(KB):
                    ins = pe.matmul(ps[:, 5, a * 128:(a + 1) * 128], kbuf[:, b, a * 128:(a + 1) * 128],
                                    vbuf[:, b, a * 128:(a + 1) * 128], start=first and a == 0, stop=True,
                                    skip_group_check=True)
                ins.then_inc(kv_used, 1)

            def node_columns(t, first=False):
                pe.wait_ge(xn_lo, t + 1)
                if not first:
                    pe.wait_ge(adj_out, t)
                for h in range(2):
                    for k in range(KB):
                        ins = pe.matmul(ps[:, 6 + h, k * P:(k + 1) * P], xn[:, h, t, k * 128:(k + 1) * 128],
                                        ident[0:P, 0:P], start=True, stop=True)
                ins.then_inc(xcol_ps, 1)

            def values(t):
                if isinstance(t, int) and t == 0:
                    pe.wait_ge(w_lo, U_WV + 1)
                else:
                    pe.wait_ge(v_done, t)
                product(ps[0:P, 4, :], lambda h, k: xnT[:, h, k, bass.ds(t * P, P)],
                        lambda h, k: weight(SLOT_WV, h, k), KB).then_inc(v_ps, 1)

            def nodes(i):
                for b in range(2):
                    t = 2 * i + b
                    first = pe.value_load(tabs[0:1, bass.ds(t, 1)], min_val=0, max_val=T * (STEPS + 1))
                    end = pe.value_load(tabs[0:1, bass.ds(t + 1, 1)], min_val=1, max_val=T * (STEPS + 1))
                    if later(i, b):
                        values(t - 1)
                    if later(i, b, 2):
                        state(t - 2, b, isinstance(i, int) and t == 2)
                    node_columns(t, not later(i, b))
                    if later(i, b):
                        pe.wait_ge(a_copied, t)
                    for c in range(3):
                        at = N_NODES - P + c * 417
                        pe.matmul(ps[0:P, c, 0:417], ident[0:P, 0:P], band[:, bass.ds(at - t * P, 417)],
                                  start=True, stop=True)
                    with pe.Fori(first, end) as v:
                        pe.wait_ge(hot_ready, v + 1)
                        for q in range(GROUP):
                            place = (v % RING) * GROUP + q
                            for c in range(3):
                                ins = pe.matmul(ps[0:P, c, 0:417], hot_dst[:, place, 0:P],
                                                hot_src[:, place, c * 417:(c + 1) * 417], start=False, stop=True,
                                                skip_group_check=True)
                        ins.then_inc(hot_used, 1)
                    pe.wait_ge(xcol_out, t + 1)
                    if later(i, b):
                        pe.wait_ge(k_act, t)
                    else:
                        pe.wait_ge(w_lo, U_WK + 1)
                    product(ps[0:P, 3, :], lambda h, k: xnT[:, h, k, bass.ds(t * P, P)],
                            lambda h, k: weight(SLOT_WK, h, k), KB).then_inc(k_ps, 1)
                    pe.wait_ge(a_copied, t + 1)
                    for s in range(T):
                        ins = pe.transpose(ps16[0:P, 6 + s // 5, (s % 5) * 128:(s % 5) * 128 + P],
                                           a_row[:, s * P:(s + 1) * P], ident[0:P, 0:P])
                    ins.then_inc(a_turned, 1)
            pe.wait_ge(const_ok, 17)
            pe.sem_inc(hot_used, RING)
            tiles(pe, nodes, peeled=2)
            values(T - 1)
            state(T - 2, 0, False)
            state(T - 1, 1, False)
            pe.wait_ge(ksum_c, T)
            for a in range(KB):
                ins = pe.matmul(ps[:, 4, 2 * a:2 * a + 2], ksum[:, a * 128:(a + 1) * 128], onesf[0:P, :],
                                start=True, stop=True)
            ins.then_inc(ksum_ps, 1)
            pe.wait_ge(adj_out, T)

            pe.wait_ge(k_act, T)
            pe.wait_ge(v_done, T)
            pe.wait_ge(w_lo, U_WQ + 1)
            for m in range(KB):
                for c, (at, w) in enumerate(COLS):
                    n = 3 * m + c
                    if n >= 6:
                        pe.wait_ge(q_act, n - 5)
                    product(ps[:, [0, 1, 2, 3, 6, 7][n % 6], 0:w],
                            lambda h, k: weight(SLOT_WQ, h, k, m * 128, 128),
                            lambda h, k: xnT[:, h, k, at:at + w], KB).then_inc(q_ps, 1)

            def attend(t):
                if t >= 2:
                    pe.wait_ge(o_done, t - 1)
                for a in range(KB):
                    ins = pe.matmul(ps[0:P, 2 * (t % 2) + a // 2, (a % 2) * 130:(a % 2) * 130 + 130],
                                    qT[:, a, t * P:(t + 1) * P], kvd[:, a, :], start=True, stop=True)
                ins.then_inc(o_ps, 1)

            pe.wait_ge(kvd_ok, 1)
            pe.wait_ge(q_act, 11)
            for m in range(KB):
                banks = [4, 5, 6, 7, 0, 1][3 * (m % 2):3 * (m % 2) + 3]
                if m == 1:
                    pe.wait_ge(o_done, T - 1)
                    pe.wait_ge(q_act, 12)
                if m >= 2:
                    pe.wait_ge(n_lo, 3 * (m - 1))
                for s in range(T):
                    for h in range(2):
                        for c, (at, w) in enumerate(COLS):
                            ins = pe.matmul(ps[:, banks[c], 0:w], xn[:, h, s, m * 128:(m + 1) * 128],
                                            adjT[:, s, at:at + w], start=s + h == 0, stop=s == T - 1 and h == 1)
                    if m == 0:
                        if s == 2:
                            pe.wait_ge(q_done, 12)
                        if 2 <= s < T - 1:
                            attend(s - 2)
                ins.then_inc(n_ps, 1)
                if m == 0:
                    for t in range(T - 3, T):
                        attend(t)

            pe.wait_ge(n_lo, 9)
            pe.wait_ge(w_lo, U_W2 + 1)
            for m in range(KB):
                for c, (at, w) in enumerate(COLS):
                    n = 3 * m + c
                    if n >= 6:
                        pe.wait_ge(g_act, n - 5)
                    product(ps[:, 2 + n % 6, 0:w], lambda h, k: weight(SLOT_W1, h, k, m * 128, 128),
                            lambda h, k: h1T[:, h, k, at:at + w], KB,
                            before_last=(n_lo, 10 + c) if m == 0 else None).then_inc(f1_ps, 1)

            pe.wait_ge(g_lo, 9)
            pe.wait_ge(g_act, 9)

            def turn2(t, b, reused):
                pe.wait_ge(z_ok, t + 1)
                if reused:
                    pe.wait_ge(ft_act, t)
                for k in range(KB):
                    ins = pe.transpose(ps[:, 6, k * P:(k + 1) * P], z2[:, b, k * 128:(k + 1) * 128],
                                       identf[0:P, 0:P])
                ins.then_inc(zt_ps, 1)

            def gates(t, b, reused):
                pe.wait_ge(ft_act, t + 1)
                if reused:
                    pe.wait_ge(lg_done, t)
                for k in range(KB):
                    ins = pe.matmul(ps[0:P, 7, 0:GATES], ft[:, b, k, :], gw[:, k, :], start=k == 0,
                                    stop=k == KB - 1)
                ins.then_inc(gate_ps, 1)

            def ein(t, j, reused):
                pe.wait_ge(f_lo, t + 1)
                if reused:
                    pe.wait_ge(ei_mul, 2 * t + j - 1)
                for half in range(2):
                    ins = product(ps[0:P, 2 * j + half, :],
                                  lambda h, k: fT[:, h, k, bass.ds(t * P, P)],
                                  lambda h, k: weight(SLOT_EIN + 2 * half + j, h, k), KB)
                ins.then_inc(ei_ps, 1)

            def second_product(t, b):
                product(ps[0:P, 4 + b, :], lambda h, k: r1T[:, h, k, bass.ds(t * P, P)],
                        lambda h, k: weight(SLOT_W2, h, k), KB,
                        before_last=(g_lo, 12) if isinstance(t, int) and t == 0 else None).then_inc(w2_ps, 1)

            def norm2(i):
                for b in range(2):
                    t = 2 * i + b
                    if isinstance(i, int) and i == 0:
                        if b == 0:
                            second_product(0, 0)
                            second_product(1, 1)
                            pe.wait_ge(identf_ok, 1)
                    else:
                        pe.wait_ge(x1_done, t - 1)
                        second_product(t, b)
                    if later(i, b):
                        gates(t - 1, 1 - b, later(i, b, 2))
                        ein(t - 1, 0, later(i, b, 2))
                    turn2(t, b, later(i, b))
                    if later(i, b):
                        ein(t - 1, 1, later(i, b, 2))
            tiles(pe, norm2, peeled=2)
            gates(T - 1, 1, True)
            ein(T - 1, 0, True)
            ein(T - 1, 1, True)

            pe.wait_ge(w_lo, U_SIN + 4)

            def sin(u, m2, c):
                at, w = COLS[c]
                n = 3 * m2 + c
                if not isinstance(u, int) or u or n >= 3:
                    pe.wait_ge(si_mul, 6 * u + n - 2)
                elif n < 2:
                    pe.wait_ge(ei_mul, 2 * T - 1 + n)
                for half in range(2):
                    ins = product(ps[:, 2 * c + half, 0:w],
                                  lambda h, k: wslots[:, SLOT_SIN + u, h,
                                                      ((m2 * 2 + half) * KB + k) * 128:((m2 * 2 + half) * KB + k + 1) * 128],
                                  lambda h, k: fT[:, h, k, at:at + w], KB)
                ins.then_inc(si_ps, 1)

            for n in range(6):
                sin(0, n // 3, n % 3)
            sin(1, 0, 0)
            pe.wait_ge(rank_in, 1)
            pe.matmul(ps[0:P, 6, 0:T * EXPERTS], ones[0:P, 0:P], before[:, 0:T, :], start=True, stop=False)
            pe.matmul(ps[0:P, 6, 0:T * EXPERTS], tri[0:P, 0:P], mask16[:, :, :], start=False, stop=True)
            pe.matmul(ps[0:P, 6, 128:128 + EXPERTS], ones[0:P, 0:P], before[:, T, :], start=True, stop=True)\
              .then_inc(rank_ps, 1)
            for n in range(1, 6):
                sin(1, n // 3, n % 3)
            sin(2, 0, 0)
            pe.wait_ge(hots_ok, 1)
            for n in range(2 * T):
                ins = pe.matmul(ps[:, 7, 0:4 * JW], hot_p[:, n, :], hot_j[:, n, :, :], start=n == 0,
                                stop=n == 2 * T - 1)
            ins.then_inc(slot_ps, 1)
            for n in range(1, 6):
                sin(2, n // 3, n % 3)
            sin(3, 0, 0)
            pe.wait_ge(slots_ok, 1)
            for t in range(T):
                ins = pe.transpose(ps16[0:EXPERTS, 6 + t // 8, (t % 8) * 128:(t % 8) * 128 + P], mask16[:, t, :],
                                   ident[0:P, 0:P])
            ins.then_inc(cnt_ps, 1)
            for n in range(1, 6):
                sin(3, n // 3, n % 3)

            def turn_rows(i, b):
                j = 2 * i + b
                pe.wait_ge(got_ok[b], 16 * i + 16)
                if later(i, b, 2):
                    pe.wait_ge(ht_hi, j - 1)
                    pe.wait_ge(ht_lo, j - 1)
                for h in range(2):
                    for k in range(HB):
                        ins = pe.transpose(ps16[:, 4 + 2 * b + h, k * 128:(k + 1) * 128],
                                           got[:, b, h * HID + k * 128:h * HID + (k + 1) * 128], ident[:, :])
                ins.then_inc(tr_ps, 1)

            pe.wait_ge(cnt_ok, 2)
            pe.wait_ge(si_lo, 21)
            pe.wait_ge(w_lo, U_SOUT + 2)

            def sout(i):
                for b in range(2):
                    t = 2 * i + b
                    if later(i, b, 2):
                        pe.wait_ge(so_done, t - 1)
                    out_ap = ps[0:P, 6 + b, :]
                    for h in range(2):
                        pe.matmul(out_ap, cntT[:, bass.ds(t * P, P)], bias9[:, h, :], start=h == 0, stop=False)
                    product(out_ap, lambda h, k: (hsl if h else hsh)[:, k, bass.ds(t * P, P)],
                            lambda h, k: weight(SLOT_SOUT + k // 4, h, k % 4), HB, start=False,
                            before_last=None if later(i, b) else (si_lo, 24)).then_inc(so_ps, 1)
            sout(0)
            turn_rows(0, 0)
            with pe.Fori(1, T // 2) as i:
                sout(i)

            def expert(i, b):
                j = 2 * i + b
                e = pe.value_load(eidt[0:1, bass.ds(j, 1)], min_val=0, max_val=EXPERTS - 1)
                pe.wait_ge(ht_hi, j + 1)
                pe.wait_ge(ht_lo, j + 1)
                if later(i, b, 2):
                    pe.wait_ge(y_ok, j - 1)
                pe.wait_ge(w_lo, e * 2 + U_EXP + 2)
                product(ps[:, b, :], lambda h, k: heT[b][:, h, k, :],
                        lambda h, k: weight(e * 2 + k // 4, h, k % 4), HB).then_inc(ex_ps, 1)

            pe.wait_ge(eid_ok, 1)

            def routed(i):
                turn_rows(i, 1)
                expert(i, 0)
                turn_rows(i + 1, 0)
                expert(i, 1)
            expert(0, 0)
            pe.wait_ge(so_done, T)
            turn_rows(0, 1)
            turn_rows(1, 0)
            expert(0, 1)
            with pe.Fori(1, MAX_TILES // 2) as i:
                routed(i)
            expert(MAX_TILES // 2, 0)


_OUT_ROWS = N_NODES + 128


def kernel(**inputs):
    import numpy as _np
    import concourse.bacc as _bacc
    from concourse import mybir as _mybir
    from concourse.bass_utils import run_bass_kernel_spmd as _run

    a = {k: _np.asarray(v) for k, v in inputs.items()}

    def units(w):
        n_in, n_out = w.shape
        w = w.reshape(n_in // 512, 4, 128, n_out // 512, 512)
        return w.transpose(3, 0, 2, 1, 4).reshape(-1, 128, UNIT)

    def paired(w):
        w = w.reshape(KB, 128, 2, 4, 2, 128)
        return w.transpose(3, 1, 4, 2, 0, 5).reshape(4, 128, UNIT)

    kv = a["L0_mix_Wkv"].T
    weights = [units(kv[:, :D]), units(kv[:, D:]), units(a["L0_mix_Wq"].T), units(a["L0_gnn_W1"]),
               units(a["L0_gnn_W2"]), units(a["L0_ffn_expert_in_w"].T), paired(a["L0_ffn_shared_in_w"].T),
               units(a["L0_ffn_shared_out_w"].T)]
    weights += [units(a["L0_ffn_expert_out_weight"][e].T) for e in range(EXPERTS)]
    gate = _np.concatenate([a["L0_ffn_group_gate_w"], a["L0_ffn_expert_gate_w"]])
    arrays = {
        "x": a["x"],
        "dst_rows": a["dst"].reshape(2, HALF, P).transpose(1, 0, 2),
        "dst_cols": a["dst"].reshape(CHUNKS, P).T,
        "src_cols": a["src"].reshape(CHUNKS, P).T,
        "weights": _np.concatenate(weights),
        "b1": a["L0_gnn_b1"].reshape(KB, 128).T,
        "b2": a["L0_gnn_b2"].reshape(1, D),
        "ln_scale": a["L0_ffn_ln_scale"].reshape(KB, 128).T,
        "ln_bias": a["L0_ffn_ln_bias"].reshape(KB, 128).T,
        "gate_w": gate.T.reshape(KB, 128, GATES).transpose(1, 0, 2),
        "gate_b": _np.concatenate([a["L0_ffn_group_bias"], a["L0_ffn_expert_bias"]]).reshape(1, GATES),
        "expert_b": a["L0_ffn_expert_out_bias"],
        "shared_b": a["L0_ffn_shared_out_b"].reshape(1, D),
    }
    arrays = {k: _np.ascontiguousarray(v) for k, v in arrays.items()}
    nc = _bacc.Bacc("TRN2", target_bir_lowering=False, num_devices=1)
    dram = {k: nc.dram_tensor(k, v.shape, _mybir.dt.from_np(v.dtype), kind="ExternalInput").ap()
            for k, v in arrays.items()}
    out = nc.dram_tensor("out", (_OUT_ROWS, D), F32, kind="ExternalOutput").ap()
    hid = nc.dram_tensor("hid", (N_NODES, 2 * HID), F16, kind="Internal").ap()
    gps_layer(nc, dram, out, hid)
    r = _run(nc, [arrays], core_ids=[0])
    return r.results[0]["out"][:N_NODES]
```
